# Optimizing a Trainium2 kernel written in Bass

```python
import numpy as np
import jax
import jax.numpy as jnp

def _softmax(x, axis=-1):
    return jax.nn.softmax(x, axis=axis)

def _gelu(x):
    return jax.nn.gelu(x, approximate=True)

def _silu(x):
    return jax.nn.silu(x)

def _sigmoid(x):
    return jax.nn.sigmoid(x)

def _layernorm(x, axis=-1, eps=1e-05):
    m = jnp.mean(x, axis=axis, keepdims=True)
    v = jnp.var(x, axis=axis, keepdims=True)
    return (x - m) / jnp.sqrt(v + eps)

def _scatter_add(tgt, idx, src, axis=0):
    return tgt.at[idx].add(src)

def _segment_sum(src, seg, n):
    return jax.ops.segment_sum(src, seg, n)
kernel_name = 'mk_decoder_postln_d1_seqx_r4_e0d5b6'

def setup_inputs(seed: int=0):
    np.random.seed(seed)
    _w = jnp.asarray

    def _rec_inputs():
        import jax
        import jax.numpy as jnp
        _rk = jax.random.key(seed)
        x = 7.22e-05 + 1 * jax.random.normal(jax.random.fold_in(_rk, 1), (2, 1024, 256), jnp.float32)
        _lenS = 1024 - jax.random.randint(jax.random.fold_in(_rk, 7), (2,), 0, max(1, 1024 // 4) + 1, jnp.int32)
        _lenS2 = 77 - jax.random.randint(jax.random.fold_in(_rk, 8), (2,), 0, max(1, 77 // 4) + 1, jnp.int32)
        _ctx_1024P = jax.random.normal(jax.random.fold_in(_rk, 11), (2, 16, 256), jnp.float32)
        _ctx_1024c = jax.random.dirichlet(jax.random.fold_in(_rk, 511), 0.3 * jnp.ones((16,), jnp.float32), (2, 77))
        _ctx_1024t = jnp.einsum('bsk,bkd->bsd', _ctx_1024c, _ctx_1024P)
        _ctx_1024t = _ctx_1024t * jax.lax.rsqrt(jnp.mean(jnp.square(_ctx_1024t)) + 1e-12) * 0.953939
        ctx_1024 = 4.13588e-05 + 0.999923 * (_ctx_1024t + 0.3 * jax.random.normal(jax.random.fold_in(_rk, 611), (2, 77, 256), jnp.float32))
        _validS = jnp.arange(1024)[None, :] < _lenS[:, None]
        _validS2 = jnp.arange(77)[None, :] < _lenS2[:, None]
        _causal = jnp.tril(jnp.ones((1024, 1024), dtype=bool))
        mask_BxSxS2_ik1 = jnp.where(jnp.broadcast_to(_validS2[:, None, :], (2, 1024, 77)), 1, 0).astype(jnp.int32)
        return (x, ctx_1024, mask_BxSxS2_ik1)
    x, ctx_1024, mask_BxSxS2_ik1 = _rec_inputs()

    def _L0_attn_setup():
        import jax, jax.numpy as jnp
        import numpy as np
        NUM_HEADS = 16
        key = jax.random.key(seed)
        kx, kq, kk, kv = jax.random.split(key, 4)
        N, S, D = (2, 1024, 256)
        scale = 1.0 / np.sqrt(D)
        x = jax.random.normal(kx, (N, S, D), dtype=jnp.float32)
        Wq = jax.random.normal(kq, (D, D), dtype=jnp.float32) * scale
        Wk = jax.random.normal(kk, (D, D), dtype=jnp.float32) * scale
        Wv = jax.random.normal(kv, (D, D), dtype=jnp.float32) * scale
        return {'x': x, 'Wq': Wq, 'Wk': Wk, 'Wv': Wv}
    _L0_attn_all = _L0_attn_setup()
    _L0_attn_in = {k: v for k, v in _L0_attn_all.items() if k in ('Wq', 'Wk', 'Wv')}
    del _L0_attn_all

    def _L0_xattn_setup():
        import jax, jax.numpy as jnp
        import numpy as np
        HID = 256
        HEADS = 16
        HEAD_DIM = HID // HEADS

        def _split_heads(x, W, b):
            B, S, _ = x.shape
            y = x @ W + b
            return y.reshape(B, S, HEADS, HEAD_DIM).transpose(0, 2, 1, 3)
        key = jax.random.key(seed)
        ks = jax.random.split(key, 12)
        B, S = (4, 512)
        inp = {'query': jax.random.normal(ks[0], (B, S, HID), dtype=jnp.float32), 'key': jax.random.normal(ks[1], (B, S, HID), dtype=jnp.float32), 'value': jax.random.normal(ks[2], (B, S, HID), dtype=jnp.float32), 'mask': jax.random.randint(ks[3], (B, S, S), 0, 2, dtype=jnp.int32), 'Wq': jax.random.normal(ks[4], (HID, HID), dtype=jnp.float32) * (1.0 / np.sqrt(HID)), 'bq': jnp.zeros((HID,), dtype=jnp.float32), 'Wk': jax.random.normal(ks[5], (HID, HID), dtype=jnp.float32) * (1.0 / np.sqrt(HID)), 'bk': jnp.zeros((HID,), dtype=jnp.float32), 'Wv': jax.random.normal(ks[6], (HID, HID), dtype=jnp.float32) * (1.0 / np.sqrt(HID)), 'bv': jnp.zeros((HID,), dtype=jnp.float32), 'Wo': jax.random.normal(ks[7], (HID, HID), dtype=jnp.float32) * (1.0 / np.sqrt(HID)), 'bo': jnp.zeros((HID,), dtype=jnp.float32)}
        return inp
    _L0_xattn_all = _L0_xattn_setup()
    _L0_xattn_in = {k: v for k, v in _L0_xattn_all.items() if k in ('Wq', 'bq', 'Wk', 'bk', 'Wv', 'bv', 'Wo', 'bo')}
    del _L0_xattn_all

    def _L0_ffn_setup():
        import jax, jax.numpy as jnp
        import numpy as np
        D_MODEL = 256
        N_EXPERTS = 8
        TOP_K = 2
        LN_EPS = 1e-05
        key = jax.random.key(seed)
        ks = jax.random.split(key, 8)
        B, S, d, E = (2, 512, D_MODEL, N_EXPERTS)
        f = 2 * d
        s_in = 0.02
        return {'x': jax.random.normal(ks[0], (B, S, d), jnp.float32), 'Wg': jax.random.normal(ks[1], (d, E), jnp.float32) * s_in, 'bg': jnp.zeros((E,), jnp.float32), 'W1': jax.random.normal(ks[2], (E, d, f), jnp.float32) * s_in, 'b1': jnp.zeros((E, f), jnp.float32), 'W2': jax.random.normal(ks[3], (E, f, d), jnp.float32) * s_in, 'b2': jnp.zeros((E, d), jnp.float32), 'gamma': jnp.ones((d,), jnp.float32), 'beta': jnp.zeros((d,), jnp.float32)}
    _L0_ffn_all = _L0_ffn_setup()
    _L0_ffn_in = {k: v for k, v in _L0_ffn_all.items() if k in ('Wg', 'bg', 'W1', 'b1', 'W2', 'b2', 'gamma', 'beta')}
    del _L0_ffn_all
    return {'x': x, 'ctx_1024': ctx_1024, 'mask_BxSxS2_ik1': mask_BxSxS2_ik1, 'L0_attn_Wq': _L0_attn_in['Wq'], 'L0_attn_Wk': _L0_attn_in['Wk'], 'L0_attn_Wv': _L0_attn_in['Wv'], 'L0_xattn_Wq': _L0_xattn_in['Wq'], 'L0_xattn_bq': _L0_xattn_in['bq'], 'L0_xattn_Wk': _L0_xattn_in['Wk'], 'L0_xattn_bk': _L0_xattn_in['bk'], 'L0_xattn_Wv': _L0_xattn_in['Wv'], 'L0_xattn_bv': _L0_xattn_in['bv'], 'L0_xattn_Wo': _L0_xattn_in['Wo'], 'L0_xattn_bo': _L0_xattn_in['bo'], 'L0_ffn_Wg': _L0_ffn_in['Wg'], 'L0_ffn_bg': _L0_ffn_in['bg'], 'L0_ffn_W1': _L0_ffn_in['W1'], 'L0_ffn_b1': _L0_ffn_in['b1'], 'L0_ffn_W2': _L0_ffn_in['W2'], 'L0_ffn_b2': _L0_ffn_in['b2'], 'L0_ffn_gamma': _L0_ffn_in['gamma'], 'L0_ffn_beta': _L0_ffn_in['beta']}

def reference(x, ctx_1024, mask_BxSxS2_ik1, L0_attn_Wq, L0_attn_Wk, L0_attn_Wv, L0_xattn_Wq, L0_xattn_bq, L0_xattn_Wk, L0_xattn_bk, L0_xattn_Wv, L0_xattn_bv, L0_xattn_Wo, L0_xattn_bo, L0_ffn_Wg, L0_ffn_bg, L0_ffn_W1, L0_ffn_b1, L0_ffn_W2, L0_ffn_b2, L0_ffn_gamma, L0_ffn_beta):
    import jax
    import jax.numpy as jnp

    def _L0_attn_ref(x, Wq, Wk, Wv):
        import jax, jax.numpy as jnp
        import numpy as np
        NUM_HEADS = 16
        N, S, D = x.shape
        H = NUM_HEADS
        hd = D // H
        q = (x @ Wq.T).reshape(N, S, H, hd).transpose(0, 2, 1, 3)
        k = (x @ Wk.T).reshape(N, S, H, hd).transpose(0, 2, 1, 3)
        v = (x @ Wv.T).reshape(N, S, H, hd).transpose(0, 2, 1, 3)
        energy = jnp.einsum('nhqd,nhkd->nhqk', q, k)
        attn = jax.nn.softmax(energy / jnp.sqrt(jnp.float32(hd)), axis=3)
        out = jnp.einsum('nhql,nhld->nhqd', attn, v)
        return out.transpose(0, 2, 1, 3).reshape(N, S, D)

    def _L0_xattn_ref(query, key, value, mask, Wq, bq, Wk, bk, Wv, bv, Wo, bo):
        import jax, jax.numpy as jnp
        import numpy as np
        HID = 256
        HEADS = 16
        HEAD_DIM = HID // HEADS

        def _split_heads(x, W, b):
            B, S, _ = x.shape
            y = x @ W + b
            return y.reshape(B, S, HEADS, HEAD_DIM).transpose(0, 2, 1, 3)
        B, S, _ = query.shape
        Q = _split_heads(query, Wq, bq)
        K = _split_heads(key, Wk, bk)
        V = _split_heads(value, Wv, bv)
        scale = 1.0 / jnp.sqrt(jnp.asarray(HEAD_DIM, dtype=Q.dtype))
        energy = jnp.einsum('bhqd,bhkd->bhqk', Q, K) * scale
        m = mask[:, None, :, :]
        energy = jnp.where(m == 0, jnp.asarray(-1000000000.0, dtype=energy.dtype), energy)
        attn = jax.nn.softmax(energy, axis=-1)
        out = jnp.einsum('bhqk,bhkd->bhqd', attn, V)
        out = out.transpose(0, 2, 1, 3).reshape(B, S, HID)
        return out @ Wo + bo

    def _L0_ffn_ref(x, Wg, bg, W1, b1, W2, b2, gamma, beta):
        import jax, jax.numpy as jnp
        import numpy as np
        D_MODEL = 256
        N_EXPERTS = 8
        TOP_K = 2
        LN_EPS = 1e-05
        logits = jnp.einsum('bsd,de->bse', x, Wg) + bg
        topk_vals, topk_idx = jax.lax.top_k(logits, TOP_K)
        topk_w = jax.nn.softmax(topk_vals, axis=-1)
        h = jax.nn.relu(jnp.einsum('bsd,edf->bsef', x, W1) + b1)
        eo = jnp.einsum('bsef,efd->bsed', h, W2) + b2
        sel = jnp.take_along_axis(eo, topk_idx[..., None], axis=2)
        mixed = jnp.sum(sel * topk_w[..., None], axis=2)
        y = mixed + x
        mu = jnp.mean(y, axis=-1, keepdims=True)
        var = jnp.mean(jnp.square(y - mu), axis=-1, keepdims=True)
        return gamma * (y - mu) * jax.lax.rsqrt(var + LN_EPS) + beta
    x = _layernorm(x + _L0_attn_ref(x, L0_attn_Wq, L0_attn_Wk, L0_attn_Wv), axis=-1)
    x = _layernorm(x + _L0_xattn_ref(x, ctx_1024, ctx_1024, mask_BxSxS2_ik1, L0_xattn_Wq, L0_xattn_bq, L0_xattn_Wk, L0_xattn_bk, L0_xattn_Wv, L0_xattn_bv, L0_xattn_Wo, L0_xattn_bo), axis=-1)
    x = _layernorm(x + _L0_ffn_ref(x, L0_ffn_Wg, L0_ffn_bg, L0_ffn_W1, L0_ffn_b1, L0_ffn_W2, L0_ffn_b2, L0_ffn_gamma, L0_ffn_beta), axis=-1)
    return x

_drawn_inputs = setup_inputs


def setup_inputs(seed=0):
    import zlib

    import numpy as np

    out = dict(_drawn_inputs(seed))
    spreads = {'L0_xattn_bq': (0.0, 0.329),
     'L0_xattn_bk': (0.0, 0.8),
     'L0_xattn_bv': (0.0, 0.1),
     'L0_xattn_bo': (0.0, 0.1),
     'L0_ffn_bg': (0.0, 0.333),
     'L0_ffn_b1': (0.0, 0.706),
     'L0_ffn_b2': (0.0, 0.1),
     'L0_ffn_gamma': (1.0, 0.2),
     'L0_ffn_beta': (0.0, 0.1)}
    factors = {}
    for name, (base, spread) in spreads.items():
        noise = np.random.default_rng([zlib.crc32(name.encode()), seed]).standard_normal(out[name].shape)
        drawn = base * np.exp(spread * noise) if base else spread * noise
        out[name] = jnp.asarray(drawn.astype(out[name].dtype))
    for name, factor in factors.items():
        out[name] = (out[name] * factor).astype(out[name].dtype)
    return out
```

```python
from contextlib import ExitStack

import concourse.bass as bass
from concourse import mybir

ALU = mybir.AluOpType
ACT = mybir.ActivationFunctionType
AX_X = mybir.AxisListType.X
F32 = mybir.dt.float32
BF16 = mybir.dt.bfloat16
I32 = mybir.dt.int32
U32 = mybir.dt.uint32

P = 128
B, S, D = 2, 1024, 256
H, HD = 16, 16
SC = 77
NE, F = 8, 512
NT = B * S // P
C2 = D // P
TG = B * S // 512
GH = 4
NG = H // GH
NGRP = B * NG
KT = S // P
UNITS = 2 * NGRP
STEPS = KT * GH
VW = 32
PR = 8
EPS = 1e-5
INV4 = 0.25
MASKED = -4.0e9
MAXROW = 96
KROWS = 98
AHEAD = 5
Q_BLOCKS = ((0, 0, 3), (48, 0, 2), (80, 0, 1))
K_BLOCKS = ((0, 0, 1), (16, 0, 1), (32, 0, 1), (48, 1, 1), (64, 1, 1), (80, 2, 1))
EC = 17
MASK_STEPS = 9
GATE_STEPS = 12
LATE = 17
LOADS = len(Q_BLOCKS) + len(K_BLOCKS)
FC = F // P


def build(nc, t):
    with ExitStack() as ctx:
        def sb(name, shape, dt=F32):
            return ctx.enter_context(nc.sbuf_tensor(name, shape, dt))

        def sem(name):
            return ctx.enter_context(nc.semaphore(name))

        bank = [ctx.enter_context(nc.psum_tensor(f"bank{i}", [P, 512], F32)) for i in range(4, 8)]
        quad = ctx.enter_context(nc.psum_tensor("quad", [P, 4, 512], F32))
        bank = [quad[:, i, :] for i in range(4)] + [b[:, :] for b in bank]
        scratch = {w: nc.dram_tensor(f"{w}_parts", (NGRP, 3, HD, GH * S), BF16, kind="Internal").ap()
                   for w in "qk"}

        ident = sb("ident", [P, P])
        ident16 = sb("ident16", [P, P], BF16)
        block8 = sb("block8", [P, 8])
        iota8 = sb("iota8", [P, NE])
        w_in = {n: sb(n, [P, C2, D]) for n in ("wq", "wk", "wv", "cwq", "cwk", "cwv", "cwo")}
        xres = sb("xres", [P, NT, D])
        attn = sb("attn", [P, 4, 4, 4, GH * HD])
        acc = attn[:, :, :, :, :].rearrange("p a k q c -> p (a k q c)").rearrange("p (n d) -> p n d", d=D)
        stats = sb("stats", [P, NT, 6])
        lnv = sb("lnv", [P, 8, NT])
        ctxT = sb("ctxT", [P, C2, B * SC])
        k2T = sb("k2T", [P, 2, B * SC])
        kbd = sb("kbd", [P, B, 2, 8, SC])
        v2 = sb("v2", [SC, B, H, HD + 1])
        maski = sb("maski", [P, NT, SC], I32)
        keep = sb("keep", [P, NT, SC])
        fill = sb("fill", [P, NT, SC])
        rows = {n: sb(f"{n}_row", [P, D]) for n in ("cbv", "cbo", "gamma", "beta")}
        cbq, cbk = sb("cbq", [P, 2]), sb("cbk", [P, 2])
        wg = sb("wg", [P, C2, NE])
        bg = sb("bg", [P, NE])
        b1 = sb("b1", [P, NE, FC])
        one = sb("one", [P, 1])
        b1e = sb("b1e", [P, 2, FC])
        b2 = sb("b2", [NE, D])
        credit = sb("credit", [P, 8])
        first = ctx.enter_context(ExitStack())

        def sb1(name, shape, dt=F32):
            return first.enter_context(nc.sbuf_tensor(name, shape, dt))

        xT = sb1("xT", [P, C2, B * S])
        parts = sb1("parts", [P, 3, 3, 512], BF16)
        rest = sb1("rest", [P, 2, 512])
        qstack = [sb1(f"qstack{i}", [P, 2, GH, 512], BF16) for i in range(2)]
        kstack = [sb1(f"kstack{i}", [P, GH, S], BF16) for i in range(2)]
        v_all = sb1("v_all", [P, NGRP, KT, GH, VW])
        vslot = [sb1(f"vslot{i}", [P, KT, GH, VW]) for i in range(2)]
        probs = sb1("probs", [P, PR, 512])
        rowmax = sb1("rowmax", [P, 2, 16])
        negparts = sb1("negparts", [P, 2, 32], BF16)
        negrows = sb1("negrows", [32, 2, P], BF16)
        outT = sb1("outT", [P, 512])
        rden = sb1("rden", [P, 16])
        first.close()
        x1 = sb("x1", [P, 4, D])
        x1b = sb("x1b", [P, 4, D])
        x1T = sb("x1T", [P, C2, 512])
        q2T = sb("q2T", [P, 2, 512])
        sc2 = sb("sc2", [P, 2, H, SC])
        max2 = sb("max2", [P, 2, H])
        pT = sb("pT", [SC, 2, H, P])
        rden2 = sb("rden2", [P, H])
        o2 = sb("o2", [P, 2, D])
        o2T = sb("o2T", [P, C2, P])
        x2 = sb("x2", [P, 4, D])
        x2T = sb("x2T", [P, C2, 512])
        x2h = sb("x2h", [P, C2, B * S], BF16)
        x2l = sb("x2l", [P, C2, B * S], BF16)
        logits = sb("logits", [P, 4, NE])
        top = sb("top", [P, 4, 8])
        topi = sb("topi", [P, 4, 8], U32)
        topf = sb("topf", [P, 4, 8])
        gw = sb("gw", [P, 4, 4])
        pick = sb("pick", [P, 2, 4, NE])
        gates = sb("gates", [P, NT, NE])
        gT = sb("gT", [NE, 4, P])
        w1raw = sb("w1raw", [P, C2, F])
        w2raw = sb("w2raw", [P, FC, D])
        w1 = [[sb(f"w1_{i}{j}", [P, C2, F], BF16) for j in "hl"] for i in range(2)]
        w2 = [[sb(f"w2_{i}{j}", [P, FC, D], BF16) for j in "hl"] for i in range(2)]
        hid = sb("hid", [P, 4, 512])
        hh = sb("hh", [P, 2, FC, 512], BF16)
        hl = sb("hl", [P, 2, FC, 512], BF16)

        loaded = {n: sem(n) for n in ("w_loaded", "const_loaded", "x_loaded")}
        xT_loaded = [sem(f"xT_loaded{i}") for i in range(TG)]
        qk_ready, hi_done, rest_done, mid_done, parts_done = map(sem, ("qk_ready", "hi_done", "rest_done", "mid_done", "parts_done"))
        parts_stored = [sem(f"parts_stored{i}") for i in range(3)]
        v_ready, v_done, v_zeroed = sem("v_ready"), sem("v_done"), sem("v_zeroed")
        ones_set = sem("ones_set")
        stack_loaded = [sem(f"stack_loaded{i}") for i in range(2)]
        vslot_loaded = [sem(f"vslot_loaded{i}") for i in range(2)]
        max_ready, max_taken = sem("max_ready"), sem("max_taken")
        neg_hi, neg_parts, neg_turned, neg_rows = map(sem, ("neg_hi", "neg_parts", "neg_turned", "neg_rows"))
        neg_loaded = sem("neg_loaded")
        scores_ready, probs_ready, probs_used = map(sem, ("scores_ready", "probs_ready", "probs_used"))
        o_copied, o_turned, o_recip, o_normed = map(sem, ("o_copied", "o_turned", "o_recip", "o_normed"))
        out_stored = sem("out_stored")
        mask_loaded, mask_step, kbd_done = sem("mask_loaded"), sem("mask_step"), sem("kbd_done")
        cross_ready, k2_done, v2_done = sem("cross_ready"), sem("k2_done"), sem("v2_done")
        chain, y1_done, root_wanted, root_done = map(sem, ("chain", "y1_done", "root_wanted", "root_done"))
        x1_done, x1_turned, x1T_done, x1b_done = map(sem, ("x1_done", "x1_turned", "x1T_done", "x1b_done"))
        q2_ready, q2_done = sem("q2_ready"), sem("q2_done")
        s2_ready, s2_taken, s2_filled, s2_max, s2_shifted, p2_done = map(sem, ("s2_ready", "s2_taken", "s2_filled", "s2_max", "s2_shifted", "p2_done"))
        p2_turned, pT_act, pT_dve = sem("p2_turned"), sem("pT_act"), sem("pT_dve")
        o2_ready, o2_recip, o2_done, o2_turned, o2T_done = map(sem, ("o2_ready", "o2_recip", "o2_done", "o2_turned", "o2T_done"))
        y2_ready, y2_done = sem("y2_ready"), sem("y2_done")
        x2_done, x2_turned, x2T_done, x2h_done, x2l_done = map(sem, ("x2_done", "x2_turned", "x2T_done", "x2h_done", "x2l_done"))
        logits_ready, gate_step, gap_done, gap_exp = map(sem, ("logits_ready", "gate_step", "gap_done", "gap_exp"))
        gates_done, gates_turned, gT_done, bias_ready, acc_set = map(sem, ("gates_done", "gates_turned", "gT_done", "bias_ready", "acc_set"))
        w_fetched = [sem("w1_fetched"), sem("w2_fetched")]
        out_done = sem("out_done")
        w_split = sem("w_split")
        h_ready, hid_done, hh_done, hl_done = map(sem, ("h_ready", "hid_done", "hh_done", "hl_done"))
        e_ready, e_added = sem("e_ready"), sem("e_added")
        block = ctx.enter_context(nc.Block())

        QK_JOBS, V_JOBS = 4 * TG, 2 * TG

        def unit_slot(k):
            return (k // 2) % 2

        @block.sync
        def _(sp):
            sp.dma_start(w_in["wq"][:, :, :], t["wqT"].rearrange("(c p) n -> p c n", p=P)).then_inc(loaded["w_loaded"], 16)
            for g in range(TG):
                sp.dma_start(xT[:, :, g * 512:(g + 1) * 512],
                             t["xT"].rearrange("(c p) n -> p c n", p=P)[:, :, g * 512:(g + 1) * 512]).then_inc(xT_loaded[g], 16)
                if g == 0:
                    for n in ("wk", "wv"):
                        sp.dma_start(w_in[n][:, :, :], t[n + "T"].rearrange("(c p) n -> p c n", p=P)).then_inc(loaded["w_loaded"], 16)
                    sp.dma_start(ident[:, :], t["ident"]).then_inc(loaded["const_loaded"], 16)
            late = [(w_in[n][:, :, :], t[n].rearrange("(c p) n -> p c n", p=P)) for n in ("cwq", "cwk", "cwv", "cwo")]
            late += [(ctxT[:, :, :], t["ctxT"].rearrange("(c p) n -> p c n", p=P)),
                     (block8[:, :], t["block8"]), (iota8[:, :], t["iota8"]),
                     (cbq[:, :], t["cbq"].rearrange("(h p) -> p h", p=P)), (cbk[:, :], t["cbk"].rearrange("(h p) -> p h", p=P)),
                     (wg[:, :, :], t["wg"].rearrange("(c p) n -> p c n", p=P)),
                     (bg[:, :], t["bg"].rearrange("(o n) -> o n", o=1).to_broadcast([P, NE])),
                     (b1[:, :, :], t["b1"].rearrange("e (c p) -> p e c", p=P)), (b2[:, :], t["b2"])]
            late += [(rows[n][:, :], t[n].rearrange("(o n) -> o n", o=1).to_broadcast([P, D])) for n in ("cbv", "cbo", "gamma", "beta")]
            assert len(late) == LATE
            with nc.allow_non_contiguous_dma(reason="small bias vectors go over the partitions"):
                for dst, src in late:
                    sp.dma_start(dst, src).then_inc(loaded["x_loaded"], 16)
            sp.dma_start(maski[:, :, :], t["mask"].rearrange("(n p) s -> p n s", p=P)).then_inc(mask_loaded, 16)
            sp.dma_start(xres[:, :, :], t["x"].rearrange("(n p) d -> p n d", p=P)).then_inc(loaded["x_loaded"], 16)

            def store_parts(n):
                g, job = n // 4, n % 4
                w, half, b = "qk"[job // 2], job % 2, g // 2
                sp.wait_ge(parts_done, n + 1)
                for part in range(3):
                    for gg in range(2):
                        layout = {"q": "d (h j s) -> h j d s", "k": "d (j h s) -> h j d s"}[w]
                        dst = scratch[w][b * NG + half * 2 + gg, part, :, :].rearrange(layout, h=2, s=512)[g % 2]
                        sp.dma_start(dst,
                                     parts[gg * 64:gg * 64 + 64, n % 3, part, :]).then_inc(parts_stored[n % 3], 16)

            def load_group(gi, slot):
                for row, part, n in Q_BLOCKS:
                    src = scratch["q"][bass.ds(gi, 1), part:part + n, :, :].rearrange("o r d s -> (o r d) s")
                    sp.dma_start(qstack[slot][row:row + n * HD, :, :, :].rearrange("p h j s -> p (h j s)"), src).then_inc(stack_loaded[slot], 16)
                for row, part, n in K_BLOCKS:
                    src = scratch["k"][bass.ds(gi, 1), part:part + n, :, :].rearrange("o r d s -> (o r d) s")
                    sp.dma_start(kstack[slot][row:row + n * HD, :, :].rearrange("p j s -> p (j s)"), src).then_inc(stack_loaded[slot], 16)
                sp.dma_start(vslot[slot][:, :, :, :].rearrange("p k j c -> p (k j c)"),
                             v_all[:, bass.ds(gi, 1), :, :, :].rearrange("p o k j c -> p (o k j c)")).then_inc(vslot_loaded[slot], 16)

            def load_negmax(rows_done, k1):
                slot, half = unit_slot(k1), k1 % 2
                sp.wait_ge(neg_rows, rows_done)
                for part in range(2):
                    sp.dma_start(qstack[slot][MAXROW + part:MAXROW + part + 1, half, :, :],
                                 negrows[part * 16:part * 16 + 16, k1 % 2, :]).then_inc(neg_loaded, 16)

            for n in range(QK_JOBS):
                store_parts(n)
            for s in range(3):
                sp.wait_ge(parts_stored[s], 96 * len(range(s, QK_JOBS, 3)))
            sp.wait_ge(v_done, V_JOBS)
            load_group(0, 0)
            load_group(1, 1)
            load_negmax(1, 0)

            def sp_unit(it, k, last):
                u = it * 4 + k
                if not (last and k == 3):
                    load_negmax(u + 2, k + 1)
                if k % 2 == 1 and not last:
                    sp.wait_ge(probs_used, u * STEPS + (STEPS + PR))
                    load_group(it * 2 + (k // 2 + 2), unit_slot(k))

            with sp.Fori(0, 3) as it:
                for k in range(4):
                    sp_unit(it, k, False)
            for k in range(4):
                sp_unit(3, k, True)
            def fetch_expert(e):
                sp.dma_start(w1raw[:, :, :], t["w1"][bass.ds(e, 1), :, :].rearrange("o (c p) f -> p (o c) f", p=P)).then_inc(w_fetched[0], 16)
                sp.dma_start(w2raw[:, :, :], t["w2"][bass.ds(e, 1), :, :].rearrange("o (c p) f -> p (o c) f", p=P)).then_inc(w_fetched[1], 16)

            sp.wait_ge(o_normed, UNITS + 1)
            fetch_expert(0)
            with sp.Fori(1, NE) as e:
                sp.wait_ge(w_split, e * 5)
                fetch_expert(e)
            out_v = t["out"].rearrange("(n p) d -> p n d", p=P)
            for n in range(NT):
                sp.wait_ge(out_done, n + 1)
                sp.dma_start(out_v[:, n, :], acc[:, n, :]).then_inc(out_stored, 16)
            sp.wait_ge(out_stored, 16 * NT)

        @block.tensor
        def _(pe):
            def project(g):
                pe.wait_ge(xT_loaded[g], 16)
                for job in range(4):
                    n = 4 * g + job
                    if n == 0:
                        pe.wait_ge(loaded["w_loaded"], 48)
                    if n >= 4:
                        pe.wait_ge(rest_done, n - 3)
                    w = w_in[("wq", "wk")[job // 2]]
                    half = job % 2
                    for c in range(C2):
                        mm = pe.matmul(bank[n % 4], w[:, c, half * P:half * P + P], xT[:, c, g * 512:g * 512 + 512],
                                       start=(c == 0), stop=(c == C2 - 1))
                    mm.then_inc(qk_ready, 1)
                for pair in range(2):
                    m = 2 * g + pair
                    if m >= 2:
                        pe.wait_ge(v_done, m - 1)
                    for i in range(2):
                        tok = g * 512 + (2 * pair + i) * P
                        for c in range(C2):
                            mm = pe.matmul(bank[4 + m % 2][:, i * D:(i + 1) * D], xT[:, c, tok:tok + P], w_in["wv"][:, c, :],
                                           start=(c == 0), stop=(c == C2 - 1))
                    mm.then_inc(v_ready, 1)

            for g in range(TG):
                project(g)

            def max_pair(u, k, p):
                slot, half, j, qt = unit_slot(k), k % 2, p // 4, p % 4
                pe.wait_ge(max_taken, u * 16 + p + 1)
                q = qstack[slot][0:MAXROW, half, j, qt * P:qt * P + P]
                for e in range(2):
                    mm = pe.matmul(bank[2 * (p % 2) + e], q, kstack[slot][0:MAXROW, j, e * 512:e * 512 + 512],
                                   start=True, stop=True)
                mm.then_inc(max_ready, 1)

            def turn_negmax(u, k, first=False):
                if not first:
                    pe.wait_ge(o_normed, u)
                pe.wait_ge(neg_parts, u + 1)
                pe.transpose(bank[7].bitcast(BF16)[0:32, 0:P], negparts[:, k % 2, :], ident16[:, :]).then_inc(neg_turned, 1)

            def scores(u, k, i):
                slot, half, kt, j = unit_slot(k), k % 2, i // 4, i % 4
                pe.wait_ge(probs_ready, u * STEPS + i + 1)
                mm = pe.matmul(bank[4 + i % 2], kstack[slot][0:KROWS, j, kt * P:kt * P + P],
                               qstack[slot][0:KROWS, half, j, :], start=True, stop=True)
                mm.then_inc(scores_ready, 1)
                return mm

            def values(u, k, i):
                slot, kt, j = unit_slot(k), i // 4, i % 4
                pe.wait_ge(probs_ready, u * STEPS + i + 3)
                pe.matmul(bank[6][32 * j:32 * j + VW, :], vslot[slot][:, kt, j, :], probs[:, i % PR, :],
                          start=(kt == 0), stop=(kt == KT - 1), skip_group_check=True).then_inc(probs_used, 1)

            pe.wait_ge(loaded["x_loaded"], 16 * (LATE + 1))
            for half in range(2):
                for c in range(C2):
                    mm = pe.matmul(bank[6][:, half * B * SC:(half + 1) * B * SC], w_in["cwk"][:, c, half * P:half * P + P], ctxT[:, c, :],
                                   start=(c == 0), stop=(c == C2 - 1))
            mm.then_inc(cross_ready, 1)
            for b in range(B):
                for c in range(C2):
                    mm = pe.matmul(bank[7][0:SC, b * D:(b + 1) * D], ctxT[:, c, b * SC:(b + 1) * SC], w_in["cwv"][:, c, :],
                                   start=(c == 0), stop=(c == C2 - 1))
            mm.then_inc(cross_ready, 1)
            pe.wait_ge(k2_done, 1)
            pe.wait_ge(v2_done, 1)
            pe.wait_ge(parts_done, QK_JOBS)
            pe.wait_ge(v_done, V_JOBS)
            pe.wait_ge(ones_set, 3)
            pe.wait_ge(stack_loaded[0], 16 * LOADS)
            for p in range(16):
                max_pair(0, 0, p)
            turn_negmax(0, 0, first=True)
            for p in range(AHEAD):
                max_pair(1, 1, p)
            pe.wait_ge(neg_loaded, 32)
            scores(0, 0, 0)
            scores(0, 0, 1)

            when = {2 * (p - AHEAD): (1, p) for p in range(AHEAD, 16)}
            when.update({22: (2, 0), 25: (2, 1), 27: (2, 2), 29: (2, 3)})

            def unit(it, k, last):
                u = it * 4 + k
                gi2 = it * 2 + k // 2
                for i in range(STEPS):
                    if i == 0:
                        if k % 2 == 0:
                            pe.wait_ge(vslot_loaded[unit_slot(k)], 16 * (it + 1))
                        pe.wait_ge(o_copied, u + 1)
                    values(u, k, i)
                    if i + 2 < STEPS:
                        mm = scores(u, k, i + 2)
                    elif not (last and k == 3):
                        if i + 2 == STEPS:
                            pe.wait_ge(neg_loaded, u * 32 + 64)
                        scores(u + 1, k + 1, i + 2 - STEPS)
                    if i in when:
                        ahead, p = when[i]
                        if not (last and k + ahead > 3):
                            if (ahead, p) == (2, 0) and (k + 2) % 2 == 0:
                                n_load = it + 1 + (1 if k + 2 > 3 else 0)
                                pe.wait_ge(stack_loaded[unit_slot(k + 2)], n_load * 16 * LOADS)
                            max_pair(u + ahead, k + ahead, p)
                    if i == 23 and not (last and k == 3):
                        turn_negmax(u + 1, k + 1)
                if not (last and k + 2 > 3):
                    max_pair(u + 2, k + 2, AHEAD - 1)
                pe.wait_ge(o_copied, u + 2)
                if not (last and k == 3):
                    pe.wait_ge(neg_rows, u + 2)
                else:
                    pe.wait_ge(o_normed, u + 1)
                for qt in range(4):
                    tr = pe.transpose(bank[7][:, qt * P:qt * P + P], outT[:, qt * P:qt * P + P], ident[:, :])
                tr.then_inc(o_turned, 1)

            with pe.Fori(0, 3) as it:
                for k in range(4):
                    unit(it, k, False)
            for k in range(4):
                unit(3, k, True)


            def cross_group(b, tt):
                g = b * 2 + tt
                pe.wait_ge(x1_done, g * 4 + 4)
                pe.wait_ge(pT_act, g * 8 + 1)
                pe.wait_ge(pT_dve, g * 8 + 1)
                for c in range(C2):
                    for i in range(4):
                        tr = pe.transpose(bank[4 + c][:, i * P:i * P + P], x1[:, i, c * P:c * P + P], ident[:, :])
                    tr.then_inc(x1_turned, 1)
                pe.wait_ge(x1T_done, g * 2 + 2)
                pe.wait_ge(o2_done, g * 4 + 1)
                pe.wait_ge(y2_done, g * 4 + 1)
                for half in range(2):
                    for c in range(C2):
                        mm = pe.matmul(bank[6 + half], w_in["cwq"][:, c, half * P:half * P + P], x1T[:, c, :], start=(c == 0), stop=(c == C2 - 1))
                    mm.then_inc(q2_ready, 1)
                pe.wait_ge(q2_done, g * 2 + 2)

                def scores2(i):
                    n = g * 4 + i
                    pe.wait_ge(s2_taken, n + 1)
                    for e in range(4):
                        mm = pe.matmul(bank[e][:, 0:4 * SC], q2T[:, e // 2, i * P:i * P + P],
                                       kbd[:, bass.ds(b, 1), e // 2, 4 * (e % 2):4 * (e % 2) + 4, :].rearrange("p o h s -> p (o h s)"),
                                       start=True, stop=True)
                    mm.then_inc(s2_ready, 1)

                def values2(i):
                    n = g * 4 + i
                    pe.wait_ge(p2_done, n + 1)
                    for q in range(4):
                        if q < 2:
                            pe.wait_ge((pT_act, pT_dve)[q], n * 2 + 1)
                        else:
                            pe.wait_ge((pT_act, pT_dve)[q - 2], n * 2 + 2)
                        for j in range(4):
                            tr = pe.transpose(bank[4 + q % 2][0:SC, j * P:j * P + P], sc2[:, (4 * tt + i) % 2, 4 * q + j, :], ident[:, :])
                        tr.then_inc(p2_turned, 1)
                    pe.wait_ge(pT_act, n * 2 + 3)
                    pe.wait_ge(pT_dve, n * 2 + 3)
                    pe.wait_ge(o2_done, n + 1)
                    for h in range(H):
                        mm = pe.matmul(bank[6][:, h * (HD + 1):(h + 1) * (HD + 1)], pT[:, i % 2, h, :],
                                       v2[:, bass.ds(b, 1), h, :].rearrange("p o c -> p (o c)"), start=True, stop=True)
                    mm.then_inc(o2_ready, 1)

                def project2(i):
                    n = g * 4 + i
                    pe.wait_ge(o2_done, n + 2)
                    pe.wait_ge(y2_done, n + 1)
                    for c in range(C2):
                        tr = pe.transpose(bank[7][:, c * P:c * P + P], o2[:, i % 2, c * P:c * P + P], ident[:, :])
                    tr.then_inc(o2_turned, 1)
                    pe.wait_ge(o2T_done, n + 1)
                    for c in range(C2):
                        mm = pe.matmul(bank[7][:, D:2 * D], o2T[:, c, :], w_in["cwo"][:, c, :], start=(c == 0), stop=(c == C2 - 1))
                    mm.then_inc(y2_ready, 1)

                scores2(0)
                for i in range(4):
                    if i < 3:
                        scores2(i + 1)
                    values2(i)
                    if i:
                        project2(i - 1)
                project2(3)

            pe.wait_ge(mask_step, MASK_STEPS)
            with pe.Fori(0, B) as b:
                for tt in range(2):
                    cross_group(b, tt)

            pe.wait_ge(y2_done, NT + 1)
            with pe.Fori(0, TG) as g:
                pe.wait_ge(x2_done, g * 4 + 4)
                for c in range(C2):
                    for i in range(4):
                        tr = pe.transpose(bank[4 + c][:, i * P:i * P + P], x2[:, i, c * P:c * P + P], ident[:, :])
                    tr.then_inc(x2_turned, 1)
                pe.wait_ge(x2T_done, g * 2 + 2)
                for i in range(4):
                    for c in range(C2):
                        mm = pe.matmul(bank[6][:, i * NE:(i + 1) * NE], x2T[:, c, i * P:i * P + P], wg[:, c, :], start=(c == 0), stop=(c == C2 - 1))
                mm.then_inc(logits_ready, 1)
                pe.wait_ge(gates_done, g + 1)
                for i in range(4):
                    tr = pe.transpose(bank[7][0:NE, i * P:i * P + P], pick[:, 0, i, :], ident[:, :])
                tr.then_inc(gates_turned, 1)
                pe.wait_ge(gT_done, g + 1)
                for i in range(4):
                    mm = pe.matmul(bank[i // 2][:, (i % 2) * D:(i % 2 + 1) * D], gT[:, i, :], b2[:, :], start=True, stop=True)
                mm.then_inc(bias_ready, 1)
                pe.wait_ge(acc_set, g * 4 + 4)
                pe.wait_ge(x2l_done, g * 2 + 2)

            def hidden(e, eo, g):
                n = (e * 2 + eo) * TG + g
                if g == 0:
                    pe.wait_ge(w_split, (e * 2 + eo) * 5 + 5)
                (wh, wl), tok = w1[eo], slice(g * 512, g * 512 + 512)
                for fc in range(FC):
                    pe.wait_ge(hid_done, n * FC + fc + 1)
                    terms = [(w, x, c) for c in range(C2) for w, x in ((wh, x2h), (wh, x2l), (wl, x2h))]
                    for k, (w, x, c) in enumerate(terms):
                        mm = pe.matmul(bank[fc], w[:, c, fc * P:fc * P + P], x[:, c, tok], start=(k == 0), stop=(k == len(terms) - 1))
                    mm.then_inc(h_ready, 1)

            def output(e, eo, g):
                n = (e * 2 + eo) * TG + g
                wh, wl = w2[eo]
                pe.wait_ge(hl_done, n * FC + 2 * FC)
                for i in range(4):
                    pe.wait_ge(e_added, n * 4 + i + 1)
                    terms = [(a, w, fc) for fc in range(FC) for a, w in ((hh, wh), (hl, wh), (hh, wl))]
                    for k, (a, w, fc) in enumerate(terms):
                        mm = pe.matmul(bank[4 + i][:, 0:D], a[:, g % 2, fc, i * P:i * P + P], w[:, fc, :], start=(k == 0), stop=(k == len(terms) - 1))
                    mm.then_inc(e_ready, 1)

            def expert_pair(e, last):
                for k in range(2 * TG):
                    if k < 2 * TG - 1:
                        hidden(e, (k + 1) // TG, (k + 1) % TG)
                    elif not last:
                        hidden(e + 1, 0, 0)
                    output(e, k // TG, k % TG)

            hidden(0, 0, 0)
            with pe.Fori(0, NE // 2 - 1) as e:
                expert_pair(e, False)
            expert_pair(NE // 2 - 1, True)

        @block.vector
        def _(dve):
            def split(n):
                hi, mid, low = (parts[:, n % 3, i, :] for i in range(3))
                dve.wait_ge(hi_done, n + 1)
                dve.tensor_tensor(rest[:, n % 2, :], bank[n % 4], hi, ALU.subtract).then_inc(rest_done, 1)
                dve.wait_ge(rest_done, n + 1)
                dve.tensor_copy(mid, rest[:, n % 2, :]).then_inc(mid_done, 1)
                dve.wait_ge(mid_done, n + 1)
                dve.tensor_tensor(low, rest[:, n % 2, :], mid, ALU.subtract).then_inc(parts_done, 1)

            for n in range(QK_JOBS):
                split(n)
            dve.wait_ge(cross_ready, 2)
            dve.tensor_tensor(v2[:, :, :, 0:HD].rearrange("p b h d -> p b h d"),
                              bank[7][0:SC, :].rearrange("p (b h d) -> p b h d", b=B, d=HD),
                              rows["cbv"][0:SC, :].rearrange("p (o h d) -> p o h d", o=1, d=HD).to_broadcast([SC, B, H, HD]),
                              ALU.add).then_inc(v2_done, 1)

            def reduce_max(u, k, p):
                dve.wait_ge(max_ready, u * 16 + p + 1)
                dve.tensor_reduce(rowmax[:, k % 2, p:p + 1], quad[:, 2 * (p % 2):2 * (p % 2) + 2, :].rearrange("p a n -> p (a n)"),
                                  AX_X, ALU.max).then_inc(max_taken, 1)

            def negate(u, k):
                m, hi, low = rowmax[:, k % 2, :], negparts[:, k % 2, 0:16], negparts[:, k % 2, 16:32]
                dve.wait_ge(max_taken, u * 16 + 18)
                dve.tensor_scalar(hi, m, -1.0, None, ALU.mult).then_inc(neg_hi, 1)
                dve.wait_ge(neg_hi, u + 1)
                dve.scalar_tensor_tensor(low, m, -1.0, hi, ALU.mult, ALU.subtract).then_inc(neg_parts, 1)
                dve.wait_ge(neg_turned, u + 1)
                dve.tensor_copy(negrows[:, k % 2, :], bank[7].bitcast(BF16)[0:32, 0:P]).then_inc(neg_rows, 1)

            for p in range(16):
                reduce_max(0, 0, p)
            negate(0, 0)
            for p in range(AHEAD):
                reduce_max(1, 1, p)

            def unit(it, k, last):
                u = it * 4 + k
                if not (last and k == 3):
                    for p in range(AHEAD, 16):
                        reduce_max(u + 1, k + 1, p)
                    negate(u + 1, k + 1)
                if not (last and k + 2 > 3):
                    for p in range(AHEAD):
                        reduce_max(u + 2, k + 2, p)
                sums = bank[7].rearrange("p (q j c) -> p q j c", q=4, c=VW)
                dve.wait_ge(o_turned, u + 2)
                dve.reciprocal(rden[:, :].rearrange("p (q j) -> p q j", q=4), sums[:, :, :, HD]).then_inc(o_recip, 1)
                dve.wait_ge(o_recip, u + 1)
                inv = rden[:, :].rearrange("p (q j o) -> p q j o", q=4, o=1).to_broadcast([P, 4, GH, HD])
                dst = attn[:, bass.ds(it, 1), k, :, :].rearrange("p o q (j d) -> p (o q) j d", d=HD)
                dve.tensor_tensor(dst, sums[:, :, :, 0:HD], inv, ALU.mult).then_inc(o_normed, 1)

            with dve.Fori(0, 3) as it:
                for k in range(4):
                    unit(it, k, False)
            for k in range(4):
                unit(3, k, True)


            links = [0]

            def link(ins):
                ins.then_inc(chain, 1)
                links[0] += 1
                dve.wait_ge(chain, links[0])

            roots = [0]
            MEAN, VAR, RSTD, T0, T1, ROOT = range(6)

            def moments():
                row = [lnv[:, i, :] for i in range(8)]
                me, ve, mo, vo = (stats[:, :, i] for i in (1, 2, 4, 5))
                link(dve.tensor_tensor(row[T0], me, mo, ALU.add))
                link(dve.tensor_scalar(row[MEAN], row[T0], 0.5, None, ALU.mult))
                link(dve.tensor_tensor(row[T0], me, mo, ALU.subtract))
                link(dve.tensor_tensor(row[T0], row[T0], row[T0], ALU.mult))
                link(dve.tensor_tensor(row[T1], ve, vo, ALU.add))
                link(dve.tensor_scalar(row[T1], row[T1], 1.0 / D, EPS, ALU.mult, ALU.add))
                dve.scalar_tensor_tensor(row[VAR], row[T0], 0.25, row[T1], ALU.mult, ALU.add).then_inc(root_wanted, 1)
                roots[0] += 1
                dve.wait_ge(root_done, roots[0])
                link(dve.reciprocal(row[T0], row[ROOT]))
                link(dve.tensor_tensor(row[T0], row[VAR], row[T0], ALU.mult))
                link(dve.tensor_tensor(row[T0], row[T0], row[ROOT], ALU.add))
                link(dve.reciprocal(row[T0], row[T0]))
                link(dve.tensor_scalar(row[RSTD], row[T0], 2.0, None, ALU.mult))

            attn_v = attn[:, :, :, :, :].rearrange("p (b g) (f h) q c -> p b h q g f c", b=B, h=2)
            dve.wait_ge(loaded["x_loaded"], 16 * (LATE + 1))
            dve.wait_ge(o_normed, UNITS + 1)
            dve.wait_ge(mask_step, MASK_STEPS)
            for n in range(NT):
                b, h, q = n // 8, n // 4 % 2, n % 4
                link(dve.tensor_tensor(xres[:, n, :].rearrange("p (g f c) -> p g f c", g=2, f=2),
                                       xres[:, n, :].rearrange("p (g f c) -> p g f c", g=2, f=2), attn_v[:, b, h, q], ALU.add))
                link(dve.bn_stats(stats[:, n, :], xres[:, n, :]))
            moments()

            def norm_tile(out, n, src=xres):
                return dve.tensor_scalar(out, src[:, bass.ds(n, 1), :].rearrange("p o d -> p (o d)"),
                                         lnv[:, MEAN, bass.ds(n, 1)], lnv[:, RSTD, bass.ds(n, 1)], ALU.subtract, ALU.mult)

            def cross_group(b, tt):
                g = b * 2 + tt
                dve.wait_ge(x1b_done, g + 1)
                for i in range(4):
                    norm_tile(x1[:, i, :], g * 4 + i).then_inc(x1_done, 1)

                def take(i):
                    n = g * 4 + i
                    dve.wait_ge(s2_ready, n + 1)
                    dve.wait_ge(p2_turned, n * 4 + 4)
                    dve.tensor_tensor(sc2[:, i % 2, :, :].rearrange("p (e h) s -> p e h s", e=4),
                                      quad[:, :, 0:4 * SC].rearrange("p e (h s) -> p e h s", s=SC),
                                      keep[:, bass.ds(n, 1), :].rearrange("p o (u s) -> p o u s", u=1).to_broadcast([P, 4, 4, SC]),
                                      ALU.mult).then_inc(s2_taken, 1)

                def rowmax2(i):
                    n = g * 4 + i
                    dve.wait_ge(s2_filled, n + 1)
                    dve.tensor_reduce(max2[:, i % 2, :], sc2[:, i % 2, :, :], AX_X, ALU.max).then_inc(s2_max, 1)

                def copy_turned(i):
                    n = g * 4 + i
                    dve.wait_ge(o2_ready, n + 1)
                    for q in (1, 3):
                        dve.wait_ge(p2_turned, n * 4 + q + 1 + 8)
                        dve.tensor_copy(pT[:, i % 2, 4 * q:4 * q + 4, :].rearrange("p h q -> p (h q)"), bank[5][0:SC, :]).then_inc(pT_dve, 1)

                def normalise2(i):
                    n = g * 4 + i
                    dve.wait_ge(o2_ready, n + 3)
                    o = bank[6][:, 0:H * (HD + 1)].rearrange("p (h c) -> p h c", c=HD + 1)
                    dve.reciprocal(rden2[:, :], o[:, :, HD]).then_inc(o2_recip, 1)
                    dve.wait_ge(o2_recip, n + 1)
                    dve.tensor_tensor(o2[:, i % 2, :].rearrange("p (h d) -> p h d", d=HD), o[:, :, 0:HD],
                                      rden2[:, :].rearrange("p (h o) -> p h o", o=1).to_broadcast([P, H, HD]), ALU.mult).then_inc(o2_done, 1)

                def residual2(i):
                    n = g * 4 + i
                    dve.wait_ge(y2_ready, n + 1)
                    dve.wait_ge(x1b_done, g + 2)
                    dve.tensor_tensor(xres[:, bass.ds(n, 1), :].rearrange("p o d -> p (o d)"), bank[7][:, D:2 * D], x1b[:, i, :],
                                      ALU.add).then_inc(y2_done, 1)

                take(0)
                rowmax2(0)
                for i in range(4):
                    if i < 3:
                        take(i + 1)
                    copy_turned(i)
                    if i < 3:
                        rowmax2(i + 1)
                    normalise2(i)
                    if i:
                        residual2(i - 1)
                residual2(3)

            with dve.Fori(0, B) as b:
                for tt in range(2):
                    cross_group(b, tt)

            dve.wait_ge(y2_done, NT + 1)
            for n in range(NT):
                bn = dve.bn_stats(stats[:, n, :], xres[:, n, :])
            link(bn)
            moments()

            with dve.Fori(0, TG) as g:
                dve.wait_ge(x2_turned, g * 2 + 1)
                for i in range(4):
                    norm_tile(x2[:, i, :], g * 4 + i).then_inc(x2_done, 1)
                for c in range(C2):
                    dve.wait_ge(x2h_done, g * 2 + c + 1)
                    dve.tensor_tensor(x2l[:, c, bass.ds(g * 512, 512)], bank[4 + c], x2h[:, c, bass.ds(g * 512, 512)],
                                      ALU.subtract).then_inc(x2l_done, 1)
                steps = [0]

                def step(ins):
                    ins.then_inc(gate_step, 1)
                    steps[0] += 1
                    dve.wait_ge(gate_step, g * GATE_STEPS + steps[0])

                dve.wait_ge(logits_ready, g + 1)
                step(dve.tensor_tensor(logits[:, :, :], bank[6][:, 0:4 * NE].rearrange("p (i e) -> p i e", e=NE),
                                       bg[:, :].rearrange("p (o e) -> p o e", o=1).to_broadcast([P, 4, NE]), ALU.add))
                for i in range(4):
                    norm_tile(xres[:, bass.ds(g * 4 + i, 1), :].rearrange("p o d -> p (o d)"), g * 4 + i)
                for i in range(4):
                    mx = dve.max(top[:, i, :], logits[:, i, :])
                step(mx)
                dve.tensor_tensor(gw[:, :, 0], top[:, :, 1], top[:, :, 0], ALU.subtract).then_inc(gap_done, 1)
                for i in range(4):
                    mx = dve.max_index(topi[:, i, :], top[:, i, :], logits[:, i, :])
                step(mx)
                step(dve.tensor_copy(topf[:, :, :], topi[:, :, :]))
                for j in range(2):
                    step(dve.tensor_tensor(pick[:, j, :, :], iota8[:, :].rearrange("p (o e) -> p o e", o=1).to_broadcast([P, 4, NE]),
                                           topf[:, :, j:j + 1].to_broadcast([P, 4, NE]), ALU.is_equal))
                dve.wait_ge(gap_exp, g + 1)
                step(dve.tensor_scalar(gw[:, :, 3], gw[:, :, 1], 1.0, None, ALU.add))
                step(dve.reciprocal(gw[:, :, 2], gw[:, :, 3]))
                step(dve.tensor_tensor(gw[:, :, 3], gw[:, :, 1], gw[:, :, 2], ALU.mult))
                for j in range(2):
                    step(dve.tensor_tensor(pick[:, j, :, :], pick[:, j, :, :], gw[:, :, 2 + j:3 + j].to_broadcast([P, 4, NE]), ALU.mult))
                step(dve.tensor_tensor(pick[:, 0, :, :], pick[:, 0, :, :], pick[:, 1, :, :], ALU.add))
                dve.tensor_copy(gates[:, bass.ds(g * 4, 4), :], pick[:, 0, :, :]).then_inc(gates_done, 1)
                dve.wait_ge(gates_turned, g + 1)
                dve.tensor_copy(gT[:, :, :].rearrange("p i t -> p (i t)"), bank[7][0:NE, :]).then_inc(gT_done, 1)
                dve.wait_ge(bias_ready, g + 1)
                for i in range(4):
                    dve.tensor_tensor(acc[:, bass.ds(g * 4 + i, 1), :].rearrange("p o d -> p (o d)"),
                                      bank[i // 2][:, (i % 2) * D:(i % 2 + 1) * D],
                                      xres[:, bass.ds(g * 4 + i, 1), :].rearrange("p o d -> p (o d)"), ALU.add).then_inc(acc_set, 1)
                assert steps[0] == GATE_STEPS

            dve.wait_ge(gates_done, TG)
            dve.wait_ge(acc_set, NT)

            def split_hidden(e, eo, g):
                n = (e * 2 + eo) * TG + g
                for fc in range(FC):
                    m = n * FC + fc
                    dve.wait_ge(hid_done, m + FC + 1)
                    if fc == 0:
                        dve.wait_ge(e_ready, n * 4 + (EC - 4))
                    dve.tensor_copy(hh[:, g % 2, fc, :], hid[:, fc, :]).then_inc(hh_done, 1)
                    dve.wait_ge(hh_done, m + 1)
                    dve.tensor_tensor(hl[:, g % 2, fc, :], hid[:, fc, :], hh[:, g % 2, fc, :], ALU.subtract).then_inc(hl_done, 1)

            def add_expert(e, eo, g):
                n = (e * 2 + eo) * TG + g
                for i in range(4):
                    dve.wait_ge(e_ready, n * 4 + (i + 1 + EC))
                    if i == 0:
                        dve.wait_ge(e_added, n * 4 + 4)
                    dve.scalar_tensor_tensor(acc[:, g * 4 + i, :], bank[4 + i][:, 0:D],
                                             gates[:, g * 4 + i, bass.ds(e * 2 + eo, 1)], acc[:, g * 4 + i, :],
                                             ALU.mult, ALU.add).then_inc(e_added, 1)

            def expert_pair(e, last):
                for k in range(2 * TG):
                    if k < 2 * TG - 1:
                        split_hidden(e, (k + 1) // TG, (k + 1) % TG)
                    elif not last:
                        split_hidden(e + 1, 0, 0)
                    add_expert(e, k // TG, k % TG)

            split_hidden(0, 0, 0)
            with dve.Fori(0, NE // 2 - 1) as e:
                expert_pair(e, False)
            expert_pair(NE // 2 - 1, True)

            dve.wait_ge(e_added, 4 * NE * TG + 4)
            for n in range(NT):
                bn = dve.bn_stats(stats[:, n, :], acc[:, n, :])
            link(bn)
            moments()
            for n in range(NT):
                link(dve.tensor_scalar(acc[:, n, :], acc[:, n, :], lnv[:, MEAN, n:n + 1], lnv[:, RSTD, n:n + 1], ALU.subtract, ALU.mult))
                link(dve.tensor_tensor(acc[:, n, :], acc[:, n, :], rows["gamma"][:, :], ALU.mult))
                link(dve.tensor_tensor(acc[:, n, :], acc[:, n, :], rows["beta"][:, :], ALU.add))
                link(dve.tensor_tensor(acc[:, n, :], acc[:, n, :], xres[:, n, :], ALU.add))
                link(dve.bn_stats(stats[:, n, :], acc[:, n, :]))
            moments()
            for n in range(NT):
                dve.tensor_scalar(acc[:, n, :], acc[:, n, :], lnv[:, MEAN, n:n + 1], lnv[:, RSTD, n:n + 1],
                                  ALU.subtract, ALU.mult).then_inc(out_done, 1)

        @block.scalar
        def _(act):
            def high(n):
                act.wait_ge(qk_ready, n + 1)
                if n >= 3:
                    act.wait_ge(parts_stored[n % 3], 96 * (n // 3))
                act.activation(parts[:, n % 3, 0, :], bank[n % 4], ACT.Copy).then_inc(hi_done, 1)

            def keep_values(m):
                act.wait_ge(v_ready, m + 1)
                g, pair = m // 2, m % 2
                for i in range(2):
                    tile = 4 * g + 2 * pair + i
                    b, kt = tile // KT, tile % KT
                    cp = act.activation(v_all[:, b * NG:(b + 1) * NG, kt, :, 0:HD],
                                        bank[4 + m % 2][:, i * D:(i + 1) * D].rearrange("p (g j d) -> p g j d", g=NG, d=HD), ACT.Copy)
                cp.then_inc(v_done, 1)

            act.wait_ge(v_zeroed, 2)
            for g in range(TG):
                for job in range(4):
                    high(4 * g + job)
                keep_values(2 * g)
                keep_values(2 * g + 1)
            act.wait_ge(cross_ready, 1)
            for half in range(2):
                cp = act.activation(k2T[:, half, :], bank[6][:, half * B * SC:(half + 1) * B * SC], ACT.Identity, bias=cbk[:, half:half + 1])
            cp.then_inc(k2_done, 1)

            def exps(u, k, i):
                n = u * STEPS + i
                act.wait_ge(scores_ready, n + 1)
                act.wait_ge(probs_used, n + 1)
                act.activation(probs[:, i % PR, :], bank[4 + i % 2], ACT.Exp, scale=INV4).then_inc(probs_ready, 1)

            def unit(it, k):
                u = it * 4 + k
                for i in range(STEPS):
                    exps(u, k, i)
                act.wait_ge(probs_used, u * STEPS + STEPS + PR)
                act.wait_ge(o_turned, u + 1)
                act.activation(outT[:, :], bank[6], ACT.Copy).then_inc(o_copied, 1)

            with act.Fori(0, 4) as it:
                for k in range(4):
                    unit(it, k)


            def root(k):
                act.wait_ge(root_wanted, k)
                act.activation(lnv[:, 5, :], lnv[:, 1, :], ACT.Sqrt).then_inc(root_done, 1)

            root(1)

            def cross_group(b, tt):
                g = b * 2 + tt
                for c in range(C2):
                    act.wait_ge(x1_turned, g * 2 + c + 1)
                    act.activation(x1T[:, c, :], bank[4 + c], ACT.Copy).then_inc(x1T_done, 1)
                for half in range(2):
                    act.wait_ge(q2_ready, g * 2 + half + 1)
                    act.activation(q2T[:, half, :], bank[6 + half], ACT.Identity, bias=cbq[:, half:half + 1]).then_inc(q2_done, 1)

                def exp2(i):
                    n = g * 4 + i
                    act.wait_ge(s2_shifted, n + 1)
                    act.activation(sc2[:, i % 2, :, :], sc2[:, i % 2, :, :], ACT.Exp, scale=INV4).then_inc(p2_done, 1)

                def copy_turned(i):
                    n = g * 4 + i
                    act.wait_ge(o2_ready, n + 1)
                    for q in (0, 2):
                        act.wait_ge(p2_turned, n * 4 + q + 1 + 8)
                        act.activation(pT[:, i % 2, 4 * q:4 * q + 4, :].rearrange("p h q -> p (h q)"), bank[4][0:SC, :], ACT.Copy).then_inc(pT_act, 1)

                def copy_o(i):
                    n = g * 4 + i
                    act.wait_ge(o2_turned, n + 1)
                    act.activation(o2T[:, :, :].rearrange("p c q -> p (c q)"), bank[7][:, 0:D], ACT.Copy).then_inc(o2T_done, 1)

                exp2(0)
                for i in range(4):
                    copy_turned(i)
                    if i < 3:
                        exp2(i + 1)
                    if i:
                        copy_o(i - 1)
                copy_o(3)

            with act.Fori(0, B) as b:
                for tt in range(2):
                    cross_group(b, tt)
            root(2)
            with act.Fori(0, TG) as g:
                for c in range(C2):
                    act.wait_ge(x2_turned, g * 2 + c + 2)
                    act.activation(x2T[:, c, :], bank[4 + c], ACT.Copy).then_inc(x2T_done, 1)
                    act.activation(x2h[:, c, bass.ds(g * 512, 512)], bank[4 + c], ACT.Copy).then_inc(x2h_done, 1)
                act.wait_ge(gap_done, g + 1)
                act.activation(gw[:, :, 1], gw[:, :, 0], ACT.Exp).then_inc(gap_exp, 1)

            def relu(e, eo, g):
                n = (e * 2 + eo) * TG + g
                for fc in range(FC):
                    m = n * FC + fc
                    act.wait_ge(h_ready, m + 1)
                    act.wait_ge(hl_done, m + 1)
                    if g == 0 and fc == 0:
                        act.wait_ge(w_split, (e * 2 + eo) * 5 + 5)
                    act.activation(hid[:, fc, :], bank[fc], ACT.Relu, bias=b1e[:, eo, fc:fc + 1]).then_inc(hid_done, 1)

            with act.Fori(0, NE // 2) as e:
                for eo in range(2):
                    for g in range(TG):
                        relu(e, eo, g)
            root(3)
            root(4)

        @block.gpsimd
        def _(pool):
            pool.memset(v_all[:, :, :, :, HD:HD + 1], 1.0).then_inc(v_zeroed, 1)
            pool.wait_ge(v_zeroed, 1)
            pool.memset(v_all[:, :, :, :, HD + 1:VW], 0.0).then_inc(v_zeroed, 1)
            pool.wait_ge(v_zeroed, 2)
            for i in range(2):
                pool.memset(kstack[i][MAXROW:P, :, :], 1.0).then_inc(ones_set, 1)
                pool.wait_ge(ones_set, i + 1)
            pool.memset(credit[:, 0:1], 0.0).then_inc(max_taken, 2)
            pool.wait_ge(max_taken, 2)
            pool.memset(credit[:, 1:2], 0.0).then_inc(probs_ready, 2)
            pool.wait_ge(probs_ready, 2)
            pool.memset(credit[:, 2:3], 0.0).then_inc(probs_used, PR)
            pool.wait_ge(probs_used, PR)
            pool.wait_ge(loaded["const_loaded"], 16)
            pool.tensor_copy(ident16[:, :], ident[:, :]).then_inc(ones_set, 1)
            for i, (s_, k_) in enumerate(((o_copied, 1), (o_turned, 1), (o_normed, 1), (x1b_done, 1), (pT_act, 1), (pT_dve, 1), (o2_done, 1),
                           (y2_done, 1), (s2_taken, 1), (p2_turned, 8), (o2_ready, 2), (x2_turned, 1), (hid_done, FC),
                           (e_added, 4), (e_ready, EC), (hl_done, FC))):
                pool.wait_ge(ones_set, 3 + i)
                pool.memset(credit[:, 3:4], 0.0).then_inc(s_, k_)
                pool.wait_ge(s_, k_)
                pool.memset(credit[:, 4:5], 0.0).then_inc(ones_set, 1)
            count = [0]

            def step(ins):
                ins.then_inc(mask_step, 1)
                count[0] += 1
                pool.wait_ge(mask_step, count[0])

            pool.wait_ge(mask_loaded, 16)
            step(pool.memset(v2[:, :, :, HD:HD + 1], 1.0))
            step(pool.memset(one[:, :], 1.0))
            step(pool.tensor_scalar(fill[:, :, :], maski[:, :, :], 0.0, MASKED, ALU.is_equal, ALU.mult))
            step(pool.tensor_scalar(keep[:, :, :], maski[:, :, :], 0.0, -1.0, ALU.is_equal, ALU.mult))
            step(pool.tensor_scalar(keep[:, :, :], keep[:, :, :], 1.0, None, ALU.add))
            pool.wait_ge(k2_done, 1)
            for b in range(B):
                for half in range(2):
                    step(pool.tensor_tensor(kbd[:, b, half, :, :],
                                            k2T[:, half, b * SC:(b + 1) * SC].rearrange("p (o s) -> p o s", o=1).to_broadcast([P, 8, SC]),
                                            block8[:, :].rearrange("p (h o) -> p h o", o=1).to_broadcast([P, 8, SC]), ALU.mult))
            assert count[0] == MASK_STEPS

            def cross_group(b, tt):
                g = b * 2 + tt
                pool.wait_ge(x1_done, g * 4 + 4)
                pool.wait_ge(y2_done, g * 4 + 1)
                pool.tensor_tensor(x1b[:, :, :], x1[:, :, :], rows["cbo"][:, :].rearrange("p (o d) -> p o d", o=1).to_broadcast([P, 4, D]),
                                   ALU.add).then_inc(x1b_done, 1)
                for i in range(4):
                    n = g * 4 + i
                    sc = sc2[:, i % 2, :, :]
                    pool.wait_ge(s2_taken, n + 2)
                    pool.tensor_tensor(sc, sc, fill[:, bass.ds(n, 1), :].to_broadcast([P, H, SC]), ALU.add).then_inc(s2_filled, 1)
                    pool.wait_ge(s2_max, n + 1)
                    pool.tensor_tensor(sc, sc, max2[:, i % 2, :].rearrange("p (h o) -> p h o", o=1).to_broadcast([P, H, SC]),
                                       ALU.subtract).then_inc(s2_shifted, 1)

            with pool.Fori(0, B) as b:
                for tt in range(2):
                    cross_group(b, tt)

            def split_weights(e, eo):
                m = e * 2 + eo
                pool.wait_ge(e_ready, m * 16 + (EC - 16))
                for k, (raw, w) in enumerate(((w1raw, w1), (w2raw, w2))):
                    pool.wait_ge(w_fetched[k], m * 16 + 16)
                    pool.tensor_tensor(w[eo][0][:, :, :], raw[:, :, :], one[:, :].rearrange("p (a b) -> p a b", a=1).to_broadcast(list(raw.shape)), ALU.mult).then_inc(w_split, 1)
                    if k == 0:
                        pool.tensor_copy(b1e[:, eo, :].rearrange("p (o c) -> p o c", o=1), b1[:, bass.ds(m, 1), :]).then_inc(w_split, 1)
                    pool.wait_ge(w_split, m * 5 + (2, 4)[k])
                    pool.tensor_tensor(w[eo][1][:, :, :], raw[:, :, :], w[eo][0][:, :, :], ALU.subtract).then_inc(w_split, 1)

            with pool.Fori(0, NE // 2) as e:
                for eo in range(2):
                    split_weights(e, eo)


def kernel(**inputs):
    import numpy as np
    import concourse.bacc as bacc
    from concourse.bass_utils import run_bass_kernel_spmd as run

    x = np.ascontiguousarray(inputs["x"]).reshape(B * S, D)
    def a(name):
        return np.ascontiguousarray(inputs[name])

    arrays = {
        "ctxT": np.ascontiguousarray(a("ctx_1024").reshape(B * SC, D).T), "mask": a("mask_BxSxS2_ik1").reshape(B * S, SC),
        "cwq": a("L0_xattn_Wq"), "cwk": a("L0_xattn_Wk"), "cwv": a("L0_xattn_Wv"), "cwo": a("L0_xattn_Wo"),
        "cbq": a("L0_xattn_bq"), "cbk": a("L0_xattn_bk"), "cbv": a("L0_xattn_bv"), "cbo": a("L0_xattn_bo"),
        "wg": a("L0_ffn_Wg"), "bg": a("L0_ffn_bg"), "w1": a("L0_ffn_W1"), "b1": a("L0_ffn_b1"),
        "w2": a("L0_ffn_W2"), "b2": a("L0_ffn_b2"), "gamma": a("L0_ffn_gamma"), "beta": a("L0_ffn_beta"),
        "x": x, "xT": np.ascontiguousarray(x.T),
        "wqT": np.ascontiguousarray(np.asarray(inputs["L0_attn_Wq"]).T),
        "wkT": np.ascontiguousarray(np.asarray(inputs["L0_attn_Wk"]).T),
        "wvT": np.ascontiguousarray(np.asarray(inputs["L0_attn_Wv"]).T),
        "ident": np.eye(P, dtype=np.float32),
        "block8": np.repeat(np.eye(8, dtype=np.float32), HD, axis=0),
        "iota8": np.tile(np.arange(NE, dtype=np.float32), (P, 1)),
    }
    nc = bacc.Bacc("TRN2", target_bir_lowering=False, num_devices=1)
    t = {n: nc.dram_tensor(f"in_{n}", a.shape, mybir.dt.from_np(a.dtype), kind="ExternalInput").ap() for n, a in arrays.items()}
    t["out"] = nc.dram_tensor("out_y", (B * S, D), F32, kind="ExternalOutput").ap()
    build(nc, t)
    r = run(nc, [{f"in_{n}": a for n, a in arrays.items()}], core_ids=[0])
    return r.results[0]["out_y"].reshape(B, S, D)
```

```python
from contextlib import ExitStack

import concourse.bass as bass
from concourse import mybir

ALU = mybir.AluOpType
ACT = mybir.ActivationFunctionType
AX_X = mybir.AxisListType.X
F32 = mybir.dt.float32
BF16 = mybir.dt.bfloat16
I32 = mybir.dt.int32
U32 = mybir.dt.uint32

P = 128
B, S, D = 2, 1024, 256
H, HD = 16, 16
SC = 77
NE, F = 8, 512
NT = B * S // P
C2 = D // P
TG = B * S // 512
GH = 4
NG = H // GH
NGRP = B * NG
KT = S // P
UNITS = 2 * NGRP
STEPS = KT * GH
VW = 32
PR = 8
EPS = 1e-5
INV4 = 0.25
MASKED = -4.0e9
NO_CAP = 3.0e38
SR = 4
FAR = 3
HALF = H // 2
VC = -(-HALF * SC // P)
VROWS = [min(P, HALF * SC - c * P) for c in range(VC)]
TURNS = [[(h, c) for c in range(VC - 1)] for h in range(2)] + [[(h, VC - 1) for h in range(2)]]
V_RUNS = []
for _h in range(HALF):
    _s = 0
    while _s < SC:
        _r = _h * SC + _s
        _n = min(SC - _s, P - _r % P)
        V_RUNS.append((_h, _s, _n, _r // P, _r % P))
        _s += _n
MAXROW = 96
KROWS = 98
AHEAD = 6
Q_BLOCKS = ((0, 0, 3), (48, 0, 2), (80, 0, 1))
K_BLOCKS = ((0, 0, 1), (16, 0, 1), (32, 0, 1), (48, 1, 1), (64, 1, 1), (80, 2, 1))
EC = 17
MASK_STEPS = 9
LATE = 17
LOADS = len(Q_BLOCKS) + len(K_BLOCKS)
FC = F // P


def build(nc, t):
    with ExitStack() as ctx:
        def sb(name, shape, dt=F32):
            return ctx.enter_context(nc.sbuf_tensor(name, shape, dt))

        def sem(name):
            return ctx.enter_context(nc.semaphore(name))

        bank = [ctx.enter_context(nc.psum_tensor(f"bank{i}", [P, 512], F32)) for i in range(4, 8)]
        quad = ctx.enter_context(nc.psum_tensor("quad", [P, 4, 512], F32))
        bank = [quad[:, i, :] for i in range(4)] + [b[:, :] for b in bank]
        scratch = {w: nc.dram_tensor(f"{w}_parts", (2 * B, 3, HD, 2 * GH * S), BF16, kind="Internal").ap()
                   for w in "qk"}

        ident = sb("ident", [P, P])
        ident16 = sb("ident16", [P, P], BF16)
        block8 = sb("block8", [P, 8])
        iota8 = sb("iota8", [P, NE])
        w_in = {n: sb(n, [P, C2, D]) for n in ("wq", "wk", "wv", "cwq", "cwk", "cwv", "cwo")}
        xres = sb("xres", [P, NT, D])
        attn = sb("attn", [P, 4, 4, 4, GH * HD])
        acc = attn[:, :, :, :, :].rearrange("p a k q c -> p (a k q c)").rearrange("p (n d) -> p n d", d=D)
        stats = sb("stats", [P, NT, 6])
        lnv = sb("lnv", [P, 8, NT])
        ctxT = sb("ctxT", [P, C2, B * SC])
        k2T = sb("k2T", [P, 2, B * SC])
        kbd = sb("kbd", [P, B, 2, 8, SC])
        v2 = sb("v2", [SC, B, D])
        vbd = sb("vbd", [P, B, 2, VC, P])
        cap = sb("cap", [P, NT, SC])
        maski = cap[:, :, :].bitcast(I32)
        power = sb("power", [P, NT])
        rows = {n: sb(f"{n}_row", [P, D]) for n in ("cbv", "cbo", "gamma", "beta")}
        cbq, cbk = sb("cbq", [P, 2]), sb("cbk", [P, 2])
        wg = sb("wg", [P, C2, NE])
        bg = sb("bg", [P, NE])
        b1 = sb("b1", [P, NE, FC])
        one = sb("one", [P, 1])
        b1e = sb("b1e", [P, 2, FC])
        b2d = sb("b2d", [P, 4, D])
        credit = sb("credit", [P, 8])
        first = ctx.enter_context(ExitStack())

        def sb1(name, shape, dt=F32):
            return first.enter_context(nc.sbuf_tensor(name, shape, dt))

        xT = sb1("xT", [P, C2, B * S])
        parts = sb1("parts", [P, 3, 3, 512], BF16)
        rest = sb1("rest", [P, 2, 512])
        qstack = [sb1(f"qstack{i}", [P, 2, GH, 512], BF16) for i in range(2)]
        kstack = [sb1(f"kstack{i}", [P, GH, S], BF16) for i in range(2)]
        v_all = sb1("v_all", [P, NGRP, KT, GH, VW])
        vslot = [sb1(f"vslot{i}", [P, KT, GH, VW]) for i in range(2)]
        probs = sb1("probs", [P, PR, 512])
        rowmax = sb1("rowmax", [P, 2, 16])
        negparts = sb1("negparts", [P, 2, 32], BF16)
        negrows = sb1("negrows", [32, 2, P], BF16)
        outT = sb1("outT", [P, 512])
        rden = sb1("rden", [P, 16])
        first.close()
        w1raw = sb("w1raw", [P, C2, F])
        w2raw = sb("w2raw", [P, FC, D])
        w1 = [[sb(f"w1_{i}{j}", [P, C2, F], BF16) for j in "hl"] for i in range(2)]
        w2 = [[sb(f"w2_{i}{j}", [P, FC, D], BF16) for j in "hl"] for i in range(2)]
        second = ctx.enter_context(ExitStack())

        def sb2(name, shape, dt=F32):
            return second.enter_context(nc.sbuf_tensor(name, shape, dt))

        x1 = sb2("x1", [P, 4, D])
        x1T = sb2("x1T", [P, C2, 512])
        q2T = sb2("q2T", [P, 2, 512])
        sc2 = sb2("sc2", [P, SR, H, SC])
        max2 = sb2("max2", [P, SR, H])
        sum2 = sb2("sum2", [P, SR, H])
        inv2 = sb2("inv2", [P, SR, H])
        pT = sb2("pT", [P, 2, VC, 512])
        o2T = sb2("o2T", [P, 2, 512])
        second.close()
        x2T = sb("x2T", [P, C2, B * S])
        x2h = sb("x2h", [P, C2, B * S], BF16)
        x2l = sb("x2l", [P, C2, B * S], BF16)
        logits = sb("logits", [P, NT, NE])
        top = sb("top", [P, NT, 8])
        topi = sb("topi", [P, NT, 8], U32)
        topf = sb("topf", [P, NT, 8])
        gw = sb("gw", [P, NT, 4])
        pick = sb("pick", [P, 2, NT, NE])
        gates = sb("gates", [P, NT, NE])
        gT = sb("gT", [P, P])
        hid = sb("hid", [P, 4, 512])
        hh = sb("hh", [P, 2, FC, 512], BF16)
        hl = sb("hl", [P, 2, FC, 512], BF16)

        loaded = {n: sem(n) for n in ("w_loaded", "const_loaded", "x_loaded")}
        xT_loaded = [sem(f"xT_loaded{i}") for i in range(TG)]
        qk_ready, hi_done, rest_done, mid_done, parts_done = map(sem, ("qk_ready", "hi_done", "rest_done", "mid_done", "parts_done"))
        parts_stored = [sem(f"parts_stored{i}") for i in range(3)]
        v_ready, v_done, v_zeroed = sem("v_ready"), sem("v_done"), sem("v_zeroed")
        ones_set = sem("ones_set")
        stack_loaded = [sem(f"stack_loaded{i}") for i in range(2)]
        vslot_loaded = [sem(f"vslot_loaded{i}") for i in range(2)]
        max_ready, max_taken = sem("max_ready"), sem("max_taken")
        neg_hi, neg_parts, neg_turned, neg_rows = map(sem, ("neg_hi", "neg_parts", "neg_turned", "neg_rows"))
        neg_loaded = sem("neg_loaded")
        scores_ready, probs_ready, probs_used = map(sem, ("scores_ready", "probs_ready", "probs_used"))
        o_copied, o_turned, o_recip, o_normed = map(sem, ("o_copied", "o_turned", "o_recip", "o_normed"))
        out_stored = sem("out_stored")
        mask_loaded, mask_step, kbd_done = sem("mask_loaded"), sem("mask_step"), sem("kbd_done")
        cross_ready, k2_done, v2_done = sem("cross_ready"), sem("k2_done"), sem("v2_done")
        chain, y1_done, root_wanted, root_done = map(sem, ("chain", "y1_done", "root_wanted", "root_done"))
        x1_done, x1_turned, x1T_done, x1b_done = map(sem, ("x1_done", "x1_turned", "x1T_done", "x1b_done"))
        v2_placed, v2_zeroed = sem("v2_placed"), sem("v2_zeroed")
        q2_ready, q2_done = sem("q2_ready"), sem("q2_done")
        s2_ready, s2_taken, s2_max, s2_shifted, p2_exp = map(sem, ("s2_ready", "s2_taken", "s2_max", "s2_shifted", "p2_exp"))
        s2_summed, s2_recip, p2_done, p2_turned, pT_done = map(sem, ("s2_summed", "s2_recip", "p2_done", "p2_turned", "pT_done"))
        o2_ready, o2T_done = sem("o2_ready"), sem("o2T_done")
        y2_ready, y2_done = sem("y2_ready"), sem("y2_done")
        x2_done, x2_turned, x2T_done, x2h_done, x2l_done = map(sem, ("x2_done", "x2_turned", "x2T_done", "x2h_done", "x2l_done"))
        logits_ready, gap_done, gap_exp, stat_done, mom_done = map(sem, ("logits_ready", "gap_done", "gap_exp", "stat_done", "mom_done"))
        pool_chain, xb_done = sem("pool_chain"), sem("xb_done")
        gates_done, gates_turned, gT_done, bias_ready, acc_set = map(sem, ("gates_done", "gates_turned", "gT_done", "bias_ready", "acc_set"))
        w_fetched = [sem("w1_fetched"), sem("w2_fetched")]
        out_done = sem("out_done")
        w_split = sem("w_split")
        h_ready, hid_done, hh_done, hl_done = map(sem, ("h_ready", "hid_done", "hh_done", "hl_done"))
        e_ready, e_added = sem("e_ready"), sem("e_added")
        block = ctx.enter_context(nc.Block())

        ORDER = [(0, 0), (0, 1), (1, 0), (0, 2), (1, 1), (0, 3), (1, 2), (1, 3)]
        MOMENTS = [o for o in ORDER if o[1] < TG - 1]
        QK_JOBS, V_JOBS = 4 * TG, 2 * TG
        QK_BANK = [4 + n % 2 for n in range(QK_JOBS)]
        V_BANK = [6 + m % 2 for m in range(V_JOBS)]

        def unit_slot(k):
            return (k // 2) % 2

        @block.sync
        def _(sp):
            sp.dma_start(w_in["wq"][:, :, :], t["wqT"].rearrange("(c p) n -> p c n", p=P)).then_inc(loaded["w_loaded"], 16)
            for g in range(TG):
                sp.dma_start(xT[:, :, g * 512:(g + 1) * 512],
                             t["xT"].rearrange("(c p) n -> p c n", p=P)[:, :, g * 512:(g + 1) * 512]).then_inc(xT_loaded[g], 16)
                if g == 0:
                    for n in ("wk", "wv"):
                        sp.dma_start(w_in[n][:, :, :], t[n + "T"].rearrange("(c p) n -> p c n", p=P)).then_inc(loaded["w_loaded"], 16)
                    sp.dma_start(ident[:, :], t["ident"]).then_inc(loaded["const_loaded"], 16)
            late = [(w_in[n][:, :, :], t[n].rearrange("(c p) n -> p c n", p=P)) for n in ("cwq", "cwk", "cwv", "cwo")]
            late += [(ctxT[:, :, :], t["ctxT"].rearrange("(c p) n -> p c n", p=P)),
                     (block8[:, :], t["block8"]), (iota8[:, :], t["iota8"]),
                     (cbq[:, :], t["cbq"].rearrange("(h p) -> p h", p=P)), (cbk[:, :], t["cbk"].rearrange("(h p) -> p h", p=P)),
                     (wg[:, :, :], t["wg"].rearrange("(c p) n -> p c n", p=P)),
                     (bg[:, :], t["bg"].rearrange("(o n) -> o n", o=1).to_broadcast([P, NE])),
                     (b1[:, :, :], t["b1"].rearrange("e (c p) -> p e c", p=P)), (b2d[:, :, :], t["b2d"])]
            late += [(rows[n][:, :], t[n].rearrange("(o n) -> o n", o=1).to_broadcast([P, D])) for n in ("cbv", "cbo", "gamma", "beta")]
            assert len(late) == LATE
            with nc.allow_non_contiguous_dma(reason="small bias vectors go over the partitions"):
                for dst, src in late:
                    sp.dma_start(dst, src).then_inc(loaded["x_loaded"], 16)
            sp.dma_start(maski[:, :, :], t["mask"].rearrange("(n p) s -> p n s", p=P)).then_inc(mask_loaded, 16)
            sp.dma_start(xres[:, :, :], t["x"].rearrange("(n p) d -> p n d", p=P)).then_inc(loaded["x_loaded"], 16)

            def store_parts(n):
                g, job = n // 4, n % 4
                w, half, b = "qk"[job // 2], job % 2, g // 2
                sp.wait_ge(parts_done, n + 1)
                for part in range(3):
                    layout = {"q": "d (h j s) -> h j d s", "k": "d (j h s) -> h j d s"}[w]
                    dst = scratch[w][b * 2 + half, part, :, :].rearrange(layout, h=2, s=512)[g % 2]
                    sp.dma_start(dst, parts[:, n % 3, part, :]).then_inc(parts_stored[n % 3], 16)

            def load_group(pair, slot):
                for row, part, n in Q_BLOCKS:
                    src = scratch["q"][bass.ds(pair, 1), part:part + n, :, :].rearrange("o r d (h g s) -> g (o r d) h s", h=2, g=2)[slot]
                    sp.dma_start(qstack[slot][row:row + n * HD, :, :, :].rearrange("p h j s -> p h (j s)"), src).then_inc(stack_loaded[slot], 16)
                for row, part, n in K_BLOCKS:
                    src = scratch["k"][bass.ds(pair, 1), part:part + n, :, :].rearrange("o r d (g s) -> g (o r d) s", g=2)[slot]
                    sp.dma_start(kstack[slot][row:row + n * HD, :, :].rearrange("p j s -> p (j s)"), src).then_inc(stack_loaded[slot], 16)
                sp.dma_start(vslot[slot][:, :, :, :].rearrange("p k j c -> p (k j c)"),
                             v_all[:, bass.ds(pair * 2 + slot, 1), :, :, :].rearrange("p o k j c -> p (o k j c)")).then_inc(vslot_loaded[slot], 16)

            def load_negmax(rows_done, k1):
                slot, half = unit_slot(k1), k1 % 2
                sp.wait_ge(neg_rows, rows_done)
                for part in range(2):
                    sp.dma_start(qstack[slot][MAXROW + part:MAXROW + part + 1, half, :, :],
                                 negrows[part * 16:part * 16 + 16, k1 % 2, :]).then_inc(neg_loaded, 16)

            for n in range(8):
                store_parts(n)
            for i in range(3):
                sp.wait_ge(parts_stored[i], 48 * len(range(i, 8, 3)))
            sp.wait_ge(v_done, 4)
            load_group(0, 0)
            load_group(0, 1)
            for n in range(8, QK_JOBS):
                store_parts(n)
            load_negmax(1, 0)
            for i in range(3):
                sp.wait_ge(parts_stored[i], 48 * len(range(i, QK_JOBS, 3)))
            sp.wait_ge(v_done, V_JOBS)
            sp.wait_ge(v2_done, 1)
            sp.wait_ge(v2_zeroed, 1)
            for h, s0, n, c, row in V_RUNS:
                sp.dma_start(vbd[row:row + n, :, :, c, h * HD:(h + 1) * HD].rearrange("p b h d -> p (b h) d"),
                             v2[s0:s0 + n, :, :].rearrange("p b (h d) -> p (b h) d", h=2)[:, :, h * HD:(h + 1) * HD]).then_inc(v2_placed, 16)

            def sp_unit(it, k, last):
                u = it * 4 + k
                if not (last and k == 3):
                    load_negmax(u + 2, k + 1)
                if k % 2 == 1 and not last:
                    sp.wait_ge(probs_used, u * STEPS + (STEPS + PR))
                    load_group(it + 1, unit_slot(k))

            def fetch_expert(e):
                sp.dma_start(w1raw[:, :, :], t["w1"][bass.ds(e, 1), :, :].rearrange("o (c p) f -> p (o c) f", p=P)).then_inc(w_fetched[0], 16)
                sp.dma_start(w2raw[:, :, :], t["w2"][bass.ds(e, 1), :, :].rearrange("o (c p) f -> p (o c) f", p=P)).then_inc(w_fetched[1], 16)

            fetch_expert(0)
            with sp.Fori(0, 3) as it:
                for k in range(4):
                    sp_unit(it, k, False)
            for k in range(4):
                sp_unit(3, k, True)
            for e in range(1, 3):
                sp.wait_ge(w_split, e * 5)
                fetch_expert(e)
            with sp.Fori(3, NE) as e:
                sp.wait_ge(w_split, e * 5)
                fetch_expert(e)
            out_v = t["out"].rearrange("(n p) d -> p n d", p=P)
            for n in range(NT):
                sp.wait_ge(out_done, n + 1)
                sp.dma_start(out_v[:, n, :], acc[:, n, :]).then_inc(out_stored, 16)
            sp.wait_ge(out_stored, 16 * NT)

        @block.tensor
        def _(pe):
            def project(g, between=lambda: None):
                pe.wait_ge(xT_loaded[g], 16)
                for job in range(4):
                    between()
                    n = 4 * g + job
                    if n == 0:
                        pe.wait_ge(loaded["w_loaded"], 48)
                    if n >= 2:
                        pe.wait_ge(rest_done, n - 1)
                    w = w_in[("wq", "wk")[job // 2]]
                    half = job % 2
                    for c in range(C2):
                        mm = pe.matmul(bank[QK_BANK[n]], w[:, c, half * P:half * P + P], xT[:, c, g * 512:g * 512 + 512],
                                       start=(c == 0), stop=(c == C2 - 1))
                    mm.then_inc(qk_ready, 1)
                for pair in range(2):
                    between()
                    m = 2 * g + pair
                    if m >= 2:
                        pe.wait_ge(v_done, m - 1)
                    if m == V_JOBS - 1:
                        pe.wait_ge(neg_rows, 1)
                    if m == V_JOBS - 2:
                        pe.wait_ge(k2_done, 1)
                        pe.wait_ge(v2_done, 1)
                    for i in range(2):
                        tok = g * 512 + (2 * pair + i) * P
                        for c in range(C2):
                            mm = pe.matmul(bank[V_BANK[m]][:, i * D:(i + 1) * D], xT[:, c, tok:tok + P], w_in["wv"][:, c, :],
                                           start=(c == 0), stop=(c == C2 - 1))
                    mm.then_inc(v_ready, 1)

            def max_pair(u, k, p, halves=(0, 1)):
                slot, half, j, qt = unit_slot(k), k % 2, p // 4, p % 4
                if 0 in halves:
                    pe.wait_ge(max_taken, u * 16 + p + 1)
                q = qstack[slot][0:MAXROW, half, j, qt * P:qt * P + P]
                for e in halves:
                    mm = pe.matmul(bank[2 * (p % 2) + e], q, kstack[slot][0:MAXROW, j, e * 512:e * 512 + 512],
                                   start=True, stop=True)
                if e == 1:
                    mm.then_inc(max_ready, 1)

            def turn_negmax(u, k, first=False):
                if first:
                    pe.wait_ge(v_done, V_JOBS - 2)
                else:
                    pe.wait_ge(o_normed, u)
                pe.wait_ge(neg_parts, u + 1)
                pe.transpose(bank[7].bitcast(BF16)[0:32, 0:P], negparts[:, k % 2, :], ident16[:, :]).then_inc(neg_turned, 1)

            def scores(u, k, i):
                slot, half, kt, j = unit_slot(k), k % 2, i // 4, i % 4
                pe.wait_ge(probs_ready, u * STEPS + i + 1)
                mm = pe.matmul(bank[4 + i % 2], kstack[slot][0:KROWS, j, kt * P:kt * P + P],
                               qstack[slot][0:KROWS, half, j, :], start=True, stop=True)
                mm.then_inc(scores_ready, 1)
                return mm

            def values(u, k, i):
                slot, kt, j = unit_slot(k), i // 4, i % 4
                pe.wait_ge(probs_ready, u * STEPS + i + 3)
                pe.matmul(bank[6][32 * j:32 * j + VW, :], vslot[slot][:, kt, j, :], probs[:, i % PR, :],
                          start=(kt == 0), stop=(kt == KT - 1), skip_group_check=True).then_inc(probs_used, 1)

            for g in range(TG - 1):
                project(g)
            pe.wait_ge(v_done, V_JOBS - 2)
            pe.wait_ge(loaded["x_loaded"], 16 * (LATE + 1))
            for half in range(2):
                for c in range(C2):
                    mm = pe.matmul(bank[6][:, half * B * SC:(half + 1) * B * SC], w_in["cwk"][:, c, half * P:half * P + P], ctxT[:, c, :],
                                   start=(c == 0), stop=(c == C2 - 1))
            mm.then_inc(cross_ready, 1)
            for b in range(B):
                for c in range(C2):
                    mm = pe.matmul(bank[7][0:SC, b * D:(b + 1) * D], ctxT[:, c, b * SC:(b + 1) * SC], w_in["cwv"][:, c, :],
                                   start=(c == 0), stop=(c == C2 - 1))
            mm.then_inc(cross_ready, 1)
            pe.wait_ge(k2_done, 1)
            pe.wait_ge(v2_done, 1)
            pe.wait_ge(ones_set, 3)
            pe.wait_ge(stack_loaded[0], 16 * LOADS)
            early = [(0, p) for p in range(16)] + [(1, p) for p in range(AHEAD)]
            slices = [early[i * 3:i * 3 + 3] for i in range(6)] + [early[18:]]

            def next_pairs():
                for u, p in slices.pop(0):
                    if (u, p) == (1, 0):
                        turn_negmax(0, 0, first=True)
                    max_pair(u, u, p)

            project(TG - 1, next_pairs)
            next_pairs()
            pe.wait_ge(v_done, V_JOBS)
            pe.wait_ge(parts_done, QK_JOBS)
            pe.wait_ge(neg_loaded, 32)
            scores(0, 0, 0)
            scores(0, 0, 1)

            pairs = [(1, p) for p in range(AHEAD, 16)] + [(2, p) for p in range(AHEAD - 1)]
            when = [pairs[2 * m:2 * m + 2] for m in range(KT)]
            TURN = 6

            def unit(it, k, last):
                u = it * 4 + k

                def ahead(i):
                    if i < STEPS:
                        scores(u, k, i)
                    elif not (last and k == 3):
                        if i == STEPS:
                            pe.wait_ge(neg_loaded, u * 32 + 64)
                        scores(u + 1, k + 1, i - STEPS)

                def pair(a, p, halves=(0, 1)):
                    if last and k + a > 3:
                        return
                    if (a, p) == (2, 0) and k % 2 == 0 and 0 in halves:
                        n_load = it + 1 + (1 if k + 2 > 3 else 0)
                        pe.wait_ge(stack_loaded[unit_slot(k + 2)], n_load * 16 * LOADS)
                    max_pair(u + a, k + a, p, halves)

                def heads(m):
                    if m == 0:
                        if k % 2 == 0:
                            pe.wait_ge(vslot_loaded[unit_slot(k)], 16 * (it + 1))
                        pe.wait_ge(o_copied, u + 1)
                    for j in range(GH):
                        values(u, k, GH * m + j)

                for m in range(KT):
                    ahead(4 * m + 2)
                    if m == TURN and not (last and k == 3):
                        turn_negmax(u + 1, k + 1)
                    if m:
                        heads(m - 1)
                    ahead(4 * m + 3)
                    pair(*when[m][0])
                    ahead(4 * m + 4)
                    if len(when[m]) > 1:
                        pair(*when[m][1], halves=(0,))
                    ahead(4 * m + 5)
                    if len(when[m]) > 1:
                        pair(*when[m][1], halves=(1,))
                heads(KT - 1)
                if not (last and k + 2 > 3):
                    max_pair(u + 2, k + 2, AHEAD - 1)
                pe.wait_ge(o_copied, u + 2)
                if not (last and k == 3):
                    pe.wait_ge(neg_rows, u + 2)
                else:
                    pe.wait_ge(o_normed, u + 1)
                for qt in range(4):
                    tr = pe.transpose(bank[7][:, qt * P:qt * P + P], outT[:, qt * P:qt * P + P], ident[:, :])
                tr.then_inc(o_turned, 1)

            with pe.Fori(0, 3) as it:
                for k in range(4):
                    unit(it, k, False)
            for k in range(4):
                unit(3, k, True)


            def turn_x1(g):
                pe.wait_ge(x1_done, g * 4 + 4)
                if g == 0:
                    pe.wait_ge(o_normed, UNITS + 1)
                elif g > 1:
                    pe.wait_ge(y2_done, g * 4 - 4)
                for c in range(C2):
                    for i in range(4):
                        tr = pe.transpose(bank[6 + c][:, i * P:i * P + P], x1[:, i, c * P:c * P + P], ident[:, :])
                    tr.then_inc(x1_turned, 1)

            def project_q2(g, half):
                if half == 0:
                    pe.wait_ge(x1T_done, g * 2 + 2)
                for c in range(C2):
                    mm = pe.matmul(bank[6 + half], w_in["cwq"][:, c, half * P:half * P + P], x1T[:, c, :], start=(c == 0), stop=(c == C2 - 1))
                mm.then_inc(q2_ready, 1)

            def scores2(n, half):
                g, i = n // 4, n % 4
                if half == 0:
                    if i == 0:
                        pe.wait_ge(q2_done, g * 2 + 2)
                    if n:
                        pe.wait_ge(s2_taken, n)
                for e in (2 * half, 2 * half + 1):
                    mm = pe.matmul(bank[e][:, 0:4 * SC], q2T[:, half, i * P:i * P + P],
                                   kbd[:, g // 2, half, 4 * (e % 2):4 * (e % 2) + 4, :].rearrange("p h s -> p (h s)"),
                                   start=True, stop=True)
                if half == 1:
                    mm.then_inc(s2_ready, 1)

            def turn_probs(n, between):
                pe.wait_ge(p2_done, n + 1)
                for j, chunks in enumerate(TURNS):
                    m = 3 * n + j
                    if m >= 2:
                        pe.wait_ge(pT_done, m - 1)
                    for k, (half, c) in enumerate(chunks):
                        flat = sc2[:, n % SR, half * HALF:(half + 1) * HALF, :].rearrange("p h s -> p (h s)")
                        tr = pe.transpose(bank[4 + m % 2][0:VROWS[c], k * P:k * P + P], flat[:, c * P:c * P + VROWS[c]], ident[:, :])
                    tr.then_inc(p2_turned, 1)
                    if j:
                        between(j - 1)

            def values2(g):
                pe.wait_ge(pT_done, 12 * g + 12)
                pe.wait_ge(q2_done, min(2 * g + 4, 2 * TG))
                if g:
                    pe.wait_ge(y2_done, 4 * g)
                for half in range(2):
                    for c in range(VC):
                        mm = pe.matmul(bank[6 + half], vbd[0:VROWS[c], g // 2, half, c, :], pT[0:VROWS[c], half, c, :],
                                       start=(c == 0), stop=(c == VC - 1))
                    mm.then_inc(o2_ready, 1)

            def project_o2(g):
                pe.wait_ge(o2T_done, g * 2 + 2)
                for i in range(4):
                    for c in range(C2):
                        mm = pe.matmul(bank[6 + i // 2][:, (i % 2) * D:(i % 2 + 1) * D], o2T[:, c, i * P:i * P + P], w_in["cwo"][:, c, :],
                                       start=(c == 0), stop=(c == C2 - 1))
                    mm.then_inc(y2_ready, 1)

            turn_x1(0)
            for half in range(2):
                project_q2(0, half)
            pe.wait_ge(mask_step, MASK_STEPS)
            pe.wait_ge(v2_placed, 16 * len(V_RUNS))
            for n in range(FAR):
                for half in range(2):
                    scores2(n, half)
            for n in range(NT):
                g, i = n // 4, n % 4

                def next_scores(half):
                    if n + FAR < NT:
                        scores2(n + FAR, half)

                if i == 1 and g < TG - 1:
                    turn_probs(n, lambda half: project_q2(g + 1, half))
                    for half in range(2):
                        next_scores(half)
                else:
                    turn_probs(n, next_scores)
                if i == 0 and g < TG - 1:
                    turn_x1(g + 1)
                if i == 3:
                    values2(g)
                    project_o2(g)

            pe.wait_ge(s2_taken, NT)
            pe.wait_ge(y2_done, NT)
            for m in range(C2 * TG):
                g, c = m // C2, m % C2
                pe.wait_ge(x2_done, g * 4 + 4)
                for i in range(4):
                    tr = pe.transpose(bank[m][:, i * P:i * P + P], xres[:, 4 * g + i, c * P:c * P + P], ident[:, :])
                tr.then_inc(x2_turned, 1)
            pe.wait_ge(x2T_done, 2 * TG)
            pe.wait_ge(x2l_done, 2 * TG)
            for n in range(NT):
                for c in range(C2):
                    mm = pe.matmul(bank[4][:, n * NE:(n + 1) * NE], x2T[:, c, n * P:n * P + P], wg[:, c, :], start=(c == 0), stop=(c == C2 - 1))
            mm.then_inc(logits_ready, 1)

            def hidden(e, eo, g):
                n = (e * 2 + eo) * TG + g
                if g == 0:
                    pe.wait_ge(w_split, (e * 2 + eo) * 5 + 5)
                (wh, wl), tok = w1[eo], slice(g * 512, g * 512 + 512)
                for fc in range(FC):
                    pe.wait_ge(hid_done, n * FC + fc + 1)
                    terms = [(w, x, c) for c in range(C2) for w, x in ((wh, x2h), (wh, x2l), (wl, x2h))]
                    for k, (w, x, c) in enumerate(terms):
                        mm = pe.matmul(bank[fc], w[:, c, fc * P:fc * P + P], x[:, c, tok], start=(k == 0), stop=(k == len(terms) - 1))
                    mm.then_inc(h_ready, 1)

            def output(e, eo, g):
                n = (e * 2 + eo) * TG + g
                wh, wl = w2[eo]
                pe.wait_ge(hl_done, n * FC + 2 * FC)
                for i in range(4):
                    pe.wait_ge(e_added, n * 4 + i + 1)
                    terms = [(a, w, fc) for fc in range(FC) for a, w in ((hh, wh), (hl, wh), (hh, wl))]
                    for k, (a, w, fc) in enumerate(terms):
                        mm = pe.matmul(bank[4 + i][:, 0:D], a[:, g % 2, fc, i * P:i * P + P], w[:, fc, :], start=(k == 0), stop=(k == len(terms) - 1))
                    mm.then_inc(e_ready, 1)

            def expert_pair(e, last):
                for k in range(2 * TG):
                    if k < 2 * TG - 1:
                        hidden(e, (k + 1) // TG, (k + 1) % TG)
                    elif not last:
                        hidden(e + 1, 0, 0)
                    output(e, k // TG, k % TG)

            hidden(0, 0, 0)
            pe.wait_ge(gates_done, 1)
            pe.transpose(bank[5][:, 0:P], gates[:, :, :].rearrange("p n e -> p (n e)"), ident[:, :]).then_inc(gates_turned, 1)
            pe.wait_ge(gT_done, 1)
            for n in range(NT):
                q, row = n // 2, n // 4 * 32
                if n % 2 == 0 and q >= 4:
                    pe.wait_ge(acc_set, q - 3)
                mm = pe.matmul(bank[4 + q % 4][:, (n % 2) * D:(n % 2 + 1) * D], gT[row:row + 32, :], b2d[row:row + 32, n % 4, :], start=True, stop=True)
                if n % 2:
                    mm.then_inc(bias_ready, 1)
            pe.wait_ge(acc_set, NT // 2)
            with pe.Fori(0, NE // 2 - 1) as e:
                expert_pair(e, False)
            expert_pair(NE // 2 - 1, True)

        @block.vector
        def _(dve):
            def split(n):
                hi, mid, low = (parts[:, n % 3, i, :] for i in range(3))
                dve.wait_ge(hi_done, n + 1)
                dve.tensor_tensor(rest[:, n % 2, :], bank[QK_BANK[n]], hi, ALU.subtract).then_inc(rest_done, 1)
                dve.wait_ge(rest_done, n + 1)
                dve.tensor_copy(mid, rest[:, n % 2, :]).then_inc(mid_done, 1)
                dve.wait_ge(mid_done, n + 1)
                dve.tensor_tensor(low, rest[:, n % 2, :], mid, ALU.subtract).then_inc(parts_done, 1)

            for n in range(QK_JOBS - 4):
                split(n)
            dve.wait_ge(cross_ready, 2)
            dve.tensor_tensor(v2[:, :, :], bank[7][0:SC, :].rearrange("p (b d) -> p b d", b=B),
                              rows["cbv"][0:SC, :].rearrange("p (o d) -> p o d", o=1).to_broadcast([SC, B, D]), ALU.add).then_inc(v2_done, 1)

            def reduce_max(u, k, p):
                dve.wait_ge(max_ready, u * 16 + p + 1)
                dve.tensor_reduce(rowmax[:, k % 2, p:p + 1], quad[:, 2 * (p % 2):2 * (p % 2) + 2, :].rearrange("p a n -> p (a n)"),
                                  AX_X, ALU.max).then_inc(max_taken, 1)

            def negate(u, k):
                m, hi, low = rowmax[:, k % 2, :], negparts[:, k % 2, 0:16], negparts[:, k % 2, 16:32]
                dve.wait_ge(max_taken, u * 16 + 18)
                dve.tensor_scalar(hi, m, -1.0, None, ALU.mult).then_inc(neg_hi, 1)
                dve.wait_ge(neg_hi, u + 1)
                dve.scalar_tensor_tensor(low, m, -1.0, hi, ALU.mult, ALU.subtract).then_inc(neg_parts, 1)
                dve.wait_ge(neg_turned, u + 1)
                dve.tensor_copy(negrows[:, k % 2, :], bank[7].bitcast(BF16)[0:32, 0:P]).then_inc(neg_rows, 1)

            early = [(0, p) for p in range(16)] + [(1, p) for p in range(AHEAD)]
            for i in range(7):
                for u, p in (early[i * 3:i * 3 + 3] if i < 6 else early[18:]):
                    if (u, p) == (1, 0):
                        negate(0, 0)
                    reduce_max(u, u, p)
                if i < 4:
                    split(QK_JOBS - 4 + i)

            links = [0]

            def mark(ins):
                ins.then_inc(chain, 1)
                links[0] += 1
                return links[0]

            def link(ins):
                dve.wait_ge(chain, mark(ins))

            roots = [0]
            MEAN, VAR, RSTD, T0, T1, ROOT = range(6)

            def moments(lo, hi):
                row = [lnv[:, i, lo:hi] for i in range(8)]
                me, ve, mo, vo = (stats[:, lo:hi, i] for i in (1, 2, 4, 5))
                dve.tensor_tensor(row[T1], ve, vo, ALU.add).then_inc(chain, 1)
                dve.tensor_tensor(row[MEAN], me, mo, ALU.add).then_inc(chain, 1)
                links[0] += 2
                link(dve.tensor_tensor(row[T0], me, mo, ALU.subtract))
                dve.tensor_scalar(row[MEAN], row[MEAN], 0.5, None, ALU.mult).then_inc(chain, 1)
                dve.tensor_tensor(row[T0], row[T0], row[T0], ALU.mult).then_inc(chain, 1)
                links[0] += 2
                link(dve.tensor_scalar(row[T1], row[T1], 1.0 / D, EPS, ALU.mult, ALU.add))
                dve.scalar_tensor_tensor(row[VAR], row[T0], 0.25, row[T1], ALU.mult, ALU.add).then_inc(root_wanted, 1)
                roots[0] += 1
                dve.wait_ge(root_done, roots[0])
                link(dve.tensor_tensor(row[T0], row[ROOT], row[ROOT], ALU.mult))
                link(dve.scalar_tensor_tensor(row[T0], row[T0], -0.5, row[VAR], ALU.mult, ALU.mult))
                link(dve.scalar_tensor_tensor(row[RSTD], row[T0], 1.5, row[ROOT], ALU.add, ALU.mult))

            def add_attention(tiles):
                marks = {}
                for n in list(tiles) + [None]:
                    if n is not None:
                        b, h, q = n // 8, n // 4 % 2, n % 4
                        xv = xres[:, n, :].rearrange("p (g f c) -> p g f c", g=2, f=2)
                        marks[n] = mark(dve.tensor_tensor(xv, xv, attn_v[:, b, h, q], ALU.add))
                    for m in [m for m in marks if n is None or m < n]:
                        dve.wait_ge(chain, marks.pop(m))
                        bn = dve.bn_stats(stats[:, m, :], xres[:, m, :])
                return bn

            attn_v = attn[:, :, :, :, :].rearrange("p (b g) (f h) q c -> p b h q g f c", b=B, h=2)

            def norm_tile(out, n, src=xres):
                return dve.tensor_scalar(out, src[:, bass.ds(n, 1), :].rearrange("p o d -> p (o d)"),
                                         lnv[:, MEAN, bass.ds(n, 1)], lnv[:, RSTD, bass.ds(n, 1)], ALU.subtract, ALU.mult)

            def norm_x1(g):
                if g:
                    dve.wait_ge(x1_turned, g * 2)
                    dve.wait_ge(x1b_done, 4 * g)
                for i in range(4):
                    n = g * 4 + i
                    dve.tensor_scalar(x1[:, i, :], xres[:, n, :], lnv[:, MEAN, n:n + 1], lnv[:, RSTD, n:n + 1],
                                      ALU.subtract, ALU.mult).then_inc(x1_done, 1)

            def unit(it, k, last):
                u = it * 4 + k
                if not (last and k == 3):
                    for p in range(AHEAD, 16):
                        reduce_max(u + 1, k + 1, p)
                    negate(u + 1, k + 1)
                if not (last and k + 2 > 3):
                    for p in range(AHEAD):
                        reduce_max(u + 2, k + 2, p)
                if last and k == 3:
                    dve.wait_ge(loaded["x_loaded"], 16 * (LATE + 1))
                    dve.wait_ge(v_done, V_JOBS)
                    dve.wait_ge(o_normed, 2 * KT // 2 + 1)
                    link(add_attention(range(KT)))
                    moments(0, KT)
                    norm_x1(0)
                sums = bank[7].rearrange("p (q j c) -> p q j c", q=4, c=VW)
                dve.wait_ge(o_turned, u + 2)
                dve.reciprocal(rden[:, :].rearrange("p (q j) -> p q j", q=4), sums[:, :, :, HD]).then_inc(o_recip, 1)
                dve.wait_ge(o_recip, u + 1)
                inv = rden[:, :].rearrange("p (q j o) -> p q j o", q=4, o=1).to_broadcast([P, 4, GH, HD])
                dst = attn[:, bass.ds(it, 1), k, :, :].rearrange("p o q (j d) -> p (o q) j d", d=HD)
                dve.tensor_tensor(dst, sums[:, :, :, 0:HD], inv, ALU.mult).then_inc(o_normed, 1)

            with dve.Fori(0, 3) as it:
                for k in range(4):
                    unit(it, k, False)
            for k in range(4):
                unit(3, k, True)


            def take(n):
                dve.wait_ge(s2_ready, n + 1)
                if n >= SR:
                    dve.wait_ge(p2_turned, 3 * (n - SR) + 3)
                dve.tensor_tensor(sc2[:, n % SR, :, :].rearrange("p (e h) s -> p e h s", e=4),
                                  quad[:, :, 0:4 * SC].rearrange("p e (h s) -> p e h s", s=SC),
                                  cap[:, n:n + 1, :].rearrange("p o (u s) -> p o u s", u=1).to_broadcast([P, 4, 4, SC]),
                                  ALU.min).then_inc(s2_taken, 1)
                dve.wait_ge(s2_taken, n + 1)
                dve.tensor_reduce(max2[:, n % SR, :], sc2[:, n % SR, :, :], AX_X, ALU.max).then_inc(s2_max, 1)

            def sums(n):
                dve.wait_ge(p2_exp, n + 1)
                dve.tensor_reduce(sum2[:, n % SR, :], sc2[:, n % SR, :, :], AX_X, ALU.add).then_inc(s2_summed, 1)
                dve.wait_ge(s2_summed, n + 1)
                dve.reciprocal(inv2[:, n % SR, :], sum2[:, n % SR, :]).then_inc(s2_recip, 1)

            def residual2(g):
                dve.wait_ge(x1b_done, 4 * g + 4)
                for i in range(5):
                    n = 4 * g + i
                    if i < 4:
                        dve.wait_ge(y2_ready, (n | 1) + 1)
                        dve.tensor_tensor(xres[:, n, :], bank[6 + i // 2][:, (i % 2) * D:(i % 2 + 1) * D], xres[:, n, :], ALU.add).then_inc(y2_done, 1)
                    if i:
                        dve.wait_ge(y2_done, n)
                        bn = dve.bn_stats(stats[:, n - 1, :], xres[:, n - 1, :])
                return bn

            dve.wait_ge(mask_step, MASK_STEPS)
            for n in range(FAR):
                take(n)
            norm_x1(1)
            sums(0)
            for n in range(NT):
                g, i = n // 4, n % 4
                if i == 0 and g:
                    residual2(g - 1)
                if n + 1 < NT:
                    sums(n + 1)
                if n + FAR < NT:
                    take(n + FAR)
                if n < 4:
                    bn = add_attention(range(KT + 2 * n, KT + 2 * n + 2))
                    if n == 3:
                        link(bn)
                        moments(KT, NT)
                if i == 3 and g < TG - 2:
                    norm_x1(g + 2)
            link(residual2(TG - 1))
            moments(0, NT)

            def low_x2(g):
                for c in range(C2):
                    dve.wait_ge(x2h_done, g * 2 + c + 1)
                    dve.tensor_tensor(x2l[:, c, g * 512:g * 512 + 512], bank[2 * g + c], x2h[:, c, g * 512:g * 512 + 512],
                                      ALU.subtract).then_inc(x2l_done, 1)

            for g in range(TG):
                for n in range(4 * g, 4 * g + 4):
                    dve.tensor_scalar(xres[:, n, :], xres[:, n, :], lnv[:, MEAN, n:n + 1], lnv[:, RSTD, n:n + 1],
                                      ALU.subtract, ALU.mult).then_inc(x2_done, 1)
                if g:
                    low_x2(g - 1)
            low_x2(TG - 1)
            dve.wait_ge(logits_ready, 1)
            link(dve.tensor_tensor(logits[:, :, :], bank[4][:, 0:NT * NE].rearrange("p (n e) -> p n e", e=NE),
                                   bg[:, :].rearrange("p (o e) -> p o e", o=1).to_broadcast([P, NT, NE]), ALU.add))
            for n in range(NT):
                mx = dve.max(top[:, n, :], logits[:, n, :])
            link(mx)
            dve.tensor_tensor(gw[:, :, 0], top[:, :, 1], top[:, :, 0], ALU.subtract).then_inc(gap_done, 1)
            for n in range(NT):
                mx = dve.max_index(topi[:, n, :], top[:, n, :], logits[:, n, :])
            link(mx)
            link(dve.tensor_copy(topf[:, :, :], topi[:, :, :]))
            for j in range(2):
                eq = dve.tensor_tensor(pick[:, j, :, :], iota8[:, :].rearrange("p (o e) -> p o e", o=1).to_broadcast([P, NT, NE]),
                                       topf[:, :, j:j + 1].to_broadcast([P, NT, NE]), ALU.is_equal)
            dve.wait_ge(gap_exp, 1)
            link(dve.tensor_scalar(gw[:, :, 3], gw[:, :, 1], 1.0, None, ALU.add))
            link(dve.reciprocal(gw[:, :, 2], gw[:, :, 3]))
            link(dve.tensor_tensor(gw[:, :, 3], gw[:, :, 1], gw[:, :, 2], ALU.mult))
            for j in range(2):
                pk = dve.tensor_tensor(pick[:, j, :, :], pick[:, j, :, :], gw[:, :, 2 + j:3 + j].to_broadcast([P, NT, NE]), ALU.mult)
            link(pk)
            dve.tensor_tensor(gates[:, :, :], pick[:, 0, :, :], pick[:, 1, :, :], ALU.add).then_inc(gates_done, 1)
            dve.wait_ge(gates_turned, 1)
            dve.tensor_copy(gT[:, :], bank[5][:, 0:P]).then_inc(gT_done, 1)

            def split_hidden(e, eo, g):
                n = (e * 2 + eo) * TG + g
                for fc in range(FC):
                    m = n * FC + fc
                    dve.wait_ge(hid_done, m + FC + 1)
                    if fc == 0:
                        dve.wait_ge(e_ready, n * 4 + (EC - 4))
                    dve.tensor_copy(hh[:, g % 2, fc, :], hid[:, fc, :]).then_inc(hh_done, 1)
                    dve.wait_ge(hh_done, m + 1)
                    dve.tensor_tensor(hl[:, g % 2, fc, :], hid[:, fc, :], hh[:, g % 2, fc, :], ALU.subtract).then_inc(hl_done, 1)

            def add_expert(e, eo, g):
                n = (e * 2 + eo) * TG + g
                for i in range(4):
                    dve.wait_ge(e_ready, n * 4 + (i + 1 + EC))
                    if i == 0:
                        dve.wait_ge(e_added, n * 4 + 4)
                    dve.scalar_tensor_tensor(acc[:, g * 4 + i, :], bank[4 + i][:, 0:D],
                                             gates[:, g * 4 + i, bass.ds(e * 2 + eo, 1)], acc[:, g * 4 + i, :],
                                             ALU.mult, ALU.add).then_inc(e_added, 1)

            def expert_pair(e, last):
                for k in range(2 * TG):
                    if k < 2 * TG - 1:
                        split_hidden(e, (k + 1) // TG, (k + 1) % TG)
                    elif not last:
                        split_hidden(e + 1, 0, 0)
                    add_expert(e, k // TG, k % TG)
                    if last and k >= TG:
                        finish(k - TG)

            def group_stats(g):
                for n in range(4 * g, 4 * g + 4):
                    bn = dve.bn_stats(stats[:, n, :], acc[:, n, :])
                    bn.then_inc(stat_done, 1)
                return bn

            def await_moments(k, g):
                if g < TG - 1:
                    dve.wait_ge(mom_done, MOMENTS.index((k, g)) + 1)
                else:
                    dve.wait_ge(stat_done, 4 * ORDER.index((k, g)) + 4)
                    moments(4 * g, 4 * g + 4)

            def first_norm(g):
                await_moments(0, g)
                if g == 0:
                    dve.wait_ge(xb_done, 1)
                tiles = range(4 * g, 4 * g + 4)
                for n in tiles:
                    ins = dve.scalar_tensor_tensor(acc[:, n, :], acc[:, n, :], lnv[:, MEAN, n:n + 1], rows["gamma"][:, :], ALU.subtract, ALU.mult)
                link(ins)
                for n in tiles:
                    ins = dve.scalar_tensor_tensor(acc[:, n, :], acc[:, n, :], lnv[:, RSTD, n:n + 1], xres[:, n, :], ALU.mult, ALU.add)
                link(ins)
                group_stats(g)

            def last_norm(g):
                await_moments(1, g)
                for n in range(4 * g, 4 * g + 4):
                    dve.tensor_scalar(acc[:, n, :], acc[:, n, :], lnv[:, MEAN, n:n + 1], lnv[:, RSTD, n:n + 1],
                                      ALU.subtract, ALU.mult).then_inc(out_done, 1)

            def finish(g):
                dve.wait_ge(e_added, 4 * (NE - 1) * TG + 4 * g + 8)
                group_stats(g)
                if g:
                    first_norm(g - 1)
                if g > 1:
                    last_norm(g - 2)

            for q in range(NT // 2):
                dve.wait_ge(bias_ready, q + 1)
                dve.tensor_tensor(acc[:, 2 * q:2 * q + 2, :], bank[4 + q % 4].rearrange("p (n d) -> p n d", d=D),
                                  xres[:, 2 * q:2 * q + 2, :], ALU.add).then_inc(acc_set, 1)
            split_hidden(0, 0, 0)
            dve.wait_ge(acc_set, NT // 2)
            with dve.Fori(0, NE // 2 - 1) as e:
                expert_pair(e, False)
            expert_pair(NE // 2 - 1, True)

            first_norm(TG - 1)
            for g in range(TG - 2, TG):
                last_norm(g)

        @block.scalar
        def _(act):
            def high(n):
                act.wait_ge(qk_ready, n + 1)
                if n >= 3:
                    act.wait_ge(parts_stored[n % 3], 48 * (n // 3))
                act.activation(parts[:, n % 3, 0, :], bank[QK_BANK[n]], ACT.Copy).then_inc(hi_done, 1)

            def keep_values(m):
                act.wait_ge(v_ready, m + 1)
                g, pair = m // 2, m % 2
                for i in range(2):
                    tile = 4 * g + 2 * pair + i
                    b, kt = tile // KT, tile % KT
                    cp = act.activation(v_all[:, b * NG:(b + 1) * NG, kt, :, 0:HD],
                                        bank[V_BANK[m]][:, i * D:(i + 1) * D].rearrange("p (g j d) -> p g j d", g=NG, d=HD), ACT.Copy)
                cp.then_inc(v_done, 1)

            act.wait_ge(v_zeroed, 2)
            for g in range(TG):
                if g == TG - 1:
                    act.wait_ge(cross_ready, 1)
                    for half in range(2):
                        cp = act.activation(k2T[:, half, :], bank[6][:, half * B * SC:(half + 1) * B * SC], ACT.Identity, bias=cbk[:, half:half + 1])
                    cp.then_inc(k2_done, 1)
                for job in range(4):
                    high(4 * g + job)
                keep_values(2 * g)
                keep_values(2 * g + 1)

            def exps(u, k, i):
                n = u * STEPS + i
                act.wait_ge(scores_ready, n + 1)
                act.wait_ge(probs_used, n + 1)
                act.activation(probs[:, i % PR, :], bank[4 + i % 2], ACT.Exp, scale=INV4).then_inc(probs_ready, 1)

            def unit(it, k):
                u = it * 4 + k
                for i in range(STEPS):
                    exps(u, k, i)
                act.wait_ge(probs_used, u * STEPS + STEPS + PR)
                act.wait_ge(o_turned, u + 1)
                act.activation(outT[:, :], bank[6], ACT.Copy).then_inc(o_copied, 1)

            with act.Fori(0, 4) as it:
                for k in range(4):
                    unit(it, k)


            def exp2(n):
                act.wait_ge(s2_shifted, n + 1)
                act.activation(sc2[:, n % SR, :, :], sc2[:, n % SR, :, :], ACT.Exp, scale=INV4).then_inc(p2_exp, 1)

            def keep_turned(n):
                g, i = n // 4, n % 4
                if i == 0 and g:
                    act.wait_ge(o2_ready, 2 * g)
                for j, chunks in enumerate(TURNS):
                    m = 3 * n + j
                    act.wait_ge(p2_turned, m + 1)
                    (half, c), k = chunks[0], len(chunks)
                    rows_ = VROWS[c]
                    dst = pT[0:rows_, half, c:c + k, i * P:i * P + P] if j < 2 else pT[0:rows_, :, c, i * P:i * P + P]
                    act.activation(dst, bank[4 + m % 2][0:rows_, 0:k * P].rearrange("p (k q) -> p k q", q=P), ACT.Copy).then_inc(pT_done, 1)

            def keep_x1T(g):
                for c in range(C2):
                    act.wait_ge(x1_turned, g * 2 + c + 1)
                    if g:
                        act.wait_ge(q2_ready, g * 2)
                    act.activation(x1T[:, c, :], bank[6 + c], ACT.Copy).then_inc(x1T_done, 1)

            def keep_q2(g):
                for half in range(2):
                    act.wait_ge(q2_ready, g * 2 + half + 1)
                    if g:
                        act.wait_ge(s2_ready, g * 4)
                    act.activation(q2T[:, half, :], bank[6 + half], ACT.Identity, bias=cbq[:, half:half + 1]).then_inc(q2_done, 1)

            def keep_o2(g):
                for half in range(2):
                    act.wait_ge(o2_ready, g * 2 + half + 1)
                    if g:
                        act.wait_ge(y2_ready, g * 4)
                    act.activation(o2T[:, half, :], bank[6 + half], ACT.Copy).then_inc(o2T_done, 1)

            keep_x1T(0)
            keep_q2(0)
            for n in range(FAR - 1):
                exp2(n)
            for n in range(NT):
                g, i = n // 4, n % 4
                keep_turned(n)
                if i == 0 and g < TG - 1:
                    keep_x1T(g + 1)
                if i == 1 and g < TG - 1:
                    keep_q2(g + 1)
                if i == 3:
                    keep_o2(g)
                if n + FAR - 1 < NT:
                    exp2(n + FAR - 1)

            for m in range(C2 * TG):
                g, c = m // C2, m % C2
                act.wait_ge(x2_turned, m + 1)
                act.activation(x2T[:, c, g * 512:g * 512 + 512], bank[m], ACT.Copy).then_inc(x2T_done, 1)
                act.activation(x2h[:, c, g * 512:g * 512 + 512], bank[m], ACT.Copy).then_inc(x2h_done, 1)
            act.wait_ge(gap_done, 1)
            act.activation(gw[:, :, 1], gw[:, :, 0], ACT.Exp).then_inc(gap_exp, 1)

            def relu(e, eo, g):
                n = (e * 2 + eo) * TG + g
                for fc in range(FC):
                    m = n * FC + fc
                    act.wait_ge(h_ready, m + 1)
                    act.wait_ge(hl_done, m + 1)
                    if g == 0 and fc == 0:
                        act.wait_ge(w_split, (e * 2 + eo) * 5 + 5)
                    act.activation(hid[:, fc, :], bank[fc], ACT.Relu, bias=b1e[:, eo, fc:fc + 1]).then_inc(hid_done, 1)

            with act.Fori(0, NE // 2) as e:
                for eo in range(2):
                    for g in range(TG):
                        relu(e, eo, g)

        @block.gpsimd
        def _(pool):
            pool.memset(v_all[:, :, :, :, HD:HD + 1], 1.0).then_inc(v_zeroed, 1)
            pool.wait_ge(v_zeroed, 1)
            pool.memset(v_all[:, :, :, :, HD + 1:VW], 0.0).then_inc(v_zeroed, 1)
            pool.wait_ge(v_zeroed, 2)
            for i in range(2):
                pool.memset(kstack[i][MAXROW:P, :, :], 1.0).then_inc(ones_set, 1)
                pool.wait_ge(ones_set, i + 1)
            pool.memset(credit[:, 0:1], 0.0).then_inc(max_taken, 2)
            pool.wait_ge(max_taken, 2)
            pool.memset(credit[:, 1:2], 0.0).then_inc(probs_ready, 2)
            pool.wait_ge(probs_ready, 2)
            pool.memset(credit[:, 2:3], 0.0).then_inc(probs_used, PR)
            pool.wait_ge(probs_used, PR)
            pool.wait_ge(loaded["const_loaded"], 16)
            pool.tensor_copy(ident16[:, :], ident[:, :]).then_inc(ones_set, 1)
            for i, (s_, k_) in enumerate(((o_copied, 1), (o_turned, 1), (o_normed, 1), 
                           (hid_done, FC),
                           (e_added, 4), (e_ready, EC), (hl_done, FC))):
                pool.wait_ge(ones_set, 3 + i)
                pool.memset(credit[:, 3:4], 0.0).then_inc(s_, k_)
                pool.wait_ge(s_, k_)
                pool.memset(credit[:, 4:5], 0.0).then_inc(ones_set, 1)
            count = [0]

            def step(ins):
                ins.then_inc(mask_step, 1)
                count[0] += 1
                pool.wait_ge(mask_step, count[0])

            pool.wait_ge(mask_loaded, 16)
            step(pool.memset(one[:, :], 1.0))
            step(pool.memset(power[:, :], -0.5))
            step(pool.memset(vbd[:, :, :, :, :], 0.0))
            pool.memset(credit[:, 5:6], 0.0).then_inc(v2_zeroed, 1)
            step(pool.tensor_scalar(cap[:, :, :], maski[:, :, :], 0.0, -NO_CAP, ALU.is_equal, ALU.mult))
            step(pool.tensor_scalar(cap[:, :, :], cap[:, :, :], NO_CAP, MASKED, ALU.add, ALU.add))
            pool.wait_ge(k2_done, 1)
            for b in range(B):
                for half in range(2):
                    step(pool.tensor_tensor(kbd[:, b, half, :, :],
                                            k2T[:, half, b * SC:(b + 1) * SC].rearrange("p (o s) -> p o s", o=1).to_broadcast([P, 8, SC]),
                                            block8[:, :].rearrange("p (h o) -> p h o", o=1).to_broadcast([P, 8, SC]), ALU.mult))
            assert count[0] == MASK_STEPS

            def split_weights(e, eo):
                m = e * 2 + eo
                pool.wait_ge(e_ready, m * 16 + (EC - 16))
                for k, (raw, w) in enumerate(((w1raw, w1), (w2raw, w2))):
                    pool.wait_ge(w_fetched[k], m * 16 + 16)
                    pool.tensor_tensor(w[eo][0][:, :, :], raw[:, :, :], one[:, :].rearrange("p (a b) -> p a b", a=1).to_broadcast(list(raw.shape)), ALU.mult).then_inc(w_split, 1)
                    if k == 0:
                        pool.tensor_copy(b1e[:, eo, :].rearrange("p (o c) -> p o c", o=1), b1[:, bass.ds(m, 1), :]).then_inc(w_split, 1)
                    pool.wait_ge(w_split, m * 5 + (2, 4)[k])
                    pool.tensor_tensor(w[eo][1][:, :, :], raw[:, :, :], w[eo][0][:, :, :], ALU.subtract).then_inc(w_split, 1)
            pool.wait_ge(loaded["x_loaded"], 16 * (LATE + 1))
            split_weights(0, 0)

            def root(k, lo, hi):
                pool.wait_ge(root_wanted, k)
                pool.tensor_tensor(lnv[:, 5, lo:hi], lnv[:, 1, lo:hi], power[:, lo:hi], ALU.pow).then_inc(root_done, 1)

            def add_bias2(n):
                pool.wait_ge(x1_done, n // 4 * 4 + 4)
                pool.tensor_tensor(xres[:, n, :], x1[:, n % 4, :], rows["cbo"][:, :], ALU.add).then_inc(x1b_done, 1)

            def over_heads(v):
                return v.rearrange("p (h o) -> p h o", o=1).to_broadcast([P, H, SC])

            def shift(n):
                pool.wait_ge(s2_max, n + 1)
                sc = sc2[:, n % SR, :, :]
                pool.tensor_tensor(sc, sc, over_heads(max2[:, n % SR, :]), ALU.subtract).then_inc(s2_shifted, 1)

            def divide(n):
                pool.wait_ge(s2_recip, n + 1)
                sc = sc2[:, n % SR, :, :]
                pool.tensor_tensor(sc, sc, over_heads(inv2[:, n % SR, :]), ALU.mult).then_inc(p2_done, 1)

            root(1, 0, KT)
            for n in range(4):
                add_bias2(n)
            for n in range(FAR):
                shift(n)
            divide(0)
            for n in range(NT):
                if n + 1 < NT:
                    divide(n + 1)
                if n + FAR < NT:
                    shift(n + FAR)
                if n == 3:
                    root(2, KT, NT)
                if n + 4 < NT:
                    add_bias2(n + 4)
            root(3, 0, NT)

            split_weights(0, 1)
            pool.wait_ge(acc_set, NT // 2)
            pool.tensor_tensor(xres[:, :, :], xres[:, :, :], rows["beta"][:, :].rearrange("p (o d) -> p o d", o=1).to_broadcast([P, NT, D]),
                               ALU.add).then_inc(xb_done, 1)
            with pool.Fori(1, NE // 2) as e:
                for eo in range(2):
                    split_weights(e, eo)

            links = [0]

            def link(ins):
                ins.then_inc(pool_chain, 1)
                links[0] += 1
                pool.wait_ge(pool_chain, links[0])

            def moments(k, g):
                lo, hi = 4 * g, 4 * g + 4
                mean, var, rstd, a, b, root_ = (lnv[:, i, lo:hi] for i in range(6))
                me, ve, mo, vo = (stats[:, lo:hi, i] for i in (1, 2, 4, 5))
                pool.wait_ge(stat_done, 4 * ORDER.index((k, g)) + 4)
                link(pool.tensor_tensor(mean, me, mo, ALU.add))
                link(pool.tensor_tensor(a, me, mo, ALU.subtract))
                link(pool.tensor_tensor(b, ve, vo, ALU.add))
                link(pool.tensor_scalar(mean, mean, 0.5, None, ALU.mult))
                link(pool.tensor_tensor(a, a, a, ALU.mult))
                link(pool.tensor_scalar(b, b, 1.0 / D, EPS, ALU.mult, ALU.add))
                link(pool.tensor_scalar(a, a, 0.25, None, ALU.mult))
                link(pool.tensor_tensor(var, a, b, ALU.add))
                link(pool.tensor_tensor(root_, var, power[:, lo:hi], ALU.pow))
                link(pool.tensor_tensor(a, root_, root_, ALU.mult))
                link(pool.tensor_tensor(a, a, var, ALU.mult))
                link(pool.tensor_scalar(a, a, -0.5, 1.5, ALU.mult, ALU.add))
                pool.tensor_tensor(rstd, a, root_, ALU.mult).then_inc(mom_done, 1)

            for k, g in MOMENTS:
                if (k, g) == (1, TG - 2):
                    root(4, NT - 4, NT)
                moments(k, g)
            root(5, NT - 4, NT)


def kernel(**inputs):
    import numpy as np
    import concourse.bacc as bacc
    from concourse.bass_utils import run_bass_kernel_spmd as run

    x = np.ascontiguousarray(inputs["x"]).reshape(B * S, D)
    def a(name):
        return np.ascontiguousarray(inputs[name])

    b2d = np.zeros((P, 4, D), np.float32)
    for n in range(NT):
        b2d[n * NE:(n + 1) * NE, n % 4] = a("L0_ffn_b2")
    arrays = {
        "ctxT": np.ascontiguousarray(a("ctx_1024").reshape(B * SC, D).T), "mask": a("mask_BxSxS2_ik1").reshape(B * S, SC),
        "cwq": a("L0_xattn_Wq"), "cwk": a("L0_xattn_Wk"), "cwv": a("L0_xattn_Wv"), "cwo": a("L0_xattn_Wo"),
        "cbq": a("L0_xattn_bq"), "cbk": a("L0_xattn_bk"), "cbv": a("L0_xattn_bv"), "cbo": a("L0_xattn_bo"),
        "wg": a("L0_ffn_Wg"), "bg": a("L0_ffn_bg"), "w1": a("L0_ffn_W1"), "b1": a("L0_ffn_b1"),
        "w2": a("L0_ffn_W2"), "b2d": b2d, "gamma": a("L0_ffn_gamma"), "beta": a("L0_ffn_beta"),
        "x": x, "xT": np.ascontiguousarray(x.T),
        "wqT": np.ascontiguousarray(np.asarray(inputs["L0_attn_Wq"]).T),
        "wkT": np.ascontiguousarray(np.asarray(inputs["L0_attn_Wk"]).T),
        "wvT": np.ascontiguousarray(np.asarray(inputs["L0_attn_Wv"]).T),
        "ident": np.eye(P, dtype=np.float32),
        "block8": np.repeat(np.eye(8, dtype=np.float32), HD, axis=0),
        "iota8": np.tile(np.arange(NE, dtype=np.float32), (P, 1)),
    }
    nc = bacc.Bacc("TRN2", target_bir_lowering=False, num_devices=1)
    t = {n: nc.dram_tensor(f"in_{n}", a.shape, mybir.dt.from_np(a.dtype), kind="ExternalInput").ap() for n, a in arrays.items()}
    t["out"] = nc.dram_tensor("out_y", (B * S, D), F32, kind="ExternalOutput").ap()
    build(nc, t)
    r = run(nc, [{f"in_{n}": a for n, a in arrays.items()}], core_ids=[0])
    return r.results[0]["out_y"].reshape(B, S, D)
```

```python
from contextlib import ExitStack

import concourse.bass as bass
from concourse import mybir

ALU = mybir.AluOpType
ACT = mybir.ActivationFunctionType
AX_X = mybir.AxisListType.X
F32 = mybir.dt.float32
BF16 = mybir.dt.bfloat16
I32 = mybir.dt.int32
U32 = mybir.dt.uint32

P = 128
B, S, D = 2, 1024, 256
H, HD = 16, 16
SC = 77
NE, F = 8, 512
NT = B * S // P
C2 = D // P
TG = B * S // 512
GH = 4
NG = H // GH
NGRP = B * NG
KT = S // P
UNITS = 2 * NGRP
STEPS = KT * GH
VW = 32
PR = 8
EPS = 1e-5
INV4 = 0.25
MASKED = -4.0e9
NO_CAP = 3.0e38
SR = 4
FAR = 3
HALF = H // 2
VC = -(-HALF * SC // P)
VROWS = [min(P, HALF * SC - c * P) for c in range(VC)]
TURNS = [[(h, c) for c in range(VC - 1)] for h in range(2)] + [[(h, VC - 1) for h in range(2)]]
V_RUNS = []
for _h in range(HALF):
    _s = 0
    while _s < SC:
        _r = _h * SC + _s
        _n = min(SC - _s, P - _r % P)
        V_RUNS.append((_h, _s, _n, _r // P, _r % P))
        _s += _n
MAXROW = 96
KROWS = 98
AHEAD = 6
Q_BLOCKS = ((0, 0, 3), (48, 0, 2), (80, 0, 1))
K_BLOCKS = ((0, 0, 1), (16, 0, 1), (32, 0, 1), (48, 1, 1), (64, 1, 1), (80, 2, 1))
EC = 17
MASK_STEPS = 9
SOON = 14
LATE = 6
LOADS = len(Q_BLOCKS) + len(K_BLOCKS)
FC = F // P


def build(nc, t):
    with ExitStack() as ctx:
        def sb(name, shape, dt=F32):
            return ctx.enter_context(nc.sbuf_tensor(name, shape, dt))

        def sem(name):
            return ctx.enter_context(nc.semaphore(name))

        bank = [ctx.enter_context(nc.psum_tensor(f"bank{i}", [P, 512], F32)) for i in range(4, 8)]
        quad = ctx.enter_context(nc.psum_tensor("quad", [P, 4, 512], F32))
        bank = [quad[:, i, :] for i in range(4)] + [b[:, :] for b in bank]
        scratch = {w: nc.dram_tensor(f"{w}_parts", (2 * B, 3, HD, 2 * GH * S), BF16, kind="Internal").ap()
                   for w in "qk"}

        ident = sb("ident", [P, P])
        ident16 = sb("ident16", [P, P], BF16)
        block8 = sb("block8", [P, 8])
        iota8 = sb("iota8", [P, NE])
        w_in = {n: sb(n, [P, C2, D]) for n in ("wq", "wk", "wv", "cwq", "cwk", "cwv", "cwo")}
        xres = sb("xres", [P, NT, D])
        attn = sb("attn", [P, 4, 4, 4, GH * HD])
        acc = attn[:, :, :, :, :].rearrange("p a k q c -> p (a k q c)").rearrange("p (n d) -> p n d", d=D)
        stats = sb("stats", [P, NT, 6])
        lnv = sb("lnv", [P, 8, NT])
        ctxT = sb("ctxT", [P, C2, B * SC])
        k2T = sb("k2T", [P, 2, B * SC])
        kbd = sb("kbd", [P, B, 2, 8, SC])
        v2 = sb("v2", [SC, B, D])
        vbd = sb("vbd", [P, B, 2, VC, P])
        cap = sb("cap", [P, NT, SC])
        maski = cap[:, :, :].bitcast(I32)
        power = sb("power", [P, NT])
        rows = {n: sb(f"{n}_row", [P, D]) for n in ("cbv", "cbo", "gamma", "beta")}
        cbq, cbk = sb("cbq", [P, 2]), sb("cbk", [P, 2])
        wg = sb("wg", [P, C2, NE])
        bg = sb("bg", [P, NE])
        b1 = sb("b1", [P, NE, FC])
        one = sb("one", [P, 1])
        b1e = sb("b1e", [P, 2, FC])
        b2r = sb("b2r", [P, D])
        b2parts = sb("b2parts", [P, 2, D])
        b2s = sb("b2s", [P, D], BF16)
        part_of = sb("part_of", [P, 2])
        gstack = sb("gstack", [P, NT, 32], BF16)
        credit = sb("credit", [P, 8])
        first = ctx.enter_context(ExitStack())

        def sb1(name, shape, dt=F32):
            return first.enter_context(nc.sbuf_tensor(name, shape, dt))

        xT = sb1("xT", [P, C2, B * S])
        parts = sb1("parts", [P, 3, 3, 512], BF16)
        rest = sb1("rest", [P, 2, 512])
        stacks = [(sb1(f"qstack{i}", [P, 2, GH, 512], BF16), sb1(f"kstack{i}", [P, GH, S], BF16)) for i in (1, 0)][::-1]
        qstack, kstack = zip(*stacks)
        v_all = sb1("v_all", [P, NGRP, KT, GH, VW])
        vslot = [sb1(f"vslot{i}", [P, KT, GH, VW]) for i in range(2)]
        probs = sb1("probs", [P, PR, 512])
        rowmax = sb1("rowmax", [P, 2, 16])
        negparts = sb1("negparts", [P, 2, 32], BF16)
        negrows = sb1("negrows", [32, 2, P], BF16)
        outT = sb1("outT", [P, 512])
        rden = sb1("rden", [P, 16])
        first.close()
        w1raw = sb("w1raw", [P, C2, F])
        w2raw = sb("w2raw", [P, FC, D])
        w1 = [[sb(f"w1_{i}{j}", [P, C2, F], BF16) for j in "hl"] for i in range(2)]
        w2 = [[sb(f"w2_{i}{j}", [P, FC, D], BF16) for j in "hl"] for i in range(2)]
        x1 = sb("x1", [P, 4, D])
        x2T = sb("x2T", [P, C2, B * S])
        x2h = sb("x2h", [P, C2, B * S], BF16)
        x2l = sb("x2l", [P, C2, B * S], BF16)
        logits = sb("logits", [P, NT, NE])
        top = sb("top", [P, NT, 8])
        topi = sb("topi", [P, NT, 8], U32)
        topf = sb("topf", [P, NT, 8])
        gw = sb("gw", [P, NT, 4])
        pick = sb("pick", [P, 2, NT, NE])
        gates = sb("gates", [P, NT, NE])
        gT = sb("gT", [P, 4, P], BF16)
        second = ctx.enter_context(ExitStack())

        def sb2(name, shape, dt=F32):
            return second.enter_context(nc.sbuf_tensor(name, shape, dt))

        x1T = sb2("x1T", [P, C2, 512])
        q2T = sb2("q2T", [P, 2, 512])
        sc2 = sb2("sc2", [P, SR, H, SC])
        max2 = sb2("max2", [P, SR, H])
        sum2 = sb2("sum2", [P, SR, H])
        inv2 = sb2("inv2", [P, SR, H])
        pT = sb2("pT", [P, 2, VC, 512])
        o2T = sb2("o2T", [P, 2, 512])
        second.close()
        hid = sb("hid", [P, 4, 512])
        hh = sb("hh", [P, 2, FC, 512], BF16)
        hl = sb("hl", [P, 2, FC, 512], BF16)

        loaded = {n: sem(n) for n in ("const_loaded", "soon_loaded", "late_loaded")}
        w_loaded = [sem(f"w_loaded{i}") for i in range(3)]
        xT_loaded = [sem(f"xT_loaded{i}") for i in range(TG)]
        qk_ready, hi_done, rest_done, mid_done, parts_done = map(sem, ("qk_ready", "hi_done", "rest_done", "mid_done", "parts_done"))
        parts_stored = [sem(f"parts_stored{i}") for i in range(3)]
        v_ready, v_done, v_zeroed = sem("v_ready"), sem("v_done"), sem("v_zeroed")
        ones_set = sem("ones_set")
        stack_loaded = [sem(f"stack_loaded{i}") for i in range(2)]
        vslot_loaded = [sem(f"vslot_loaded{i}") for i in range(2)]
        max_ready, max_taken = sem("max_ready"), sem("max_taken")
        neg_hi, neg_parts, neg_turned, neg_rows = map(sem, ("neg_hi", "neg_parts", "neg_turned", "neg_rows"))
        neg_loaded = sem("neg_loaded")
        scores_ready, probs_ready, probs_used = map(sem, ("scores_ready", "probs_ready", "probs_used"))
        o_copied, o_turned, o_recip, o_normed = map(sem, ("o_copied", "o_turned", "o_recip", "o_normed"))
        out_stored = sem("out_stored")
        mask_step = sem("mask_step")
        cross_ready, k2_done, v2_done = sem("cross_ready"), sem("k2_done"), sem("v2_done")
        chain, root_wanted, root_done = map(sem, ("chain", "root_wanted", "root_done"))
        x1_done, x1_turned, x1T_done, x1b_done = map(sem, ("x1_done", "x1_turned", "x1T_done", "x1b_done"))
        v2_placed, v2_zeroed = sem("v2_placed"), sem("v2_zeroed")
        q2_ready, q2_done = sem("q2_ready"), sem("q2_done")
        s2_ready, s2_taken, s2_max, s2_shifted, p2_exp = map(sem, ("s2_ready", "s2_taken", "s2_max", "s2_shifted", "p2_exp"))
        s2_summed, s2_recip, p2_done, p2_turned, pT_done = map(sem, ("s2_summed", "s2_recip", "p2_done", "p2_turned", "pT_done"))
        o2_ready, o2T_done = sem("o2_ready"), sem("o2T_done")
        y2_ready, y2_done = sem("y2_ready"), sem("y2_done")
        x2_done, x2_turned, x2T_done, x2h_done, x2l_done = map(sem, ("x2_done", "x2_turned", "x2T_done", "x2h_done", "x2l_done"))
        logits_ready, gap_done, gap_exp, stat_done, mom_done = map(sem, ("logits_ready", "gap_done", "gap_exp", "stat_done", "mom_done"))
        pool_chain, xb_done = sem("pool_chain"), sem("xb_done")
        last_done = sem("last_done")
        logits_taken, b2_split = sem("logits_taken"), sem("b2_split")
        gates_done, gates_turned, gT_done, bias_ready, acc_set = map(sem, ("gates_done", "gates_turned", "gT_done", "bias_ready", "acc_set"))
        w_fetched = [sem("w1_fetched"), sem("w2_fetched")]
        out_done = sem("out_done")
        w_split = sem("w_split")
        h_ready, hid_done, hh_done, hl_done = map(sem, ("h_ready", "hid_done", "hh_done", "hl_done"))
        e_ready, e_added = sem("e_ready"), sem("e_added")
        block = ctx.enter_context(nc.Block())

        ORDER = [(0, 0), (0, 1), (1, 0), (0, 2), (1, 1), (0, 3), (1, 2), (1, 3)]
        MOMENTS = [o for o in ORDER if o[1] < TG - 1]
        EARLY = [(0, p) for p in range(16)] + [(1, p) for p in range(AHEAD)]
        EARLY = [EARLY[2 * i:2 * i + 2] for i in range(8)] + [[e] for e in EARLY[16:20]] + [EARLY[20:]]
        X1_BANK, Q2_BANK = [0, 6, 6, 6], [2, 6, 6, 6]
        DIVIDED = ((1,), (1, 2), (), (1,))
        START2 = (2, 3, 5)
        BIAS_TILES = [(8 * (q // 4) + q % 4, 8 * (q // 4) + q % 4 + 4) for q in range(NT // 2)]
        LOGITS_BANK = [0, 1, 2, 4]
        NORM2 = (5, 8, 12)
        QK_JOBS, V_JOBS = 4 * TG, 2 * TG
        QK_BANK = [4 + n % 2 for n in range(QK_JOBS)]
        V_BANK = [6 + m % 2 for m in range(V_JOBS)]

        def unit_slot(k):
            return (k // 2) % 2

        @block.sync
        def _(sp):
            sp.dma_start(w_in["wq"][:, :, :], t["wqT"].rearrange("(c p) n -> p c n", p=P)).then_inc(w_loaded[0], 16)
            for g in range(TG):
                sp.dma_start(xT[:, :, g * 512:(g + 1) * 512],
                             t["xT"].rearrange("(c p) n -> p c n", p=P)[:, :, g * 512:(g + 1) * 512]).then_inc(xT_loaded[g], 16)
                if g == 0:
                    for i, n in enumerate(("wk", "wv")):
                        sp.dma_start(w_in[n][:, :, :], t[n + "T"].rearrange("(c p) n -> p c n", p=P)).then_inc(w_loaded[i + 1], 16)
                    sp.dma_start(ident[:, :], t["ident"]).then_inc(loaded["const_loaded"], 16)
            def load_late():
                late = [(w_in[n][:, :, :], t[n].rearrange("(c p) n -> p c n", p=P)) for n in ("cwq", "cwo")]
                late += [(b2r[:, :], t["b2r"]), (b1[:, :, :], t["b1"].rearrange("e (c p) -> p e c", p=P)),
                         (maski, t["mask"].rearrange("(n p) s -> p n s", p=P)),
                         (xres[:, :, :], t["x"].rearrange("(n p) d -> p n d", p=P))]
                assert len(late) == LATE
                with nc.allow_non_contiguous_dma(reason="the small bias of the experts goes over the partitions"):
                    for dst, src in late:
                        sp.dma_start(dst, src).then_inc(loaded["late_loaded"], 16)

            def store_parts(n):
                g, job = n // 4, n % 4
                w, half, b = "qk"[job // 2], job % 2, g // 2
                sp.wait_ge(parts_done, n + 1)
                for part in range(3):
                    layout = {"q": "d (h j s) -> h j d s", "k": "d (j h s) -> h j d s"}[w]
                    dst = scratch[w][b * 2 + half, part, :, :].rearrange(layout, h=2, s=512)[g % 2]
                    sp.dma_start(dst, parts[:, n % 3, part, :]).then_inc(parts_stored[n % 3], 16)

            def load_group(pair, slot):
                for row, part, n in Q_BLOCKS:
                    src = scratch["q"][bass.ds(pair, 1), part:part + n, :, :].rearrange("o r d (h g s) -> g (o r d) h s", h=2, g=2)[slot]
                    sp.dma_start(qstack[slot][row:row + n * HD, :, :, :].rearrange("p h j s -> p h (j s)"), src).then_inc(stack_loaded[slot], 16)
                for row, part, n in K_BLOCKS:
                    src = scratch["k"][bass.ds(pair, 1), part:part + n, :, :].rearrange("o r d (g s) -> g (o r d) s", g=2)[slot]
                    sp.dma_start(kstack[slot][row:row + n * HD, :, :].rearrange("p j s -> p (j s)"), src).then_inc(stack_loaded[slot], 16)
                sp.dma_start(vslot[slot][:, :, :, :].rearrange("p k j c -> p (k j c)"),
                             v_all[:, bass.ds(pair * 2 + slot, 1), :, :, :].rearrange("p o k j c -> p (o k j c)")).then_inc(vslot_loaded[slot], 16)

            def load_negmax(rows_done, k1):
                slot, half = unit_slot(k1), k1 % 2
                sp.wait_ge(neg_rows, rows_done)
                for part in range(2):
                    sp.dma_start(qstack[slot][MAXROW + part:MAXROW + part + 1, half, :, :],
                                 negrows[part * 16:part * 16 + 16, k1 % 2, :]).then_inc(neg_loaded, 16)

            for n in range(8):
                store_parts(n)
            for i in range(3):
                sp.wait_ge(parts_stored[i], 48 * len(range(i, 8, 3)))
            sp.wait_ge(v_done, 4)
            load_group(0, 0)
            for n in range(8, 12):
                store_parts(n)
            load_group(0, 1)
            for n in range(12, QK_JOBS):
                store_parts(n)
            load_negmax(1, 0)
            for i in range(3):
                sp.wait_ge(parts_stored[i], 48 * len(range(i, QK_JOBS, 3)))
            sp.wait_ge(v_done, V_JOBS)
            sp.wait_ge(v2_done, 1)
            sp.wait_ge(v2_zeroed, 1)
            for h, s0, n, c, row in V_RUNS:
                sp.dma_start(vbd[row:row + n, :, :, c, h * HD:(h + 1) * HD].rearrange("p b h d -> p (b h) d"),
                             v2[s0:s0 + n, :, :].rearrange("p b (h d) -> p (b h) d", h=2)[:, :, h * HD:(h + 1) * HD]).then_inc(v2_placed, 16)

            def sp_unit(it, k, last):
                u = it * 4 + k
                if not (last and k == 3):
                    load_negmax(u + 2, k + 1)
                if k % 2 == 1 and not last:
                    sp.wait_ge(probs_used, u * STEPS + (STEPS + PR))
                    load_group(it + 1, unit_slot(k))

            def fetch_expert(e):
                sp.dma_start(w1raw[:, :, :], t["w1"][bass.ds(e, 1), :, :].rearrange("o (c p) f -> p (o c) f", p=P)).then_inc(w_fetched[0], 16)
                sp.dma_start(w2raw[:, :, :], t["w2"][bass.ds(e, 1), :, :].rearrange("o (c p) f -> p (o c) f", p=P)).then_inc(w_fetched[1], 16)

            load_late()
            fetch_expert(0)
            with sp.Fori(0, 3) as it:
                for k in range(4):
                    sp_unit(it, k, False)
            for k in range(4):
                sp_unit(3, k, True)
            for e in range(1, 3):
                sp.wait_ge(w_split, e * 5)
                fetch_expert(e)
            with sp.Fori(3, NE) as e:
                sp.wait_ge(w_split, e * 5)
                fetch_expert(e)
            out_v = t["out"].rearrange("(n p) d -> p n d", p=P)
            for n in range(NT):
                if n < NT - 4:
                    sp.wait_ge(out_done, n + 1)
                else:
                    sp.wait_ge(last_done, n - (NT - 4) + 1)
                sp.dma_start(out_v[:, n, :], acc[:, n, :]).then_inc(out_stored, 16)
            sp.wait_ge(out_stored, 16 * NT)

        @block.tensor
        def _(pe):
            def project(g, between=lambda: None):
                pe.wait_ge(xT_loaded[g], 16)
                for job in range(4):
                    n = 4 * g + job
                    if g == 0 and job % 2 == 0:
                        pe.wait_ge(w_loaded[job // 2], 16)
                    if n >= 2:
                        pe.wait_ge(rest_done, n - 1)
                    w = w_in[("wq", "wk")[job // 2]]
                    half = job % 2
                    for c in range(C2):
                        between()
                        mm = pe.matmul(bank[QK_BANK[n]], w[:, c, half * P:half * P + P], xT[:, c, g * 512:g * 512 + 512],
                                       start=(c == 0), stop=(c == C2 - 1))
                    mm.then_inc(qk_ready, 1)
                if g == 0:
                    pe.wait_ge(w_loaded[2], 16)
                for pair in range(2):
                    m = 2 * g + pair
                    if m >= 2:
                        pe.wait_ge(v_done, m - 1)
                    if m == V_JOBS - 1:
                        pe.wait_ge(neg_rows, 1)
                    if m == V_JOBS - 2:
                        pe.wait_ge(k2_done, 1)
                        pe.wait_ge(v2_done, 1)
                    for i in range(2):
                        between()
                        tok = g * 512 + (2 * pair + i) * P
                        for c in range(C2):
                            mm = pe.matmul(bank[V_BANK[m]][:, i * D:(i + 1) * D], xT[:, c, tok:tok + P], w_in["wv"][:, c, :],
                                           start=(c == 0), stop=(c == C2 - 1))
                    mm.then_inc(v_ready, 1)

            def max_pair(u, k, p, halves=(0, 1)):
                slot, half, j, qt = unit_slot(k), k % 2, p // 4, p % 4
                if 0 in halves:
                    pe.wait_ge(max_taken, u * 16 + p + 1)
                q = qstack[slot][0:MAXROW, half, j, qt * P:qt * P + P]
                for e in halves:
                    mm = pe.matmul(bank[2 * (p % 2) + e], q, kstack[slot][0:MAXROW, j, e * 512:e * 512 + 512],
                                   start=True, stop=True)
                if e == 1:
                    mm.then_inc(max_ready, 1)

            def turn_negmax(u, k, first=False):
                if first:
                    pe.wait_ge(v_done, V_JOBS - 2)
                else:
                    pe.wait_ge(o_normed, u)
                pe.wait_ge(neg_parts, u + 1)
                pe.transpose(bank[7].bitcast(BF16)[0:32, 0:P], negparts[:, k % 2, :], ident16[:, :]).then_inc(neg_turned, 1)

            def scores(u, k, i):
                slot, half, kt, j = unit_slot(k), k % 2, i // 4, i % 4
                pe.wait_ge(probs_ready, u * STEPS + i + 1)
                mm = pe.matmul(bank[4 + i % 2], kstack[slot][0:KROWS, j, kt * P:kt * P + P],
                               qstack[slot][0:KROWS, half, j, :], start=True, stop=True)
                mm.then_inc(scores_ready, 1)
                return mm

            def values(u, k, i):
                slot, kt, j = unit_slot(k), i // 4, i % 4
                pe.wait_ge(probs_ready, u * STEPS + i + 3)
                pe.matmul(bank[6][32 * j:32 * j + VW, :], vslot[slot][:, kt, j, :], probs[:, i % PR, :],
                          start=(kt == 0), stop=(kt == KT - 1), skip_group_check=True).then_inc(probs_used, 1)

            for g in range(TG - 1):
                project(g)
            pe.wait_ge(v_done, V_JOBS - 2)
            pe.wait_ge(loaded["soon_loaded"], 16 * SOON)
            for half in range(2):
                for c in range(C2):
                    mm = pe.matmul(bank[6][:, half * B * SC:(half + 1) * B * SC], w_in["cwk"][:, c, half * P:half * P + P], ctxT[:, c, :],
                                   start=(c == 0), stop=(c == C2 - 1))
            mm.then_inc(cross_ready, 1)
            for b in range(B):
                for c in range(C2):
                    mm = pe.matmul(bank[7][0:SC, b * D:(b + 1) * D], ctxT[:, c, b * SC:(b + 1) * SC], w_in["cwv"][:, c, :],
                                   start=(c == 0), stop=(c == C2 - 1))
            mm.then_inc(cross_ready, 1)
            pe.wait_ge(k2_done, 1)
            pe.wait_ge(v2_done, 1)
            pe.wait_ge(ones_set, 3)
            pe.wait_ge(stack_loaded[0], 16 * LOADS)
            slices = list(EARLY)

            def next_pairs():
                for u, p in slices.pop(0):
                    if (u, p) == (1, 0):
                        turn_negmax(0, 0, first=True)
                    max_pair(u, u, p)

            project(TG - 1, next_pairs)
            next_pairs()
            pe.wait_ge(v_done, V_JOBS)
            pe.wait_ge(parts_done, QK_JOBS)
            pe.wait_ge(neg_loaded, 32)
            for i in range(3):
                scores(0, 0, i)

            def turn_x1(g):
                pe.wait_ge(x1_done, g * 4 + 4)
                if g == 0:
                    pe.wait_ge(loaded["late_loaded"], 16 * LATE)
                    pe.wait_ge(max_taken, UNITS * 16 + 2)
                elif g == 1:
                    pe.wait_ge(o_normed, UNITS + 1)
                elif g > 1:
                    pe.wait_ge(y2_done, g * 4 - 4)
                for c in range(C2):
                    for i in range(4):
                        tr = pe.transpose(bank[X1_BANK[g] + c][:, i * P:i * P + P], x1[:, i, c * P:c * P + P], ident[:, :])
                    tr.then_inc(x1_turned, 1)

            def project_q2(g, half):
                if half == 0:
                    pe.wait_ge(x1T_done, g * 2 + 2)
                for c in range(C2):
                    mm = pe.matmul(bank[Q2_BANK[g] + half], w_in["cwq"][:, c, half * P:half * P + P], x1T[:, c, :], start=(c == 0), stop=(c == C2 - 1))
                mm.then_inc(q2_ready, 1)

            def scores2(n, half):
                g, i = n // 4, n % 4
                if i == 0:
                    pe.wait_ge(q2_done, g * 2 + half + 1)
                if half == 0:
                    if n:
                        pe.wait_ge(s2_taken, n)
                for e in (2 * half, 2 * half + 1):
                    mm = pe.matmul(bank[e][:, 0:4 * SC], q2T[:, half, i * P:i * P + P],
                                   kbd[:, g // 2, half, 4 * (e % 2):4 * (e % 2) + 4, :].rearrange("p h s -> p (h s)"),
                                   start=True, stop=True)
                if half == 1:
                    mm.then_inc(s2_ready, 1)

            def turn_probs(n, between):
                pe.wait_ge(p2_done, n + 1)
                for j, chunks in enumerate(TURNS):
                    m = 3 * n + j
                    if m >= 2:
                        pe.wait_ge(pT_done, m - 1)
                    for k, (half, c) in enumerate(chunks):
                        flat = sc2[:, n % SR, half * HALF:(half + 1) * HALF, :].rearrange("p h s -> p (h s)")
                        tr = pe.transpose(bank[4 + m % 2][0:VROWS[c], k * P:k * P + P], flat[:, c * P:c * P + VROWS[c]], ident[:, :])
                    tr.then_inc(p2_turned, 1)
                    if j:
                        between(j - 1)

            def values2(g):
                pe.wait_ge(pT_done, 12 * g + 12)
                pe.wait_ge(q2_done, min(2 * g + 4, 2 * TG))
                if g:
                    pe.wait_ge(y2_done, 4 * g)
                if g == TG - 1:
                    pe.wait_ge(x2l_done, 2 * (TG - 1))
                for half in range(2):
                    for c in range(VC):
                        mm = pe.matmul(bank[6 + half], vbd[0:VROWS[c], g // 2, half, c, :], pT[0:VROWS[c], half, c, :],
                                       start=(c == 0), stop=(c == VC - 1))
                    mm.then_inc(o2_ready, 1)

            def project_o2(g):
                pe.wait_ge(o2T_done, g * 2 + 2)
                for i in range(4):
                    for c in range(C2):
                        mm = pe.matmul(bank[6 + i // 2][:, (i % 2) * D:(i % 2 + 1) * D], o2T[:, c, i * P:i * P + P], w_in["cwo"][:, c, :],
                                       start=(c == 0), stop=(c == C2 - 1))
                    mm.then_inc(y2_ready, 1)

            def turn_x2(g):
                pe.wait_ge(x2_done, g * 4 + 4)
                if g:
                    pe.wait_ge(x2l_done, g * 2)
                else:
                    pe.wait_ge(y2_done, 4 * (TG - 1))
                for c in range(C2):
                    for i in range(4):
                        tr = pe.transpose(bank[6 + c][:, i * P:i * P + P], xres[:, 4 * g + i, c * P:c * P + P], ident[:, :])
                    tr.then_inc(x2_turned, 1)

            def logits2(g):
                pe.wait_ge(x2T_done, 2 * g + 2)
                pe.wait_ge(s2_taken, NT)
                for i in range(4):
                    for c in range(C2):
                        mm = pe.matmul(bank[LOGITS_BANK[g]][:, i * NE:(i + 1) * NE], x2T[:, c, (4 * g + i) * P:(4 * g + i + 1) * P], wg[:, c, :],
                                       start=(c == 0), stop=(c == C2 - 1))
                mm.then_inc(logits_ready, 1)

            pairs = [(1, p) for p in range(AHEAD, 16)] + [(2, p) for p in range(AHEAD - 1)]
            when = [pairs[2 * m:2 * m + 2] for m in range(KT)]
            SPREAD = (1, 2, 1)
            TURN = 6

            def unit(it, k, last):
                u = it * 4 + k

                def ahead(i):
                    if i < STEPS:
                        scores(u, k, i)
                    elif not (last and k == 3):
                        if i == STEPS:
                            pe.wait_ge(neg_loaded, u * 32 + 64)
                        scores(u + 1, k + 1, i - STEPS)

                def pair(a, p, halves=(0, 1)):
                    if last and k + a > 3:
                        return
                    if (a, p) == (2, 0) and k % 2 == 0 and 0 in halves:
                        n_load = it + 1 + (1 if k + 2 > 3 else 0)
                        pe.wait_ge(stack_loaded[unit_slot(k + 2)], n_load * 16 * LOADS)
                    max_pair(u + a, k + a, p, halves)

                def heads(m):
                    if m == 0:
                        if k % 2 == 0:
                            pe.wait_ge(vslot_loaded[unit_slot(k)], 16 * (it + 1))
                        pe.wait_ge(o_copied, u + 1)
                    for j in range(GH):
                        values(u, k, GH * m + j)

                for m in range(KT):
                    if m:
                        ahead(4 * m + 2)
                    if m == TURN and not (last and k == 3):
                        turn_negmax(u + 1, k + 1)
                    if m:
                        heads(m - 1)
                    halves = [(p, e) for p in when[m] for e in range(2)]
                    for i, n in enumerate(SPREAD):
                        ahead(4 * m + 3 + i)
                        for p, e in halves[:n]:
                            pair(*p, halves=(e,))
                        halves = halves[n:]
                    if last and k == 3:
                        if m == 0:
                            turn_x1(0)
                        elif m == 1:
                            for half in range(2):
                                project_q2(0, half)
                            pe.wait_ge(mask_step, MASK_STEPS)
                        elif m in START2:
                            for half in range(2):
                                scores2(START2.index(m), half)
                heads(KT - 1)
                if not (last and k + 2 > 3):
                    max_pair(u + 2, k + 2, AHEAD - 1)
                ahead(STEPS + 2)
                pe.wait_ge(o_copied, u + 2)
                if not (last and k == 3):
                    pe.wait_ge(neg_rows, u + 2)
                else:
                    pe.wait_ge(o_normed, u + 1)
                for qt in range(4):
                    tr = pe.transpose(bank[7][:, qt * P:qt * P + P], outT[:, qt * P:qt * P + P], ident[:, :])
                tr.then_inc(o_turned, 1)

            with pe.Fori(0, 3) as it:
                for k in range(4):
                    unit(it, k, False)
            for k in range(4):
                unit(3, k, True)

            pe.wait_ge(v2_placed, 16 * len(V_RUNS))
            for n in range(NT):
                g, i = n // 4, n % 4

                def next_scores(half):
                    if n + FAR < NT:
                        scores2(n + FAR, half)

                if i == 1 and g < TG - 1:
                    turn_probs(n, lambda k: [project_q2(g + 1, half) for half in range(2)] if k == 0 else None)
                    for half in range(2):
                        next_scores(half)
                else:
                    turn_probs(n, next_scores)
                if i == 0 and g < TG - 1:
                    turn_x1(g + 1)
                if g == TG - 1 and i < 3:
                    turn_x2(i)
                if i == 3:
                    values2(g)
                    project_o2(g)
                if g == TG - 1 and i > 0:
                    logits2(i - 1)

            def hidden(e, eo, g):
                n = (e * 2 + eo) * TG + g
                if g == 0:
                    pe.wait_ge(w_split, (e * 2 + eo) * 5 + 5)
                (wh, wl), tok = w1[eo], slice(g * 512, g * 512 + 512)
                for fc in range(FC):
                    pe.wait_ge(hid_done, n * FC + fc + 1)
                    terms = [(w, x, c) for c in range(C2) for w, x in ((wh, x2h), (wh, x2l), (wl, x2h))]
                    for k, (w, x, c) in enumerate(terms):
                        mm = pe.matmul(bank[fc], w[:, c, fc * P:fc * P + P], x[:, c, tok], start=(k == 0), stop=(k == len(terms) - 1))
                    mm.then_inc(h_ready, 1)

            def output(e, eo, g):
                n = (e * 2 + eo) * TG + g
                wh, wl = w2[eo]
                pe.wait_ge(hl_done, n * FC + 2 * FC)
                for i in range(4):
                    pe.wait_ge(e_added, n * 4 + i + 1)
                    terms = [(a, w, fc) for fc in range(FC) for a, w in ((hh, wh), (hl, wh), (hh, wl))]
                    for k, (a, w, fc) in enumerate(terms):
                        mm = pe.matmul(bank[4 + i][:, 0:D], a[:, g % 2, fc, i * P:i * P + P], w[:, fc, :], start=(k == 0), stop=(k == len(terms) - 1))
                    mm.then_inc(e_ready, 1)

            def expert_pair(e, last):
                for k in range(2 * TG):
                    if k < 2 * TG - 1:
                        hidden(e, (k + 1) // TG, (k + 1) % TG)
                    elif not last:
                        hidden(e + 1, 0, 0)
                    output(e, k // TG, k % TG)

            pe.wait_ge(logits_taken, TG - 1)
            hidden(0, 0, 0)
            pe.wait_ge(y2_done, NT)
            turn_x2(TG - 1)
            logits2(TG - 1)
            pe.wait_ge(x2l_done, 2 * TG)
            pe.wait_ge(gates_done, 1)
            for g in range(TG):
                tr = pe.transpose(bank[5].bitcast(BF16)[:, g * P:(g + 1) * P], gstack[:, 4 * g:4 * g + 4, :].rearrange("p n e -> p (n e)"), ident16[:, :])
            tr.then_inc(gates_turned, 1)
            pe.wait_ge(gT_done, 1)
            pe.wait_ge(b2_split, 6)
            for q, tiles in enumerate(BIAS_TILES):
                if q >= 4:
                    pe.wait_ge(acc_set, q - 3)
                for i, n in enumerate(tiles):
                    row = n % 4 * 32
                    mm = pe.matmul(bank[4 + q % 4][:, i * D:(i + 1) * D], gT[row:row + 32, n // 4, :], b2s[row:row + 32, :], start=True, stop=True)
                mm.then_inc(bias_ready, 1)
            with pe.Fori(0, NE // 2 - 1) as e:
                expert_pair(e, False)
            expert_pair(NE // 2 - 1, True)

        @block.vector
        def _(dve):
            def split(n):
                hi, mid, low = (parts[:, n % 3, i, :] for i in range(3))
                dve.wait_ge(hi_done, n + 1)
                dve.tensor_tensor(rest[:, n % 2, :], bank[QK_BANK[n]], hi, ALU.subtract).then_inc(rest_done, 1)
                dve.wait_ge(rest_done, n + 1)
                dve.tensor_copy(mid, rest[:, n % 2, :]).then_inc(mid_done, 1)
                dve.wait_ge(mid_done, n + 1)
                dve.tensor_tensor(low, rest[:, n % 2, :], mid, ALU.subtract).then_inc(parts_done, 1)

            for n in range(QK_JOBS - 4):
                split(n)
            dve.wait_ge(cross_ready, 2)
            dve.tensor_tensor(v2[:, :, :], bank[7][0:SC, :].rearrange("p (b d) -> p b d", b=B),
                              rows["cbv"][0:SC, :].rearrange("p (o d) -> p o d", o=1).to_broadcast([SC, B, D]), ALU.add).then_inc(v2_done, 1)

            def reduce_max(u, k, p):
                dve.wait_ge(max_ready, u * 16 + p + 1)
                dve.tensor_reduce(rowmax[:, k % 2, p:p + 1], quad[:, 2 * (p % 2):2 * (p % 2) + 2, :].rearrange("p a n -> p (a n)"),
                                  AX_X, ALU.max).then_inc(max_taken, 1)

            def negate(u, k):
                m, hi, low = rowmax[:, k % 2, :], negparts[:, k % 2, 0:16], negparts[:, k % 2, 16:32]
                dve.wait_ge(max_taken, u * 16 + 18)
                dve.tensor_scalar(hi, m, -1.0, None, ALU.mult).then_inc(neg_hi, 1)
                dve.wait_ge(neg_hi, u + 1)
                dve.scalar_tensor_tensor(low, m, -1.0, hi, ALU.mult, ALU.subtract).then_inc(neg_parts, 1)
                dve.wait_ge(neg_turned, u + 1)
                dve.tensor_copy(negrows[:, k % 2, :], bank[7].bitcast(BF16)[0:32, 0:P]).then_inc(neg_rows, 1)

            for i, pairs in enumerate(EARLY):
                for u, p in pairs:
                    if (u, p) == (1, 0):
                        negate(0, 0)
                    reduce_max(u, u, p)
                if i in (2, 4, 6, 8):
                    split(QK_JOBS - 4 + i // 2 - 1)

            links = [0]

            def mark(ins):
                ins.then_inc(chain, 1)
                links[0] += 1
                return links[0]

            def link(ins):
                dve.wait_ge(chain, mark(ins))

            roots = [0]
            MEAN, VAR, RSTD, T0, T1, ROOT = range(6)

            def start_moments(lo, hi):
                row = [lnv[:, i, lo:hi] for i in range(8)]
                me, ve, mo, vo = (stats[:, lo:hi, i] for i in (1, 2, 4, 5))
                dve.tensor_tensor(row[T1], ve, vo, ALU.add).then_inc(chain, 1)
                dve.tensor_tensor(row[MEAN], me, mo, ALU.add).then_inc(chain, 1)
                links[0] += 2
                link(dve.tensor_tensor(row[T0], me, mo, ALU.subtract))
                dve.tensor_scalar(row[MEAN], row[MEAN], 0.5, None, ALU.mult).then_inc(chain, 1)
                dve.tensor_tensor(row[T0], row[T0], row[T0], ALU.mult).then_inc(chain, 1)
                links[0] += 2
                link(dve.tensor_scalar(row[T1], row[T1], 1.0 / D, EPS, ALU.mult, ALU.add))
                dve.scalar_tensor_tensor(row[VAR], row[T0], 0.25, row[T1], ALU.mult, ALU.add).then_inc(root_wanted, 1)

            def root_moments(lo, hi):
                row = [lnv[:, i, lo:hi] for i in range(8)]
                roots[0] += 1
                dve.wait_ge(root_done, roots[0])
                link(dve.tensor_tensor(row[T0], row[ROOT], row[ROOT], ALU.mult))
                link(dve.scalar_tensor_tensor(row[T0], row[T0], -0.5, row[VAR], ALU.mult, ALU.mult))
                link(dve.scalar_tensor_tensor(row[RSTD], row[T0], 1.5, row[ROOT], ALU.add, ALU.mult))

            def moments(lo, hi):
                start_moments(lo, hi)
                root_moments(lo, hi)

            def add_attention(tiles):
                marks = {}
                for n in list(tiles) + [None]:
                    if n is not None:
                        b, h, q = n // 8, n // 4 % 2, n % 4
                        xv = xres[:, n, :].rearrange("p (g f c) -> p g f c", g=2, f=2)
                        marks[n] = mark(dve.tensor_tensor(xv, xv, attn_v[:, b, h, q], ALU.add))
                    for m in [m for m in marks if n is None or m < n]:
                        dve.wait_ge(chain, marks.pop(m))
                        bn = dve.bn_stats(stats[:, m, :], xres[:, m, :])
                return bn

            attn_v = attn[:, :, :, :, :].rearrange("p (b g) (f h) q c -> p b h q g f c", b=B, h=2)

            def norm_tile(out, n, src=xres):
                return dve.tensor_scalar(out, src[:, bass.ds(n, 1), :].rearrange("p o d -> p (o d)"),
                                         lnv[:, MEAN, bass.ds(n, 1)], lnv[:, RSTD, bass.ds(n, 1)], ALU.subtract, ALU.mult)

            def norm_x1(g):
                if g:
                    dve.wait_ge(x1_turned, g * 2)
                    dve.wait_ge(x1b_done, 4 * g)
                for i in range(4):
                    n = g * 4 + i
                    dve.tensor_scalar(x1[:, i, :], xres[:, n, :], lnv[:, MEAN, n:n + 1], lnv[:, RSTD, n:n + 1],
                                      ALU.subtract, ALU.mult).then_inc(x1_done, 1)

            def take(n):
                dve.wait_ge(s2_ready, n + 1)
                if n >= SR:
                    dve.wait_ge(p2_turned, 3 * (n - SR) + 3)
                dve.tensor_tensor(sc2[:, n % SR, :, :].rearrange("p (e h) s -> p e h s", e=4),
                                  quad[:, :, 0:4 * SC].rearrange("p e (h s) -> p e h s", s=SC),
                                  cap[:, n:n + 1, :].rearrange("p o (u s) -> p o u s", u=1).to_broadcast([P, 4, 4, SC]),
                                  ALU.min).then_inc(s2_taken, 1)
                dve.wait_ge(s2_taken, n + 1)
                dve.tensor_reduce(max2[:, n % SR, :], sc2[:, n % SR, :, :], AX_X, ALU.max).then_inc(s2_max, 1)

            def sum_probs(n):
                dve.wait_ge(p2_exp, n + 1)
                dve.tensor_reduce(sum2[:, n % SR, :], sc2[:, n % SR, :, :], AX_X, ALU.add).then_inc(s2_summed, 1)
                dve.wait_ge(s2_summed, n + 1)
                dve.reciprocal(inv2[:, n % SR, :], sum2[:, n % SR, :]).then_inc(s2_recip, 1)

            def residual2(g):
                dve.wait_ge(x1b_done, 4 * g + 4)
                for i in range(5):
                    n = 4 * g + i
                    if i < 4:
                        dve.wait_ge(y2_ready, (n | 1) + 1)
                        dve.tensor_tensor(xres[:, n, :], bank[6 + i // 2][:, (i % 2) * D:(i % 2 + 1) * D], xres[:, n, :], ALU.add).then_inc(y2_done, 1)
                    if i:
                        dve.wait_ge(y2_done, n)
                        bn = dve.bn_stats(stats[:, n - 1, :], xres[:, n - 1, :])
                return bn

            def norm_x2(g):
                for n in range(4 * g, 4 * g + 4):
                    dve.tensor_scalar(xres[:, n, :], xres[:, n, :], lnv[:, MEAN, n:n + 1], lnv[:, RSTD, n:n + 1],
                                      ALU.subtract, ALU.mult).then_inc(x2_done, 1)

            def top_two(g):
                tiles = slice(4 * g, 4 * g + 4)
                dve.wait_ge(logits_ready, g + 1)
                dve.tensor_tensor(logits[:, tiles, :], bank[LOGITS_BANK[g]][:, 0:4 * NE].rearrange("p (n e) -> p n e", e=NE),
                                  bg[:, :].rearrange("p (o e) -> p o e", o=1).to_broadcast([P, 4, NE]), ALU.add).then_inc(logits_taken, 1)
                dve.wait_ge(logits_taken, g + 1)
                for n in range(4 * g, 4 * g + 4):
                    mx = dve.max(top[:, n, :], logits[:, n, :])
                link(mx)
                for n in range(4 * g, 4 * g + 4):
                    mx = dve.max_index(topi[:, n, :], top[:, n, :], logits[:, n, :])
                link(mx)

            def split_hidden(e, eo, g):
                n = (e * 2 + eo) * TG + g
                for fc in range(FC):
                    m = n * FC + fc
                    dve.wait_ge(hid_done, m + FC + 1)
                    if fc == 0:
                        dve.wait_ge(e_ready, n * 4 + (EC - 4))
                    dve.tensor_copy(hh[:, g % 2, fc, :], hid[:, fc, :]).then_inc(hh_done, 1)
                    dve.wait_ge(hh_done, m + 1)
                    dve.tensor_tensor(hl[:, g % 2, fc, :], hid[:, fc, :], hh[:, g % 2, fc, :], ALU.subtract).then_inc(hl_done, 1)

            def low_x2(g, c):
                dve.wait_ge(x2h_done, g * 2 + c + 1)
                dve.tensor_tensor(x2l[:, c, g * 512:g * 512 + 512], bank[6 + c], x2h[:, c, g * 512:g * 512 + 512],
                                  ALU.subtract).then_inc(x2l_done, 1)

            def unit(it, k, last):
                u = it * 4 + k
                if not (last and k == 3):
                    for p in range(AHEAD, 16):
                        reduce_max(u + 1, k + 1, p)
                    negate(u + 1, k + 1)
                if not (last and k + 2 > 3):
                    for p in range(AHEAD):
                        reduce_max(u + 2, k + 2, p)
                if last and k == 3:
                    dve.wait_ge(mask_step, MASK_STEPS)
                    take(0)
                    take(1)
                    sum_probs(0)
                    take(2)
                    norm_x1(1)
                    sum_probs(1)
                if last and k == 2:
                    dve.wait_ge(loaded["late_loaded"], 16 * LATE)
                    dve.wait_ge(v_done, V_JOBS)
                    dve.wait_ge(o_normed, 2 * KT // 2 + 1)
                    link(add_attention(range(KT)))
                    moments(0, KT)
                    norm_x1(0)
                sums = bank[7].rearrange("p (q j c) -> p q j c", q=4, c=VW)
                dve.wait_ge(o_turned, u + 2)
                dve.reciprocal(rden[:, :].rearrange("p (q j) -> p q j", q=4), sums[:, :, :, HD]).then_inc(o_recip, 1)
                dve.wait_ge(o_recip, u + 1)
                inv = rden[:, :].rearrange("p (q j o) -> p q j o", q=4, o=1).to_broadcast([P, 4, GH, HD])
                dst = attn[:, bass.ds(it, 1), k, :, :].rearrange("p o q (j d) -> p (o q) j d", d=HD)
                dve.tensor_tensor(dst, sums[:, :, :, 0:HD], inv, ALU.mult).then_inc(o_normed, 1)

            with dve.Fori(0, 3) as it:
                for k in range(4):
                    unit(it, k, False)
            for k in range(4):
                unit(3, k, True)

            for n in range(NT):
                g, i = n // 4, n % 4
                for m in DIVIDED[i]:
                    if 1 < n + m < NT:
                        sum_probs(n + m)
                if n == 4:
                    root_moments(KT, NT)
                    norm_x1(2)
                if i == 0 and g:
                    bn = residual2(g - 1)
                if n + FAR < NT:
                    take(n + FAR)
                if n < 4:
                    bn = add_attention(range(KT + 2 * n, KT + 2 * n + 2))
                    if n == 3:
                        link(bn)
                        start_moments(KT, NT)
                if i == 3 and g == 1:
                    norm_x1(3)
                if n - 1 in NORM2:
                    j = NORM2.index(n - 1)
                    root_moments(4 * j, 4 * j + 4)
                    norm_x2(j)
                if n in NORM2:
                    j = NORM2.index(n)
                    link(bn)
                    start_moments(4 * j, 4 * j + 4)
                if g == TG - 1 and i > 1:
                    top_two(i - 2)
                if g == TG - 1 and i < 3:
                    for c in range(C2):
                        low_x2(i, c)
            bn = residual2(TG - 1)
            link(bn)
            top_two(TG - 2)
            moments(NT - 4, NT)
            norm_x2(TG - 1)
            split_hidden(0, 0, 0)
            for c in range(C2):
                low_x2(TG - 1, c)
            top_two(TG - 1)
            dve.tensor_tensor(gw[:, :, 0], top[:, :, 1], top[:, :, 0], ALU.subtract).then_inc(gap_done, 1)
            link(dve.tensor_copy(topf[:, :, :], topi[:, :, :]))
            for j in range(2):
                dve.tensor_tensor(pick[:, j, :, :], iota8[:, :].rearrange("p (o e) -> p o e", o=1).to_broadcast([P, NT, NE]),
                                       topf[:, :, j:j + 1].to_broadcast([P, NT, NE]), ALU.is_equal)
            dve.wait_ge(gap_exp, 1)
            link(dve.tensor_scalar(gw[:, :, 3], gw[:, :, 1], 1.0, None, ALU.add))
            link(dve.reciprocal(gw[:, :, 2], gw[:, :, 3]))
            link(dve.tensor_tensor(gw[:, :, 3], gw[:, :, 1], gw[:, :, 2], ALU.mult))
            for j in range(2):
                pk = dve.tensor_tensor(pick[:, j, :, :], pick[:, j, :, :], gw[:, :, 2 + j:3 + j].to_broadcast([P, NT, NE]), ALU.mult)
            link(pk)
            link(dve.tensor_tensor(gates[:, :, :], pick[:, 0, :, :], pick[:, 1, :, :], ALU.add))
            dve.tensor_copy(gstack[:, :, 2 * NE:3 * NE], gates[:, :, :])
            link(dve.tensor_copy(gstack[:, :, 0:NE], gates[:, :, :]))
            dve.tensor_tensor(gstack[:, :, NE:2 * NE], gates[:, :, :], gstack[:, :, 0:NE], ALU.subtract).then_inc(gates_done, 1)
            dve.wait_ge(gates_turned, 1)
            dve.tensor_copy(gT[:, :, :].rearrange("p g q -> p (g q)"), bank[5].bitcast(BF16)[:, 0:4 * P]).then_inc(gT_done, 1)

            def add_expert(e, eo, g):
                n = (e * 2 + eo) * TG + g
                for i in range(4):
                    dve.wait_ge(e_ready, n * 4 + (i + 1 + EC))
                    if i == 0:
                        dve.wait_ge(e_added, n * 4 + 4)
                    dve.scalar_tensor_tensor(acc[:, g * 4 + i, :], bank[4 + i][:, 0:D],
                                             gates[:, g * 4 + i, bass.ds(e * 2 + eo, 1)], acc[:, g * 4 + i, :],
                                             ALU.mult, ALU.add).then_inc(e_added, 1)

            def expert_pair(e, last):
                for k in range(2 * TG):
                    if k < 2 * TG - 1:
                        split_hidden(e, (k + 1) // TG, (k + 1) % TG)
                    elif not last:
                        split_hidden(e + 1, 0, 0)
                    add_expert(e, k // TG, k % TG)
                    if last and k >= TG:
                        finish(k - TG)

            def group_stats(g):
                for n in range(4 * g, 4 * g + 4):
                    dve.bn_stats(stats[:, n, :], acc[:, n, :]).then_inc(stat_done, 1)

            def await_moments(k, g):
                if g < TG - 1:
                    dve.wait_ge(mom_done, MOMENTS.index((k, g)) + 1)
                else:
                    dve.wait_ge(stat_done, 4 * ORDER.index((k, g)) + 4)
                    moments(4 * g, 4 * g + 4)

            def first_norm(g):
                await_moments(0, g)
                if g == 0:
                    dve.wait_ge(xb_done, 1)
                tiles = range(4 * g, 4 * g + 4)
                for n in tiles:
                    ins = dve.scalar_tensor_tensor(acc[:, n, :], acc[:, n, :], lnv[:, MEAN, n:n + 1], rows["gamma"][:, :], ALU.subtract, ALU.mult)
                link(ins)
                for n in tiles:
                    ins = dve.scalar_tensor_tensor(acc[:, n, :], acc[:, n, :], lnv[:, RSTD, n:n + 1], xres[:, n, :], ALU.mult, ALU.add)
                link(ins)
                group_stats(g)

            def last_norm(g):
                await_moments(1, g)
                for n in range(4 * g, 4 * g + 4):
                    dve.tensor_scalar(acc[:, n, :], acc[:, n, :], lnv[:, MEAN, n:n + 1], lnv[:, RSTD, n:n + 1],
                                      ALU.subtract, ALU.mult).then_inc(last_done, 1)

            def finish(g):
                dve.wait_ge(e_added, 4 * (NE - 1) * TG + 4 * g + 8)
                group_stats(g)
                if g:
                    first_norm(g - 1)

            def over(v, q):
                return v[:, 8 * (q // 4):8 * (q // 4) + 8, :].rearrange("p (i n) d -> p i n d", n=4)[:, :, q % 4, :]

            for q in range(NT // 2):
                dve.wait_ge(bias_ready, q + 1)
                dve.tensor_tensor(over(acc, q), bank[4 + q % 4].rearrange("p (n d) -> p n d", d=D), over(xres, q), ALU.add).then_inc(acc_set if q < 4 else e_added, 1)
            with dve.Fori(0, NE // 2 - 1) as e:
                expert_pair(e, False)
            expert_pair(NE // 2 - 1, True)

            first_norm(TG - 1)
            last_norm(TG - 1)

        @block.scalar
        def _(act):
            def high(n):
                act.wait_ge(qk_ready, n + 1)
                if n >= 3:
                    act.wait_ge(parts_stored[n % 3], 48 * (n // 3))
                act.activation(parts[:, n % 3, 0, :], bank[QK_BANK[n]], ACT.Copy).then_inc(hi_done, 1)

            def keep_values(m):
                act.wait_ge(v_ready, m + 1)
                g, pair = m // 2, m % 2
                for i in range(2):
                    tile = 4 * g + 2 * pair + i
                    b, kt = tile // KT, tile % KT
                    cp = act.activation(v_all[:, b * NG:(b + 1) * NG, kt, :, 0:HD],
                                        bank[V_BANK[m]][:, i * D:(i + 1) * D].rearrange("p (g j d) -> p g j d", g=NG, d=HD), ACT.Copy)
                cp.then_inc(v_done, 1)

            soon = [(w_in[n][:, :, :], t[n].rearrange("(c p) n -> p c n", p=P)) for n in ("cwk", "cwv")]
            soon += [(ctxT[:, :, :], t["ctxT"].rearrange("(c p) n -> p c n", p=P)),
                     (block8[:, :], t["block8"]), (part_of[:, :], t["part_of"]), (iota8[:, :], t["iota8"]),
                     (cbq[:, :], t["cbq"].rearrange("(h p) -> p h", p=P)), (cbk[:, :], t["cbk"].rearrange("(h p) -> p h", p=P)),
                     (wg[:, :, :], t["wg"].rearrange("(c p) n -> p c n", p=P)),
                     (bg[:, :], t["bg"].rearrange("(o n) -> o n", o=1).to_broadcast([P, NE]))]
            soon += [(rows[n][:, :], t[n].rearrange("(o n) -> o n", o=1).to_broadcast([P, D])) for n in ("cbv", "cbo", "gamma", "beta")]
            assert len(soon) == SOON
            with nc.allow_non_contiguous_dma(reason="small bias vectors go over the partitions"):
                for dst, src in soon:
                    act.dma_start(dst, src).then_inc(loaded["soon_loaded"], 16)
            act.wait_ge(v_zeroed, 2)
            for g in range(TG):
                if g == TG - 1:
                    act.wait_ge(cross_ready, 1)
                    for half in range(2):
                        cp = act.activation(k2T[:, half, :], bank[6][:, half * B * SC:(half + 1) * B * SC], ACT.Identity, bias=cbk[:, half:half + 1])
                    cp.then_inc(k2_done, 1)
                for job in range(4):
                    high(4 * g + job)
                keep_values(2 * g)
                keep_values(2 * g + 1)

            def exps(u, k, i):
                n = u * STEPS + i
                act.wait_ge(scores_ready, n + 1)
                act.wait_ge(probs_used, n + 1)
                act.activation(probs[:, i % PR, :], bank[4 + i % 2], ACT.Exp, scale=INV4).then_inc(probs_ready, 1)

            def exp2(n):
                act.wait_ge(s2_shifted, n + 1)
                act.activation(sc2[:, n % SR, :, :], sc2[:, n % SR, :, :], ACT.Exp, scale=INV4).then_inc(p2_exp, 1)

            def keep_turned(n):
                g, i = n // 4, n % 4
                if i == 0 and g:
                    act.wait_ge(o2_ready, 2 * g)
                for j, chunks in enumerate(TURNS):
                    if j == 2 and i == 1 and g < TG - 1:
                        keep_q2(g + 1)
                    m = 3 * n + j
                    act.wait_ge(p2_turned, m + 1)
                    (half, c), k = chunks[0], len(chunks)
                    rows_ = VROWS[c]
                    dst = pT[0:rows_, half, c:c + k, i * P:i * P + P] if j < 2 else pT[0:rows_, :, c, i * P:i * P + P]
                    act.activation(dst, bank[4 + m % 2][0:rows_, 0:k * P].rearrange("p (k q) -> p k q", q=P), ACT.Copy).then_inc(pT_done, 1)

            def keep_x1T(g):
                for c in range(C2):
                    act.wait_ge(x1_turned, g * 2 + c + 1)
                    if g:
                        act.wait_ge(q2_ready, g * 2)
                    act.activation(x1T[:, c, :], bank[X1_BANK[g] + c], ACT.Copy).then_inc(x1T_done, 1)

            def keep_q2(g):
                for half in range(2):
                    act.wait_ge(q2_ready, g * 2 + half + 1)
                    if g:
                        act.wait_ge(s2_ready, g * 4)
                    act.activation(q2T[:, half, :], bank[Q2_BANK[g] + half], ACT.Identity, bias=cbq[:, half:half + 1]).then_inc(q2_done, 1)

            def keep_o2(g):
                for half in range(2):
                    act.wait_ge(o2_ready, g * 2 + half + 1)
                    if g:
                        act.wait_ge(y2_ready, g * 4)
                    act.activation(o2T[:, half, :], bank[6 + half], ACT.Copy).then_inc(o2T_done, 1)

            def keep_x2(g):
                for c in range(C2):
                    act.wait_ge(x2_turned, 2 * g + c + 1)
                    act.activation(x2T[:, c, g * 512:g * 512 + 512], bank[6 + c], ACT.Copy).then_inc(x2T_done, 1)
                    act.activation(x2h[:, c, g * 512:g * 512 + 512], bank[6 + c], ACT.Copy).then_inc(x2h_done, 1)

            def unit(it, k, last):
                u = it * 4 + k
                for i in range(2, STEPS):
                    exps(u, k, i)
                    if last and k == 3:
                        if i == 5:
                            keep_x1T(0)
                        elif i == 9:
                            keep_q2(0)
                        elif i == 4 * START2[1] + 5:
                            exp2(0)
                        elif i == 4 * START2[2] + 5:
                            exp2(1)
                if not (last and k == 3):
                    for i in range(2):
                        exps(u + 1, k + 1, i)
                act.wait_ge(probs_used, u * STEPS + STEPS + PR)
                act.wait_ge(o_turned, u + 1)
                act.activation(outT[:, :], bank[6], ACT.Copy).then_inc(o_copied, 1)

            for i in range(2):
                exps(0, 0, i)
            with act.Fori(0, 3) as it:
                for k in range(4):
                    unit(it, k, False)
            for k in range(4):
                unit(3, k, True)

            for n in range(NT):
                g, i = n // 4, n % 4
                keep_turned(n)
                if i == 0 and g < TG - 1:
                    keep_x1T(g + 1)
                if g == TG - 1 and i < 3:
                    keep_x2(i)
                if i == 3:
                    keep_o2(g)
                if n + FAR - 1 < NT:
                    exp2(n + FAR - 1)

            def relu(e, eo, g):
                n = (e * 2 + eo) * TG + g
                for fc in range(FC):
                    m = n * FC + fc
                    act.wait_ge(h_ready, m + 1)
                    act.wait_ge(hl_done, m + 1)
                    if g == 0 and fc == 0:
                        act.wait_ge(w_split, (e * 2 + eo) * 5 + 5)
                    act.activation(hid[:, fc, :], bank[fc], ACT.Relu, bias=b1e[:, eo, fc:fc + 1]).then_inc(hid_done, 1)

            relu(0, 0, 0)
            keep_x2(TG - 1)
            act.wait_ge(gap_done, 1)
            act.activation(gw[:, :, 1], gw[:, :, 0], ACT.Exp).then_inc(gap_exp, 1)
            for g in range(1, TG):
                relu(0, 0, g)
            for g in range(TG):
                relu(0, 1, g)
            with act.Fori(1, NE // 2) as e:
                for eo in range(2):
                    for g in range(TG):
                        relu(e, eo, g)
            for g in range(TG - 1):
                act.wait_ge(mom_done, MOMENTS.index((1, g)) + 1)
                for n in range(4 * g, 4 * g + 4):
                    act.activation(acc[:, n, :], acc[:, n, :], ACT.Identity, bias=lnv[:, 6, n:n + 1], scale=lnv[:, 2, n:n + 1]).then_inc(out_done, 1)

        @block.gpsimd
        def _(pool):
            pool.memset(v_all[:, :, :, :, HD:HD + 1], 1.0).then_inc(v_zeroed, 1)
            pool.wait_ge(v_zeroed, 1)
            pool.memset(v_all[:, :, :, :, HD + 1:VW], 0.0).then_inc(v_zeroed, 1)
            pool.wait_ge(v_zeroed, 2)
            for i in range(2):
                pool.memset(kstack[i][MAXROW:P, :, :], 1.0).then_inc(ones_set, 1)
                pool.wait_ge(ones_set, i + 1)
            pool.memset(credit[:, 0:1], 0.0).then_inc(max_taken, 2)
            pool.wait_ge(max_taken, 2)
            pool.memset(credit[:, 1:2], 0.0).then_inc(probs_ready, 2)
            pool.wait_ge(probs_ready, 2)
            pool.memset(credit[:, 2:3], 0.0).then_inc(probs_used, PR)
            pool.wait_ge(probs_used, PR)
            pool.wait_ge(loaded["const_loaded"], 16)
            pool.tensor_copy(ident16[:, :], ident[:, :]).then_inc(ones_set, 1)
            for i, (s_, k_) in enumerate(((o_copied, 1), (o_turned, 1), (o_normed, 1), 
                           (hid_done, FC),
                           (e_ready, EC), (hl_done, FC))):
                pool.wait_ge(ones_set, 3 + i)
                pool.memset(credit[:, 3:4], 0.0).then_inc(s_, k_)
                pool.wait_ge(s_, k_)
                pool.memset(credit[:, 4:5], 0.0).then_inc(ones_set, 1)
            count = [0]

            def step(ins):
                ins.then_inc(mask_step, 1)
                count[0] += 1
                pool.wait_ge(mask_step, count[0])

            step(pool.memset(one[:, :], 1.0))
            step(pool.memset(power[:, :], -0.5))
            step(pool.memset(vbd[:, :, :, :, :], 0.0))
            pool.memset(credit[:, 5:6], 0.0).then_inc(v2_zeroed, 1)
            pool.wait_ge(loaded["late_loaded"], 16 * LATE)
            step(pool.tensor_scalar(cap[:, :, :], maski[:, :, :], 0.0, -NO_CAP, ALU.is_equal, ALU.mult))
            step(pool.tensor_scalar(cap[:, :, :], cap[:, :, :], NO_CAP, MASKED, ALU.add, ALU.add))
            pool.wait_ge(k2_done, 1)
            for b in range(B):
                for half in range(2):
                    step(pool.tensor_tensor(kbd[:, b, half, :, :],
                                            k2T[:, half, b * SC:(b + 1) * SC].rearrange("p (o s) -> p o s", o=1).to_broadcast([P, 8, SC]),
                                            block8[:, :].rearrange("p (h o) -> p h o", o=1).to_broadcast([P, 8, SC]), ALU.mult))
            assert count[0] == MASK_STEPS

            def split_weights(e, eo):
                m = e * 2 + eo
                pool.wait_ge(e_ready, m * 16 + (EC - 16))
                for k, (raw, w) in enumerate(((w1raw, w1), (w2raw, w2))):
                    pool.wait_ge(w_fetched[k], m * 16 + 16)
                    pool.tensor_tensor(w[eo][0][:, :, :], raw[:, :, :], one[:, :].rearrange("p (a b) -> p a b", a=1).to_broadcast(list(raw.shape)), ALU.mult).then_inc(w_split, 1)
                    if k == 0:
                        pool.tensor_copy(b1e[:, eo, :].rearrange("p (o c) -> p o c", o=1), b1[:, bass.ds(m, 1), :]).then_inc(w_split, 1)
                    pool.wait_ge(w_split, m * 5 + (2, 4)[k])
                    pool.tensor_tensor(w[eo][1][:, :, :], raw[:, :, :], w[eo][0][:, :, :], ALU.subtract).then_inc(w_split, 1)
            split_weights(0, 0)

            def split(ins):
                ins.then_inc(b2_split, 1)
                parts_of_b2[0] += 1
                pool.wait_ge(b2_split, parts_of_b2[0])

            parts_of_b2 = [0]
            high, low = b2parts[:, 0, :], b2parts[:, 1, :]
            split(pool.memset(gstack[:, :, 3 * NE:32], 0.0))
            split(pool.tensor_tensor(b2s[:, :], b2r[:, :], one[:, :].to_broadcast([P, D]), ALU.mult))
            split(pool.tensor_tensor(low, b2r[:, :], b2s[:, :], ALU.subtract))
            split(pool.tensor_tensor(low, low, part_of[:, 1:2].to_broadcast([P, D]), ALU.mult))
            split(pool.tensor_tensor(high, b2s[:, :], part_of[:, 0:1].to_broadcast([P, D]), ALU.mult))
            split(pool.tensor_tensor(b2s[:, :], high, low, ALU.add))

            def root(k, lo, hi):
                pool.wait_ge(root_wanted, k)
                pool.tensor_tensor(lnv[:, 5, lo:hi], lnv[:, 1, lo:hi], power[:, lo:hi], ALU.pow).then_inc(root_done, 1)

            def add_bias2(n):
                pool.wait_ge(x1_done, n // 4 * 4 + 4)
                pool.tensor_tensor(xres[:, n, :], x1[:, n % 4, :], rows["cbo"][:, :], ALU.add).then_inc(x1b_done, 1)

            def over_heads(v):
                return v.rearrange("p (h o) -> p h o", o=1).to_broadcast([P, H, SC])

            def shift(n):
                pool.wait_ge(s2_max, n + 1)
                sc = sc2[:, n % SR, :, :]
                pool.tensor_tensor(sc, sc, over_heads(max2[:, n % SR, :]), ALU.subtract).then_inc(s2_shifted, 1)

            def divide(n):
                pool.wait_ge(s2_recip, n + 1)
                sc = sc2[:, n % SR, :, :]
                pool.tensor_tensor(sc, sc, over_heads(inv2[:, n % SR, :]), ALU.mult).then_inc(p2_done, 1)

            root(1, 0, KT)
            for n in range(4):
                add_bias2(n)
            shift(0)
            shift(1)
            divide(0)
            shift(2)
            divide(1)
            for n in range(NT):
                g, i = n // 4, n % 4
                for m in DIVIDED[i]:
                    if 1 < n + m < NT:
                        divide(n + m)
                if n + FAR < NT:
                    shift(n + FAR)
                if n == 3:
                    root(2, KT, NT)
                if n in NORM2:
                    j = NORM2.index(n)
                    root(3 + j, 4 * j, 4 * j + 4)
                if n + 4 < NT:
                    add_bias2(n + 4)
            root(6, NT - 4, NT)

            split_weights(0, 1)
            pool.wait_ge(e_added, 4)
            pool.tensor_tensor(xres[:, :, :], xres[:, :, :], rows["beta"][:, :].rearrange("p (o d) -> p o d", o=1).to_broadcast([P, NT, D]),
                               ALU.add).then_inc(xb_done, 1)
            with pool.Fori(1, NE // 2) as e:
                for eo in range(2):
                    split_weights(e, eo)

            links = [0]

            def link(ins):
                ins.then_inc(pool_chain, 1)
                links[0] += 1
                pool.wait_ge(pool_chain, links[0])

            def moments(k, g):
                lo, hi = 4 * g, 4 * g + 4
                mean, var, rstd, a, b, root_ = (lnv[:, i, lo:hi] for i in range(6))
                me, ve, mo, vo = (stats[:, lo:hi, i] for i in (1, 2, 4, 5))
                pool.wait_ge(stat_done, 4 * ORDER.index((k, g)) + 4)
                link(pool.tensor_tensor(mean, me, mo, ALU.add))
                link(pool.tensor_tensor(a, me, mo, ALU.subtract))
                link(pool.tensor_tensor(b, ve, vo, ALU.add))
                link(pool.tensor_scalar(mean, mean, 0.5, None, ALU.mult))
                link(pool.tensor_tensor(a, a, a, ALU.mult))
                link(pool.tensor_scalar(b, b, 1.0 / D, EPS, ALU.mult, ALU.add))
                link(pool.tensor_scalar(a, a, 0.25, None, ALU.mult))
                link(pool.tensor_tensor(var, a, b, ALU.add))
                link(pool.tensor_tensor(root_, var, power[:, lo:hi], ALU.pow))
                link(pool.tensor_tensor(a, root_, root_, ALU.mult))
                link(pool.tensor_tensor(a, a, var, ALU.mult))
                link(pool.tensor_scalar(a, a, -0.5, 1.5, ALU.mult, ALU.add))
                rs = pool.tensor_tensor(rstd, a, root_, ALU.mult)
                if k == 0:
                    rs.then_inc(mom_done, 1)
                else:
                    link(rs)
                    link(pool.tensor_tensor(a, mean, rstd, ALU.mult))
                    pool.tensor_scalar(lnv[:, 6, lo:hi], a, -1.0, None, ALU.mult).then_inc(mom_done, 1)

            for k, g in MOMENTS:
                if (k, g) == (1, TG - 2):
                    root(7, NT - 4, NT)
                moments(k, g)
            root(8, NT - 4, NT)


def kernel(**inputs):
    import numpy as np
    import concourse.bacc as bacc
    from concourse.bass_utils import run_bass_kernel_spmd as run

    x = np.ascontiguousarray(inputs["x"]).reshape(B * S, D)
    def a(name):
        return np.ascontiguousarray(inputs[name])

    b2r = np.zeros((4, 4, NE, D), np.float32)
    b2r[:, :3] = a("L0_ffn_b2")
    b2r = b2r.reshape(P, D)
    part_of = np.zeros((4, 4, NE, 2), np.float32)
    part_of[:, :2, :, 0] = 1
    part_of[:, 2, :, 1] = 1
    part_of = part_of.reshape(P, 2)
    arrays = {
        "ctxT": np.ascontiguousarray(a("ctx_1024").reshape(B * SC, D).T), "mask": a("mask_BxSxS2_ik1").reshape(B * S, SC),
        "cwq": a("L0_xattn_Wq"), "cwk": a("L0_xattn_Wk"), "cwv": a("L0_xattn_Wv"), "cwo": a("L0_xattn_Wo"),
        "cbq": a("L0_xattn_bq"), "cbk": a("L0_xattn_bk"), "cbv": a("L0_xattn_bv"), "cbo": a("L0_xattn_bo"),
        "wg": a("L0_ffn_Wg"), "bg": a("L0_ffn_bg"), "w1": a("L0_ffn_W1"), "b1": a("L0_ffn_b1"),
        "w2": a("L0_ffn_W2"), "b2r": b2r, "part_of": part_of, "gamma": a("L0_ffn_gamma"), "beta": a("L0_ffn_beta"),
        "x": x, "xT": np.ascontiguousarray(x.T),
        "wqT": np.ascontiguousarray(np.asarray(inputs["L0_attn_Wq"]).T),
        "wkT": np.ascontiguousarray(np.asarray(inputs["L0_attn_Wk"]).T),
        "wvT": np.ascontiguousarray(np.asarray(inputs["L0_attn_Wv"]).T),
        "ident": np.eye(P, dtype=np.float32),
        "block8": np.repeat(np.eye(8, dtype=np.float32), HD, axis=0),
        "iota8": np.tile(np.arange(NE, dtype=np.float32), (P, 1)),
    }
    nc = bacc.Bacc("TRN2", target_bir_lowering=False, num_devices=1)
    t = {n: nc.dram_tensor(f"in_{n}", a.shape, mybir.dt.from_np(a.dtype), kind="ExternalInput").ap() for n, a in arrays.items()}
    t["out"] = nc.dram_tensor("out_y", (B * S, D), F32, kind="ExternalOutput").ap()
    build(nc, t)
    r = run(nc, [{f"in_{n}": a for n, a in arrays.items()}], core_ids=[0])
    return r.results[0]["out_y"].reshape(B, S, D)
```
